# Optimizing a Trainium2 kernel written in Bass

```python
import numpy as np
import jax
import jax.numpy as jnp

def _softmax(x, axis=-1):
    return jax.nn.softmax(x, axis=axis)

def _gelu(x):
    return jax.nn.gelu(x, approximate=True)

def _silu(x):
    return jax.nn.silu(x)

def _sigmoid(x):
    return jax.nn.sigmoid(x)

def _layernorm(x, axis=-1, eps=1e-05):
    m = jnp.mean(x, axis=axis, keepdims=True)
    v = jnp.var(x, axis=axis, keepdims=True)
    return (x - m) / jnp.sqrt(v + eps)

def _scatter_add(tgt, idx, src, axis=0):
    return tgt.at[idx].add(src)

def _segment_sum(src, seg, n):
    return jax.ops.segment_sum(src, seg, n)
kernel_name = 'mk_audio_tower_d2_tok_audfeat512_r4_b8af77'

def setup_inputs(seed: int=0):
    np.random.seed(seed)
    _w = jnp.asarray

    def _rec_inputs():
        import jax
        import jax.numpy as jnp
        _rk = jax.random.key(seed)
        x = 7.22013e-05 + 1.00017 * jax.random.normal(jax.random.fold_in(_rk, 1), (32, 750, 32), jnp.float32)
        return x
    x = _rec_inputs()

    def _L0_tok_setup():
        import jax, jax.numpy as jnp
        import numpy as np
        PATCH_LEN = 16
        PATCH_STRIDE = 8
        D_MODEL = 128
        N_FEATURES = 32
        key = jax.random.key(seed)
        k_x, k_w, k_b = jax.random.split(key, 3)
        x = jax.random.normal(k_x, (64, 1024, N_FEATURES), dtype=jnp.float32)
        in_dim = PATCH_LEN * N_FEATURES
        bound = 1.0 / np.sqrt(in_dim)
        W = jax.random.uniform(k_w, (D_MODEL, in_dim), dtype=jnp.float32, minval=-bound, maxval=bound)
        b = jax.random.uniform(k_b, (D_MODEL,), dtype=jnp.float32, minval=-bound, maxval=bound)
        return {'x': x, 'W': W, 'b': b}
    _L0_tok_all = _L0_tok_setup()
    _L0_tok_in = {k: v for k, v in _L0_tok_all.items() if k in ('W', 'b')}
    del _L0_tok_all

    def _L0_attn_setup():
        import jax, jax.numpy as jnp
        import numpy as np
        B, L, U, H = (16, 256, 128, 2)
        key = jax.random.key(seed)
        ks = jax.random.split(key, 8)
        s = 0.02
        return {'inputs': jax.random.normal(ks[0], (B, L, U), dtype=jnp.float32), 'tW': jax.random.normal(ks[1], (H, U, U), dtype=jnp.float32) * s, 'tb': jnp.zeros((H, U), dtype=jnp.float32), 'cW': jax.random.normal(ks[2], (H, U, U), dtype=jnp.float32) * s, 'cb': jnp.zeros((H, U), dtype=jnp.float32), 'aW': jax.random.normal(ks[3], (3 * U,), dtype=jnp.float32) * s, 'ab': jnp.zeros((1,), dtype=jnp.float32), 'frW': jax.random.normal(ks[4], (2 * U, U), dtype=jnp.float32) * s, 'frb': jnp.zeros((U,), dtype=jnp.float32), 'ffW': jax.random.normal(ks[5], (2 * U, U), dtype=jnp.float32) * s, 'ffb': jnp.zeros((U,), dtype=jnp.float32)}
    _L0_attn_all = _L0_attn_setup()
    _L0_attn_in = {k: v for k, v in _L0_attn_all.items() if k in ('tW', 'tb', 'cW', 'cb', 'aW', 'ab', 'frW', 'frb', 'ffW', 'ffb')}
    del _L0_attn_all

    def _L0_ffn_setup():
        import jax, jax.numpy as jnp
        import numpy as np
        B, S, D, O = (1, 512, 128, 128)
        H, QD, K, PK = (8, 64, 16, 64)
        N = PK * PK
        HALF = QD // 2

        def _l2norm(x):
            n = jnp.sqrt(jnp.sum(x * x, axis=-1, keepdims=True))
            return x / jnp.maximum(n, 1e-12)
        key = jax.random.key(seed)
        ks = jax.random.split(key, 9)
        return {'hidden_states': jax.random.normal(ks[0], (B, S, D), jnp.float32), 'Wq': jax.random.normal(ks[1], (H * QD, D), jnp.float32) * 0.02, 'bq': jnp.zeros((H * QD,), jnp.float32), 'ln_g': jnp.ones((QD,), jnp.float32), 'ln_b': jnp.zeros((QD,), jnp.float32), 'keys0': jax.random.normal(ks[2], (PK, HALF), jnp.float32) * 0.02, 'keys1': jax.random.normal(ks[3], (PK, HALF), jnp.float32) * 0.02, 'expert_down': jax.random.normal(ks[4], (N, D), jnp.float32) * 0.02, 'expert_up': jax.random.normal(ks[5], (N, O), jnp.float32) * 0.02}
    _L0_ffn_all = _L0_ffn_setup()
    _L0_ffn_in = {k: v for k, v in _L0_ffn_all.items() if k in ('Wq', 'bq', 'ln_g', 'ln_b', 'keys0', 'keys1', 'expert_down', 'expert_up')}
    del _L0_ffn_all

    def _L1_attn_setup():
        import jax, jax.numpy as jnp
        import numpy as np

        def _positional_encoding(seq_len, hidden):
            pos = jnp.arange(seq_len, dtype=jnp.float32)[:, None]
            div = jnp.exp(jnp.arange(0, hidden, 2, dtype=jnp.float32) * (-jnp.log(10000.0) / hidden))
            ang = pos * div
            return jnp.concatenate([jnp.sin(ang), jnp.cos(ang)], axis=-1)
        key = jax.random.key(seed)
        B, S, H = (8, 512, 128)
        ks = jax.random.split(key, 7)
        s = 1.0 / np.sqrt(H)
        return {'inputs_embeds': jax.random.normal(ks[0], (B, S, H), dtype=jnp.float32), 'Wq': jax.random.uniform(ks[1], (H, H), jnp.float32, -s, s), 'bq': jax.random.uniform(ks[2], (H,), jnp.float32, -s, s), 'Wk': jax.random.uniform(ks[3], (H, H), jnp.float32, -s, s), 'bk': jax.random.uniform(ks[4], (H,), jnp.float32, -s, s), 'Wv': jax.random.uniform(ks[5], (H, H), jnp.float32, -s, s), 'bv': jax.random.uniform(ks[6], (H,), jnp.float32, -s, s)}
    _L1_attn_all = _L1_attn_setup()
    _L1_attn_in = {k: v for k, v in _L1_attn_all.items() if k in ('Wq', 'bq', 'Wk', 'bk', 'Wv', 'bv')}
    del _L1_attn_all

    def _L1_ffn_setup():
        import jax, jax.numpy as jnp
        import numpy as np
        H = 128
        F = 512
        E = 16
        SHARED = 2
        TOP_K = 4
        B, S = (2, 512)

        def _mlp(x, w1, b1, w2, b2):
            return jax.nn.gelu(x @ w1 + b1, approximate=False) @ w2 + b2
        key = jax.random.key(seed)
        ks = jax.random.split(key, 10)
        sc = 0.02
        return {'hidden_states': jax.random.normal(ks[0], (B, S, H), dtype=jnp.float32), 'gate_w': jax.random.normal(ks[1], (E, H), dtype=jnp.float32) * sc, 're_w1': jax.random.normal(ks[2], (E, H, F), dtype=jnp.float32) * sc, 're_b1': jnp.zeros((E, F), dtype=jnp.float32), 're_w2': jax.random.normal(ks[3], (E, F, H), dtype=jnp.float32) * sc, 're_b2': jnp.zeros((E, H), dtype=jnp.float32), 'se_w1': jax.random.normal(ks[4], (SHARED, H, F), dtype=jnp.float32) * sc, 'se_b1': jnp.zeros((SHARED, F), dtype=jnp.float32), 'se_w2': jax.random.normal(ks[5], (SHARED, F, H), dtype=jnp.float32) * sc, 'se_b2': jnp.zeros((SHARED, H), dtype=jnp.float32)}
    _L1_ffn_all = _L1_ffn_setup()
    _L1_ffn_in = {k: v for k, v in _L1_ffn_all.items() if k in ('gate_w', 're_w1', 're_b1', 're_w2', 're_b2', 'se_w1', 'se_b1', 'se_w2', 'se_b2')}
    del _L1_ffn_all
    return {'x': x, 'L0_tok_W': _L0_tok_in['W'], 'L0_tok_b': _L0_tok_in['b'], 'L0_attn_tW': _L0_attn_in['tW'], 'L0_attn_tb': _L0_attn_in['tb'], 'L0_attn_cW': _L0_attn_in['cW'], 'L0_attn_cb': _L0_attn_in['cb'], 'L0_attn_aW': _L0_attn_in['aW'], 'L0_attn_ab': _L0_attn_in['ab'], 'L0_attn_frW': _L0_attn_in['frW'], 'L0_attn_frb': _L0_attn_in['frb'], 'L0_attn_ffW': _L0_attn_in['ffW'], 'L0_attn_ffb': _L0_attn_in['ffb'], 'L0_ffn_Wq': _L0_ffn_in['Wq'], 'L0_ffn_bq': _L0_ffn_in['bq'], 'L0_ffn_ln_g': _L0_ffn_in['ln_g'], 'L0_ffn_ln_b': _L0_ffn_in['ln_b'], 'L0_ffn_keys0': _L0_ffn_in['keys0'], 'L0_ffn_keys1': _L0_ffn_in['keys1'], 'L0_ffn_expert_down': _L0_ffn_in['expert_down'], 'L0_ffn_expert_up': _L0_ffn_in['expert_up'], 'L1_attn_Wq': _L1_attn_in['Wq'], 'L1_attn_bq': _L1_attn_in['bq'], 'L1_attn_Wk': _L1_attn_in['Wk'], 'L1_attn_bk': _L1_attn_in['bk'], 'L1_attn_Wv': _L1_attn_in['Wv'], 'L1_attn_bv': _L1_attn_in['bv'], 'L1_ffn_gate_w': _L1_ffn_in['gate_w'], 'L1_ffn_re_w1': _L1_ffn_in['re_w1'], 'L1_ffn_re_b1': _L1_ffn_in['re_b1'], 'L1_ffn_re_w2': _L1_ffn_in['re_w2'], 'L1_ffn_re_b2': _L1_ffn_in['re_b2'], 'L1_ffn_se_w1': _L1_ffn_in['se_w1'], 'L1_ffn_se_b1': _L1_ffn_in['se_b1'], 'L1_ffn_se_w2': _L1_ffn_in['se_w2'], 'L1_ffn_se_b2': _L1_ffn_in['se_b2']}

def reference(x, L0_tok_W, L0_tok_b, L0_attn_tW, L0_attn_tb, L0_attn_cW, L0_attn_cb, L0_attn_aW, L0_attn_ab, L0_attn_frW, L0_attn_frb, L0_attn_ffW, L0_attn_ffb, L0_ffn_Wq, L0_ffn_bq, L0_ffn_ln_g, L0_ffn_ln_b, L0_ffn_keys0, L0_ffn_keys1, L0_ffn_expert_down, L0_ffn_expert_up, L1_attn_Wq, L1_attn_bq, L1_attn_Wk, L1_attn_bk, L1_attn_Wv, L1_attn_bv, L1_ffn_gate_w, L1_ffn_re_w1, L1_ffn_re_b1, L1_ffn_re_w2, L1_ffn_re_b2, L1_ffn_se_w1, L1_ffn_se_b1, L1_ffn_se_w2, L1_ffn_se_b2):
    import jax
    import jax.numpy as jnp

    def _L0_tok_ref(x, W, b):
        import jax, jax.numpy as jnp
        import numpy as np
        PATCH_LEN = 16
        PATCH_STRIDE = 8
        D_MODEL = 128
        N_FEATURES = 32
        B, T, C = x.shape
        n_patches = (T - PATCH_LEN) // PATCH_STRIDE + 1
        idx = jnp.arange(n_patches)[:, None] * PATCH_STRIDE + jnp.arange(PATCH_LEN)[None, :]
        patches = x[:, idx, :]
        patches = patches.reshape(B, n_patches, PATCH_LEN * C)
        return jnp.einsum('bpf,df->bpd', patches, W) + b

    def _L0_attn_ref(inputs, tW, tb, cW, cb, aW, ab, frW, frb, ffW, ffb):
        import jax, jax.numpy as jnp
        import numpy as np
        B, L, U, H = (16, 256, 128, 2)
        x = inputs
        for i in range(tW.shape[0]):
            t = jax.nn.relu(x @ tW[i] + tb[i])
            c = jax.nn.sigmoid(x @ cW[i] + cb[i])
            x = t * c + x * (1.0 - c)
        u = x.shape[-1]
        w1, w2, w3 = (aW[:u], aW[u:2 * u], aW[2 * u:])
        s1 = x @ w1
        s2 = x @ w2
        s3 = jnp.einsum('bid,bjd->bij', x * w3, x)
        A = jax.nn.relu(s1[:, :, None] + s2[:, None, :] + s3 + ab[0])
        att = jnp.einsum('bij,bjd->bid', jax.nn.softmax(A, axis=-1), x)
        concat = jnp.concatenate([inputs, att], axis=-1)
        z = jax.nn.sigmoid(concat @ ffW + ffb)
        r = jax.nn.sigmoid(concat @ frW + frb)
        f = z
        return r * inputs + f * z

    def _L0_ffn_ref(hidden_states, Wq, bq, ln_g, ln_b, keys0, keys1, expert_down, expert_up):
        import jax, jax.numpy as jnp
        import numpy as np
        B, S, D, O = (1, 512, 128, 128)
        H, QD, K, PK = (8, 64, 16, 64)
        N = PK * PK
        HALF = QD // 2

        def _l2norm(x):
            n = jnp.sqrt(jnp.sum(x * x, axis=-1, keepdims=True))
            return x / jnp.maximum(n, 1e-12)
        b, s, d = hidden_states.shape
        q = (hidden_states @ Wq.T + bq).reshape(b, s, H, QD)
        mu = jnp.mean(q, axis=-1, keepdims=True)
        var = jnp.mean((q - mu) ** 2, axis=-1, keepdims=True)
        q = (q - mu) / jnp.sqrt(var + 1e-05) * ln_g + ln_b
        q0, q1 = (q[..., :HALF], q[..., HALF:])
        s0 = jnp.einsum('bshq,eq->bshe', _l2norm(q0), _l2norm(keys0))
        s1 = jnp.einsum('bshq,eq->bshe', _l2norm(q1), _l2norm(keys1))
        sc0, ix0 = jax.lax.top_k(s0, K)
        sc1, ix1 = jax.lax.top_k(s1, K)
        cs = (sc0[..., :, None] + sc1[..., None, :]).reshape(b, s, H, K * K)
        ci = (ix0[..., :, None] + ix1[..., None, :]).reshape(b, s, H, K * K)
        fs, pos = jax.lax.top_k(cs, K)
        fi = jnp.take_along_axis(ci, pos, axis=-1)
        w = jax.nn.softmax(fs, axis=-1)
        down = expert_down[fi]
        up = expert_up[fi]
        inner = jnp.einsum('bsd,bshkd->bshk', hidden_states, down)
        act = jax.nn.gelu(inner, approximate=False)
        out = jnp.einsum('bshk,bshko->bso', act * w, up)
        return out

    def _L1_attn_ref(inputs_embeds, Wq, bq, Wk, bk, Wv, bv):
        import jax, jax.numpy as jnp
        import numpy as np

        def _positional_encoding(seq_len, hidden):
            pos = jnp.arange(seq_len, dtype=jnp.float32)[:, None]
            div = jnp.exp(jnp.arange(0, hidden, 2, dtype=jnp.float32) * (-jnp.log(10000.0) / hidden))
            ang = pos * div
            return jnp.concatenate([jnp.sin(ang), jnp.cos(ang)], axis=-1)
        B, S, H = inputs_embeds.shape
        x = inputs_embeds + _positional_encoding(S, H)[None]
        q = jnp.einsum('bsh,dh->bsd', x, Wq) + bq
        k = jnp.einsum('bsh,dh->bsd', x, Wk) + bk
        v = jnp.einsum('bsh,dh->bsd', x, Wv) + bv
        scores = jnp.einsum('bqd,bkd->bqk', q, k)
        weights = jax.nn.softmax(scores, axis=-1)
        return jnp.einsum('bqk,bkd->bqd', weights, v)

    def _L1_ffn_ref(hidden_states, gate_w, re_w1, re_b1, re_w2, re_b2, se_w1, se_b1, se_w2, se_b2):
        import jax, jax.numpy as jnp
        import numpy as np
        H = 128
        F = 512
        E = 16
        SHARED = 2
        TOP_K = 4
        B, S = (2, 512)

        def _mlp(x, w1, b1, w2, b2):
            return jax.nn.gelu(x @ w1 + b1, approximate=False) @ w2 + b2
        b, s, h = hidden_states.shape
        x = hidden_states.reshape(-1, h)
        gate_probs = jax.nn.softmax(x @ gate_w.T, axis=-1)
        top_v, top_i = jax.lax.top_k(gate_probs, TOP_K)
        top_v = jax.nn.softmax(top_v, axis=-1)
        combine = jnp.einsum('tk,tke->te', top_v, jax.nn.one_hot(top_i, E, dtype=x.dtype))
        routed = jnp.zeros_like(x)
        for e in range(E):
            routed = routed + combine[:, e:e + 1] * _mlp(x, re_w1[e], re_b1[e], re_w2[e], re_b2[e])
        shared = jnp.zeros_like(x)
        for j in range(SHARED):
            shared = shared + _mlp(x, se_w1[j], se_b1[j], se_w2[j], se_b2[j])
        shared = shared / SHARED
        return (routed + shared).reshape(b, s, h)
    h = _L0_tok_ref(x, L0_tok_W, L0_tok_b)
    h = h + _L0_attn_ref(_layernorm(h, axis=-1), L0_attn_tW, L0_attn_tb, L0_attn_cW, L0_attn_cb, L0_attn_aW, L0_attn_ab, L0_attn_frW, L0_attn_frb, L0_attn_ffW, L0_attn_ffb)
    h = h + _L0_ffn_ref(_layernorm(h, axis=-1), L0_ffn_Wq, L0_ffn_bq, L0_ffn_ln_g, L0_ffn_ln_b, L0_ffn_keys0, L0_ffn_keys1, L0_ffn_expert_down, L0_ffn_expert_up)
    h = h + _L1_attn_ref(_layernorm(h, axis=-1), L1_attn_Wq, L1_attn_bq, L1_attn_Wk, L1_attn_bk, L1_attn_Wv, L1_attn_bv)
    h = h + _L1_ffn_ref(_layernorm(h, axis=-1), L1_ffn_gate_w, L1_ffn_re_w1, L1_ffn_re_b1, L1_ffn_re_w2, L1_ffn_re_b2, L1_ffn_se_w1, L1_ffn_se_b1, L1_ffn_se_w2, L1_ffn_se_b2)
    return h

_drawn_inputs = setup_inputs


def setup_inputs(seed=0):
    import zlib

    import numpy as np

    out = dict(_drawn_inputs(seed))
    spreads = {'L0_attn_tb': (0.0, 0.8),
     'L0_attn_cb': (0.0, 0.8),
     'L0_attn_frb': (0.0, 0.28),
     'L0_attn_ffb': (0.0, 0.28),
     'L0_ffn_bq': (0.0, 0.8),
     'L0_ffn_ln_g': (1.0, 0.6),
     'L0_ffn_ln_b': (0.0, 0.8),
     'L1_ffn_re_b1': (0.0, 0.8),
     'L1_ffn_re_b2': (0.0, 0.1),
     'L1_ffn_se_b1': (0.0, 0.557),
     'L1_ffn_se_b2': (0.0, 0.1)}
    factors = {'L0_attn_tW': 8.0,
     'L0_attn_cW': 8.0,
     'L0_attn_aW': 8.0,
     'L0_ffn_Wq': 8.0,
     'L0_ffn_keys0': 8.0,
     'L0_ffn_keys1': 8.0,
     'L0_ffn_expert_down': 8.0,
     'L0_ffn_expert_up': 8.0,
     'L1_attn_bk': 8.0,
     'L1_ffn_re_w1': 2.675}
    for name, (base, spread) in spreads.items():
        noise = np.random.default_rng([zlib.crc32(name.encode()), seed]).standard_normal(out[name].shape)
        drawn = base * np.exp(spread * noise) if base else spread * noise
        out[name] = jnp.asarray(drawn.astype(out[name].dtype))
    for name, factor in factors.items():
        out[name] = (out[name] * factor).astype(out[name].dtype)
    return out
```

```python
from contextlib import ExitStack

import numpy as np

import concourse.bass as bass
from concourse import mybir

F32 = mybir.dt.float32
F16 = mybir.dt.float16
U16 = mybir.dt.uint16
I16 = mybir.dt.int16
ALU = mybir.AluOpType
ACT = mybir.ActivationFunctionType
AX = mybir.AxisListType.X

D = 128
NB, T, C = 32, 750, 32
PL, PS = 16, 8
L = (T - PL) // PS + 1
GB = 4
G = NB // GB
N = GB * L
SUBS = [(0, 128), (128, 128), (256, N - 256)]
NSUB = len(SUBS)
XR = L + 1
H, QD, PK, K = 8, 64, 64, 16
HALF = QD // 2
HP = H // 2
CELLS = [(0, 1, 16), (1, 1, 8), (2, 2, 5), (4, 4, 3), (8, 8, 1)]
SLOTS = 24
NC = sum(n * w for _, n, w in CELLS)
P16, Q8 = 16, 8
E, SH, F, TOPK = 16, 2, 512, 4
FC = F // 128
NE = E + SH
EPS = 1e-5
TAKEN = -1e30

ROWS = [("b1", NE * FC), ("b2", NE), ("tok_b", 1), ("tb", 2), ("cb", 2), ("aw", 3), ("frb", 1),
        ("ffb", 1), ("lng", 1), ("lnb", 1), ("bq", 1), ("bk", 1), ("bv", 1)]
COL, NROWS = {}, 0
for _name, _n in ROWS:
    COL[_name] = NROWS
    NROWS += _n

EORD = list(range(E, NE)) + list(range(E))
WSCALE = 1024.0
V_LINKS, P_LINKS = 68, 10


def build(nc, a, out):
    ctx = ExitStack()
    with ctx:
        def sb(name, shape, dt=F32):
            return ctx.enter_context(nc.sbuf_tensor(name, shape, dt))

        def sem(name):
            return ctx.enter_context(nc.semaphore(name))

        bank = [ctx.enter_context(nc.psum_tensor(f"bank{i}", [128, 512], F32)) for i in range(8)]
        B0, B1, B2, B3 = bank[:4]
        UP, DN = bank[4:6], bank[6:8]
        comb_dram = nc.dram_tensor("comb_dram", [G, E, N], F32, kind="Internal").ap()

        ident = sb("ident", [128, 128])
        posT = sb("posT", [128, L])
        blockmask = sb("blockmask", [128, 8])
        halfones = sb("halfones", [128, 4])
        ones = sb("ones", [1, 128])
        nhalf = sb("nhalf", [128, 16])
        rows = sb("rows", [NROWS, 128])
        cols = sb("cols", [128, NROWS])
        hcols = sb("hcols", [128, NROWS])
        ab = sb("ab", [1, 1])
        wtokT = sb("wtokT", [128, 4, 128])
        wqcT = sb("wqcT", [128, 512])
        wqkvT = sb("wqkvT", [128, 3, 128])
        gateT = sb("gateT", [128, E])
        bqc = sb("bqc", [128, 512])
        bqm = sb("bqm", [128, H])
        tw = sb("tw", [128, 2, 128])
        cw = sb("cw", [128, 2, 128])
        ffw = sb("ffw", [128, 2, 128])
        frw = sb("frw", [128, 2, 128])
        keys = sb("keys", [PK, 4, HALF])
        keys2 = sb("keys2", [PK, 4, HALF])
        kn = sb("kn", [PK, 2])
        keysBD = sb("keysBD", [128, 256])
        merge = sb("merge", [2 * NC, 2, 4 * SLOTS])
        merge16 = sb("merge16", [2 * NC, 2, 4 * SLOTS], F16)
        dnT = sb("dnT", [128, Q8, 128])
        upR = sb("upR", [128, Q8, 128])
        w1 = sb("w1", [128, NE, F])
        w2 = sb("w2", [128, NE, FC, 128])

        xin = sb("xin", [XR, GB, 2, 128])
        hT = sb("hT", [128, N])
        shared = sb("shared", [128, 2 * GB * XR + 11 * N + GB * 128])
        xT = shared[:, 0:2 * GB * XR].rearrange("p (s r) -> p s r", s=2)
        at = 2 * GB * XR
        vtok = shared[0:L, at:at + GB * 128].rearrange("p (b d) -> p b d", b=GB)
        at += GB * 128
        tT, cT, dT, x1T, x2T, uT, attT, qT, kT, probs, probsT = (shared[:, at + i * N:at + (i + 1) * N] for i in range(11))
        prob, probT = probs[0:L, :], probsT[0:L, :]
        bn = sb("bn", [128, NSUB, 6])
        mv = sb("mv", [128, NSUB, 2])
        rstd = sb("rstd", [128, NSUB])
        xn = sb("xn", [128, NSUB, 128])
        inT = sb("inT", [128, N])
        s1row = sb("s1row", [1, N])
        amax = sb("amax", [L, GB])
        asum = sb("asum", [L, GB])
        arec = sb("arec", [L, GB])
        hnT = sb("hnT", [128, N])
        act = sb("act", [128, Q8, N])
        act_raw = act[:, 0:5, :].rearrange("p q n -> p (q n)")[:, 0:12 * 128].rearrange("p (j n) -> p j n", n=128)
        dnraw = act[:, 5:8, :].rearrange("p q n -> p (q n)")[:, 0:Q8 * 128].rearrange("p (j n) -> p j n", n=128)
        qc = sb("qc", [128, 512])
        sq = sb("sq", [128, 512])
        qv = sb("qv", [128, H])
        qr = sb("qr", [128, H])
        qnT = sb("qnT", [128, HP, 128])
        sqT = sb("sqT", [128, HP, 128])
        sc = sb("sc", [128, 2 * H, PK])
        nrm = sb("nrm", [128, 2 * H])
        inv = sb("inv", [128, 2 * H])
        top = sb("top", [128, 2 * H, K])
        topn = sb("topn", [128, 2 * H, K])
        idx = sb("idx", [128, 2 * H, K], U16)
        idf = sb("idf", [128, 2 * H, K])
        cand = sb("cand", [128, H, NC])
        cand2 = sb("cand2", [128, H, NC])
        best = sb("best", [128, H, K])
        cexp = sb("cexp", [128, H, NC])
        cexpert = sb("cexpert", [128, 2, H, NC])
        cw_ = sb("cw_", [128, H, NC])
        wn = sb("wn", [128, H, NC])
        z = sb("z", [128, H])
        zr = sb("zr", [128, H])
        NK = 2 * NC
        NS = 4 * SLOTS
        epick = sb("epick", [128, H, NC])
        wcell = sq[0:NK, :]
        ecell = sb("ecell", [NK, 512], F16)
        pi = sb("pi", [NS, 256], I16)
        qi = sb("qi", [NS, 256], F16)
        whi = sb("whi", [NS, 256], F16)
        wlo = sb("wlo", [NS, 256], F16)
        hot16 = shared[0:NS, 0:5120].bitcast(F16)
        ph = hot16[:, 0:P16 * 256].rearrange("p (g k t) -> p g k t", k=P16, t=8)
        qh = hot16[:, P16 * 256:(P16 + Q8) * 256].rearrange("p (k n) -> p k n", k=Q8)
        qw = hot16[:, (P16 + Q8) * 256:(P16 + 3 * Q8) * 256].rearrange("p (h k n) -> p h k n", h=2, k=Q8)
        lg = sb("lg", [128, NSUB, E + 4])
        lg2 = sb("lg2", [128, NSUB, E + 4])
        ge = sb("ge", [128, NSUB, E])
        gs = sb("gs", [128, NSUB])
        gr = sb("gr", [128, NSUB])
        m8 = sb("m8", [128, NSUB, 8])
        t8 = sb("t8", [128, NSUB, 8])
        comb = sb("comb", [128, NSUB, E])
        combT = sb("combT", [E, N])
        combB = sb("combB", [128, 2, 4, N])
        xd = sb("xd", [128, N])
        hid = sb("hid", [128, 2, FC, N])
        term = sb("term", [128, 2, N])
        acc = sb("acc", [128, N])
        otile = sb("otile", [128, NSUB, 128])

        x_in, const_in, wts_in, exp_in, peer_in = (sem("x_in"), sem("const_in"), sem("wts_in"), sem("exp_in"),
                                                   sem("peer_in"))
        setup_v, setup_p, setup_pe, setup_a, v_set = (sem("setup_v"), sem("setup_p"), sem("setup_pe"),
                                                      sem("setup_a"), sem("v_set"))
        comb_out, out_done = sem("comb_out"), sem("out_done")
        comb_in = [sem("comb_in_even"), sem("comb_in_odd")]
        v_link, p_link = sem("v_link"), sem("p_link")
        v_met, p_met = sem("v_met"), sem("p_met")
        xt_done, xt_copied, tok_mm, h_ready = sem("xt_done"), sem("xt_copied"), sem("tok_mm"), sem("h_ready")
        ln_t, ln_mv, ln_rstd, ln_xn, ln_b, ln_out = (sem("ln_t"), sem("ln_mv"), sem("ln_rstd"), sem("ln_xn"),
                                                     sem("ln_b"), sem("ln_out"))
        hw_mm, hw_act, hw_x, u_ready = sem("hw_mm"), sem("hw_act"), sem("hw_x"), sem("u_ready")
        s1_mm, s1_row, gate_mm, gate_act = sem("s1_mm"), sem("s1_row"), sem("gate_mm"), sem("gate_act")
        qk_mm, qk_out, v_mm, v_out = sem("qk_mm"), sem("qk_out"), sem("v_mm"), sem("v_out")
        sc_mm, sc_shift, sc_exp, sc_rec, prob_ready = (sem("sc_mm"), sem("sc_shift"), sem("sc_exp"),
                                                       sem("sc_rec"), sem("prob_ready"))
        pt_mm, pt_out, att_mm, att_out = sem("pt_mm"), sem("pt_out"), sem("att_mm"), sem("att_out")
        in_mm, in_act, act_masked = sem("in_mm"), sem("in_act"), sem("act_masked")
        q_mm, q_biased, q_sq, q_var, q_rstd, q_z = (sem("q_mm"), sem("q_biased"), sem("q_sq"), sem("q_var"),
                                                    sem("q_rstd"), sem("q_z"))
        z_t, q_out, ks_mm, ks_out, n_inv = sem("z_t"), sem("q_out"), sem("ks_mm"), sem("ks_out"), sem("n_inv")
        top_done, cand_done, cand_exp, w_raw, w_norm = (sem("top_done"), sem("cand_done"), sem("cand_exp"),
                                                        sem("w_raw"), sem("w_norm"))
        cell_t, cell_out, slots_mm, pq_ready, p_hot, q_hot, pq_mm, peer_x, up_mm = (
            sem("cell_t"), sem("cell_out"), sem("slots_mm"), sem("pq_ready"), sem("p_hot"), sem("q_hot"), sem("pq_mm"), sem("peer_x"), sem("up_mm"))
        lg_mm, lg_shift, lg_exp, comb_ready, comb_t, comb_copied = (
            sem("lg_mm"), sem("lg_shift"), sem("lg_exp"), sem("comb_ready"), sem("comb_t"), sem("comb_copied"))
        ff_up, ff_gelu, ff_dn, ff_term, ff_acc = (sem("ff_up"), sem("ff_gelu"), sem("ff_dn"), sem("ff_term"),
                                                  sem("ff_acc"))
        out_t, out_copied = sem("out_t"), sem("out_copied")

        out_v = out.rearrange("(g b) l d -> g (b l) d", b=GB)
        x_v = a["x"].rearrange("(g b) t c -> g b (t c)", b=GB)

        def col(name, i=0):
            return cols[:, COL[name] + i:COL[name] + i + 1]

        def hcol(name, i=0):
            return hcols[:, COL[name] + i:COL[name] + i + 1]

        def of_group(v, gi):
            if isinstance(gi, int):
                return v[gi]
            return v[bass.ds(gi, 1)].rearrange("o a b -> (o a) b")

        def heads(t, n):
            return t[0:n, :].rearrange("p (h k) -> p h k", h=H)

        def spread(t, n, h, k):
            return t[0:n, 0:h].unsqueeze(2).broadcast_to([n, h, k])

        block = ctx.enter_context(nc.Block())
        N_CONST, N_WTS = [0], [0]

        @block.sync
        def _(sp):
            def load_x(gi):
                src = of_group(x_v, gi)
                sp.dma_start(xin[:, :, :, :].rearrange("p b s k -> p b (s k)"),
                             src[:, 0:XR * 256].rearrange("b (p k) -> p b k", k=256)).then_inc(x_in, 16)

            def const(dst, src):
                N_CONST[0] += 16
                sp.dma_start(dst, src).then_inc(const_in, 16)

            def wts(dst, src):
                N_WTS[0] += 16
                sp.dma_start(dst, src).then_inc(wts_in, 16)

            sp.sem_inc(out_done, 16)
            load_x(0)
            const(ident[:, :], a["c_ident"])
            for name, src in (("tok_b", "L0_tok_b"), ("tb", "L0_attn_tb"), ("cb", "L0_attn_cb"),
                              ("aw", "L0_attn_aW"), ("frb", "L0_attn_frb"), ("ffb", "L0_attn_ffb"),
                              ("bq", "L1_attn_bq"), ("bk", "L1_attn_bk"), ("bv", "L1_attn_bv")):
                v = a[src]
                v = v.rearrange("(o d) -> o d", d=128) if len(v.shape) == 1 else v
                const(rows[COL[name]:COL[name] + v.shape[0], :], v)
            for name, src in (("lng", "L0_ffn_ln_g"), ("lnb", "L0_ffn_ln_b")):
                for i in range(2):
                    const(rows[COL[name]:COL[name] + 1, 64 * i:64 * i + 64],
                          a[src].rearrange("(o d) -> o d", o=1))
            const(rows[0:E * FC, :], a["L1_ffn_re_b1"].rearrange("e (c f) -> (e c) f", f=128))
            const(rows[E * FC:NE * FC, :], a["L1_ffn_se_b1"].rearrange("e (c f) -> (e c) f", f=128))
            const(rows[COL["b2"]:COL["b2"] + E, :], a["L1_ffn_re_b2"])
            const(rows[COL["b2"] + E:COL["b2"] + NE, :], a["L1_ffn_se_b2"])
            const(ab[:, :], a["L0_attn_ab"].rearrange("(o d) -> o d", o=1))
            const(act_raw[:, 0:4, :], a["L0_tok_W"].rearrange("d (j k) -> d j k", k=128))
            const(act_raw[:, 4:8, :], a["L0_ffn_Wq"].rearrange("(j r) d -> r j d", r=128))
            wts(tw[:, :, :], a["L0_attn_tW"].rearrange("i d n -> d i n"))
            wts(cw[:, :, :], a["L0_attn_cW"].rearrange("i d n -> d i n"))
            wts(ffw[:, :, :], a["L0_attn_ffW"].rearrange("(i d) n -> d i n", d=128))
            wts(frw[:, :, :], a["L0_attn_frW"].rearrange("(i d) n -> d i n", d=128))
            for i in range(4):
                wts(keys[:, i, :], a[f"L0_ffn_keys{i % 2}"])
            wts(bqc[:, :], a["L0_ffn_bq"].rearrange("(o n) -> o n", o=1).broadcast_to([128, 512]))
            wts(posT[:, :], a["c_posT"])
            wts(blockmask[:, :], a["c_blockmask"])
            wts(halfones[:, :], a["c_halfones"])
            wts(merge[:, :, :], a["c_merge"])
            for i, name in enumerate(("L1_attn_Wq", "L1_attn_Wk", "L1_attn_Wv")):
                wts(act_raw[:, 8 + i, :], a[name])
            wts(act_raw[0:E, 11, :], a["L1_ffn_gate_w"])
            for dst, name in ((dnraw, "L0_ffn_expert_down"), (upR, "L0_ffn_expert_up")):
                v = a[name][0:128, :].rearrange("(p q) d -> p (q d)", q=Q8)
                for p in range(P16):
                    sp.dma_start(dst[8 * p:8 * p + 8, :, :].rearrange("t q d -> t (q d)"),
                                 v[p:p + 1, :].broadcast_to([8, Q8 * 128])).then_inc(peer_in, 16)
            for e0, e1 in ((0, 4), (4, 8), (8, 12), (12, 16)):
                sp.dma_start(w1[:, e0:e1, :], a["L1_ffn_re_w1"][e0:e1].rearrange("e d f -> d e f")).then_inc(exp_in, 16)
                sp.dma_start(w2[:, e0:e1, :, :].rearrange("p e c d -> p (e c) d"),
                             a["L1_ffn_re_w2"][e0:e1].rearrange("e (c p) d -> p (e c) d", p=128)).then_inc(exp_in, 16)
            sp.dma_start(w1[:, E:NE, :], a["L1_ffn_se_w1"].rearrange("e d f -> d e f")).then_inc(exp_in, 16)
            sp.dma_start(w2[:, E:NE, :, :].rearrange("p e c d -> p (e c) d"),
                         a["L1_ffn_se_w2"].rearrange("e (c p) d -> p (e c) d", p=128)).then_inc(exp_in, 16)

            def next_x(gi):
                sp.wait_ge(xt_done, 2 * gi)
                load_x(gi)

            def store(m):
                sp.wait_ge(out_copied, m + 2)
                dst = of_group(out_v, m)
                for s, (o, n) in enumerate(SUBS):
                    sp.dma_start(dst[o:o + n, :], otile[0:n, s, :]).then_inc(out_done, 16)

            def gates(m):
                sp.wait_ge(comb_copied, m + 1)
                mem = of_group(comb_dram, m)
                sp.dma_start(mem, combT[:, :]).then_inc(comb_out, 16)
                sp.wait_ge(comb_out, 16 * m + 16)
                for r in range(E // 4):
                    sp.wait_ge(ff_term, NE * m + 2 + (SH + 4 * (r - 1) if r > 1 else 0))
                    sp.dma_start(combB[:, r % 2, :, :].rearrange("p e n -> p (e n)"),
                                 mem[4 * r:4 * r + 4, :].rearrange("(o e) n -> o (e n)", o=1).broadcast_to([128, 4 * N])
                                 ).then_inc(comb_in[r % 2], 16)

            next_x(1)
            gates(0)
            with sp.Fori(1, G - 1) as g:
                next_x(g + 1)
                store(g - 1)
                gates(g)
            store(G - 2)
            gates(G - 1)
            store(G - 1)
            sp.wait_ge(out_done, 16 * NSUB * G + 16)

        @block.tensor
        def _(pe):
            def mm(o, lhsT, rhs, start=True, stop=True):
                return pe.matmul(o, lhsT, rhs, start=start, stop=stop)

            def tr(o, src):
                n = src.shape[0]
                return pe.transpose(o, src, ident[0:n, 0:n])

            pe.wait_ge(const_in, N_CONST[0])
            tr(B0[:, 0:NROWS], rows[:, :]).then_inc(setup_pe, 1)
            for j in range(4):
                ins = tr(B1[:, 128 * j:128 * j + 128], act_raw[:, j, :])
            ins.then_inc(setup_pe, 1)
            for j in range(4):
                ins = tr(B2[:, 128 * j:128 * j + 128], act_raw[:, 4 + j, :])
            ins.then_inc(setup_pe, 1)
            pe.wait_ge(wts_in, N_WTS[0])
            for j in range(3):
                tr(B3[:, 128 * j:128 * j + 128], act_raw[:, 8 + j, :])
            tr(B3[:, 384:384 + E], act_raw[0:E, 11, :]).then_inc(setup_pe, 1)
            pe.wait_ge(setup_p, 3)
            tr(UP[0][:, 0:PK], keys2[:, :, :].rearrange("p c k -> p (c k)")).then_inc(setup_pe, 1)
            pe.wait_ge(peer_in, 16 * 2 * P16)
            for q in range(Q8):
                ins = tr(DN[q // 4][:, 128 * (q % 4):128 * (q % 4) + 128], dnraw[:, q, :])
            ins.then_inc(setup_pe, 1)
            pe.wait_ge(setup_a, 4)
            pe.wait_ge(setup_v, 3)

            def group(gi, abc, moe):
                m = gi - 1

                def ln_in(i):
                    pe.wait_ge(h_ready, 4 * gi + i + 1)
                    b = B3 if i == 0 else B0
                    for s, (o, n) in enumerate(SUBS):
                        ins = tr(b[0:n, 128 * s:128 * s + 128], hT[:, o:o + n])
                    ins.then_inc(ln_t, 1)

                def ln_back(i):
                    pe.wait_ge(ln_xn, 4 * gi + i + 1)
                    b = B0 if i == 0 else B1
                    for s, (o, n) in enumerate(SUBS):
                        ins = tr(b[:, o:o + n], xn[0:n, s, :])
                    ins.then_inc(ln_b, 1)

                def experts(e0, e1):
                    if not moe:
                        return
                    for e in range(e0, e1):
                        for f in range(FC):
                            if e < NE:
                                j = (NE * m + e) * FC + f + 1
                                pe.wait_ge(ff_gelu, j)
                                mm(UP[f % 2][:, 0:N], w1[:, EORD[e], 128 * f:128 * f + 128], xd[:, :]).then_inc(ff_up, 1)
                            if e > 0:
                                x = NE * m + e
                                if f == 0:
                                    pe.wait_ge(ff_term, x)
                                    if e == 1:
                                        pe.wait_ge(out_copied, m + 1)
                                pe.wait_ge(ff_gelu, (x - 1) * FC + f + 3)
                                ins = mm(DN[(e - 1) % 2][:, 0:N], w2[:, EORD[e - 1], f, :], hid[:, (e - 1) % 2, f, :],
                                         start=(f == 0), stop=(f == FC - 1))
                        if e > 0:
                            ins.then_inc(ff_dn, 1)

                def probs_times_values(i):
                    pe.wait_ge(prob_ready, 2 * gi + i + 1)
                    for b in range(GB):
                        ins = tr(B0[0:L, L * b:L * b + L], prob[:, L * b:L * b + L])
                    ins.then_inc(pt_mm, 1)
                    pe.wait_ge(pt_out, 2 * gi + i + 1)
                    pe.wait_ge(v_out, 2 * gi + i + 1)
                    for b in range(GB):
                        ins = mm(B1[:, L * b:L * b + L], vtok[:, b, :], probT[:, L * b:L * b + L])
                    ins.then_inc(att_mm, 1)

                def front(s):
                    o, n = SUBS[s]
                    k = 3 * gi + s + 1
                    if s > 0:
                        pe.wait_ge(ks_out, 2 * (k - 1))
                    mm(B0[0:n, :], hnT[:, o:o + n], wqcT[:, :]).then_inc(q_mm, 1)
                    pe.wait_ge(q_z, k)
                    for c in range(HP):
                        ins = tr(B1[:, 128 * c:128 * c + n], qc[0:n, 128 * c:128 * c + 128])
                    ins.then_inc(z_t, 1)
                    pe.wait_ge(q_out, k)
                    if s == 0:
                        pe.wait_ge(in_act, Q8 * gi + Q8)
                    elif s == 1:
                        pe.wait_ge(ks_out, 2 * (k - 1))
                    else:
                        pe.wait_ge(peer_x, 3 * gi + 1)
                    for c in range(HP):
                        mm(B0[0:n, 4 * c:4 * c + 4], sqT[:, c, 0:n], halfones[:, :])
                        ins = mm((B2, B3)[c // 2][0:n, 256 * (c % 2):256 * (c % 2) + 256], qnT[:, c, 0:n], keysBD[:, :])
                    ins.then_inc(ks_mm, 1)

                def turn_cells(s):
                    o, n = SUBS[s]
                    k = 3 * gi + s + 1
                    pe.wait_ge(w_norm, k)
                    pe.wait_ge(w_raw, k)
                    if s < 2:
                        pe.wait_ge(ks_out, 2 * (k + 1))
                    for c in range(HP):
                        tr(B0[0:NK, n * c:n * c + n], wn[0:n, 2 * c:2 * c + 2, :].rearrange("p h k -> p (h k)"))
                        ins = tr(B1[0:NK, n * c:n * c + n],
                                 epick[0:n, 2 * c:2 * c + 2, :].rearrange("p h k -> p (h k)"))
                    ins.then_inc(cell_t, 1)
                    pe.wait_ge(cell_out, k)
                    for i in range(2):
                        for c in range(2):
                            mm(B0[0:NS, i * n:i * n + n], merge[:, c, :], wcell[:, (2 * i + c) * n:(2 * i + c + 1) * n],
                               start=(c == 0), stop=(c == 1))
                        for c in range(2):
                            ins = mm(B0[0:NS, (2 + i) * n:(3 + i) * n], merge16[:, c, :],
                                     ecell[:, (2 * i + c) * n:(2 * i + c + 1) * n], start=(c == 0), stop=(c == 1))
                    ins.then_inc(slots_mm, 1)

                def sums(s):
                    o, n = SUBS[s]
                    k = 3 * gi + s + 1
                    pe.wait_ge(p_hot, k)
                    pe.wait_ge(q_hot, k)
                    if s == 2:
                        pe.wait_ge(peer_x, k - 1)
                    for t in range(n // 8):
                        for c in range(2):
                            x = n * c + 8 * t
                            for part in range(2):
                                ins = mm((B2, B3)[t // 8][:, 64 * (t % 8):64 * (t % 8) + 64], ph[:, x // 8, :, :].rearrange("p k t -> p (k t)"),
                                         qw[:, part, :, x:x + 8], start=(c == 0 and part == 0),
                                         stop=(c == 1 and part == 1))
                    ins.then_inc(pq_mm, 1)

                if abc:
                    pe.wait_ge(x_in, 16 * gi + 16)
                    for s in range(2):
                        for b in range(GB):
                            ins = tr((B0, B1)[s][:, XR * b:XR * b + XR], xin[:, b, s, :])
                        ins.then_inc(xt_done, 1)
                    pe.wait_ge(xt_copied, 2 * gi + 2)
                    if moe:
                        pe.wait_ge(comb_copied, gi)
                    for j in range(4):
                        v = xT[:, j % 2, :].rearrange("p (b r) -> p b r", r=XR)[:, :, j // 2:j // 2 + L]
                        ins = mm(B2[:, 0:N], wtokT[:, j, :], v, start=(j == 0), stop=(j == 3))
                    ins.then_inc(tok_mm, 1)
                    ln_in(0)
                if moe:
                    pe.wait_ge(exp_in, 160)
                experts(0, 1)
                if abc:
                    ln_back(0)
                experts(1, 2)
                if abc:
                    for i in range(2):
                        if i == 0:
                            pe.wait_ge(ln_out, 4 * gi + 1)
                        else:
                            pe.wait_ge(hw_x, 2 * gi + 1)
                        src = (inT, x1T)[i]
                        mm((B1, B3)[i][:, 0:N], tw[:, i, :], src[:, :]).then_inc(hw_mm, 1)
                        mm((B2, B0)[i][:, 0:N], cw[:, i, :], src[:, :]).then_inc(hw_mm, 1)
                        experts(2 + i, 3 + i)
                    pe.wait_ge(hw_x, 2 * gi + 2)
                    mm(B1[0:1, 0:N], col("aw", 0), x2T[:, :]).then_inc(s1_mm, 1)
                    for b in range(GB):
                        ins = tr(B2[0:L, 128 * b:128 * b + 128], x2T[:, L * b:L * b + L])
                    ins.then_inc(v_mm, 1)
                    pe.wait_ge(u_ready, gi + 1)
                    pe.wait_ge(s1_row, gi + 1)
                    for b in range(GB):
                        t = slice(L * b, L * b + L)
                        mm(B3[0:L, t], uT[:, t], x2T[:, t], stop=False)
                        ins = mm(B3[0:L, t], s1row[0:1, t], ones[0:1, 0:L], start=False)
                    ins.then_inc(sc_mm, 1)
                else:
                    experts(2, 4)
                experts(4, 5)
                if abc:
                    probs_times_values(0)
                    pe.wait_ge(att_out, gi + 1)
                    for w, b in ((ffw, B2), (frw, B3)):
                        mm(b[:, 0:N], w[:, 0, :], inT[:, :], stop=False)
                        mm(b[:, 0:N], w[:, 1, :], attT[:, :], start=False).then_inc(gate_mm, 1)
                experts(5, 6)
                if abc:
                    ln_in(1)
                experts(6, 7)
                if abc:
                    ln_back(1)
                    pe.wait_ge(ln_out, 4 * gi + 2)
                    for q in range(Q8):
                        if q >= 2:
                            pe.wait_ge(in_act, Q8 * gi + q - 1)
                        mm((B2, B3)[q % 2][:, 0:N], dnT[:, q, :], hnT[:, :]).then_inc(in_mm, 1)
                    front(0)
                experts(7, 9)
                if abc:
                    front(1)
                experts(9, 11)
                if abc:
                    turn_cells(0)
                experts(11, 12)
                if abc:
                    sums(0)
                    front(2)
                experts(12, 14)
                if abc:
                    turn_cells(1)
                experts(14, 15)
                if abc:
                    sums(1)
                    turn_cells(2)
                experts(15, 16)
                if abc:
                    sums(2)
                    pe.wait_ge(peer_x, 3 * gi + 3)
                    for q in range(Q8):
                        ins = mm(B0[:, 0:N], upR[:, q, :], act[:, q, :], start=(q == 0), stop=(q == Q8 - 1))
                    ins.then_inc(up_mm, 1)
                    ln_in(2)
                experts(16, 17)
                if abc:
                    ln_back(2)
                    pe.wait_ge(ln_out, 4 * gi + 3)
                    mm(B2[:, 0:N], wqkvT[:, 0, :], inT[:, :]).then_inc(qk_mm, 1)
                    mm(B3[:, 0:N], wqkvT[:, 1, :], inT[:, :]).then_inc(qk_mm, 1)
                    for b in range(GB):
                        ins = mm(B1[0:L, 128 * b:128 * b + 128], inT[:, L * b:L * b + L], wqkvT[:, 2, :])
                    ins.then_inc(v_mm, 1)
                    pe.wait_ge(qk_out, 2 * gi + 2)
                    for b in range(GB):
                        t = slice(L * b, L * b + L)
                        ins = mm(B3[0:L, t], qT[:, t], kT[:, t])
                    ins.then_inc(sc_mm, 1)
                experts(17, 18)
                if abc:
                    probs_times_values(1)
                experts(18, 19)
                if abc:
                    ln_in(3)
                if moe:
                    pe.wait_ge(ff_acc, (NE + 1) * gi)
                    for s, (o, n) in enumerate(SUBS):
                        ins = tr(DN[0][0:n, 128 * s:128 * s + 128], acc[:, o:o + n])
                    ins.then_inc(out_t, 1)
                if abc:
                    ln_back(3)
                    pe.wait_ge(ln_out, 4 * gi + 4)
                    for s, (o, n) in enumerate(SUBS):
                        ins = mm(B3[0:n, E * s:E * s + E], xd[:, o:o + n], gateT[:, :])
                    ins.then_inc(lg_mm, 1)
                    pe.wait_ge(comb_ready, gi + 1)
                    for s, (o, n) in enumerate(SUBS):
                        ins = tr(B2[0:E, o:o + n], comb[0:n, s, :])
                    ins.then_inc(comb_t, 1)

            group(0, True, False)
            with pe.Fori(1, G) as g:
                group(g, True, True)
            group(G, False, True)

        @block.gpsimd
        def _(pool):
            pool.memset(ones[:, :], 1.0)
            pool.memset(nhalf[:, :], -0.5)
            pool.memset(keysBD[:, :], 0.0)
            pool.memset(mv[:, :, :], 1.0)
            pool.memset(lg[:, :, :], -1.0)
            pool.memset(m8[:, :, :], -1.0)
            pool.memset(lg2[:, :, :], TAKEN)
            pool.memset(ge[:, :, :], 0.0)
            pool.memset(t8[:, :, :], -1.0).then_inc(setup_p, 1)
            pool.wait_ge(setup_p, 1)
            pool.wait_ge(setup_v, 1)
            pool.tensor_tensor(kn[:, :], kn[:, :], nhalf[0:PK, 0:2], ALU.pow).then_inc(setup_p, 1)
            pool.wait_ge(setup_p, 2)
            for i in range(2):
                ins = pool.tensor_tensor(keys2[:, 2 * i:2 * i + 2, :], keys[:, 2 * i:2 * i + 2, :],
                                         spread(kn, PK, 2, HALF), ALU.mult)
            ins.then_inc(setup_p, 1)

            def group(gi, abc, moe):
                links = [0]

                def link(ins):
                    links[0] += 1
                    ins.then_inc(p_link, 1)
                    pool.wait_ge(p_link, gi * P_LINKS + links[0])

                def own_wait():
                    pool.sem_inc(p_met, 1)

                def ln(i):
                    pool.wait_ge(ln_mv, 4 * gi + i + 1)
                    own_wait()
                    link(pool.tensor_scalar(rstd[:, :], mv[:, :, 1], EPS, None, ALU.add))
                    pool.tensor_tensor(rstd[:, :], rstd[:, :], nhalf[:, 0:NSUB], ALU.pow).then_inc(ln_rstd, 1)

                def attention(i):
                    pool.wait_ge(sc_rec, 2 * gi + i + 1)
                    v = prob[:, :].rearrange("p (b j) -> p b j", j=L)
                    pool.tensor_tensor(v, v, spread(arec, L, GB, L), ALU.mult).then_inc(prob_ready, 1)

                def front(s):
                    n = SUBS[s][1]
                    k = 3 * gi + s + 1
                    pool.wait_ge(q_var, k)
                    own_wait()
                    link(pool.tensor_scalar(qr[0:n, :], qv[0:n, :], 1.0 / QD, EPS, ALU.mult, ALU.add))
                    pool.tensor_tensor(qr[0:n, :], qr[0:n, :], nhalf[0:n, 0:H], ALU.pow).then_inc(q_rstd, 1)
                    pool.wait_ge(ks_out, 2 * k)
                    own_wait()
                    link(pool.tensor_scalar(inv[0:n, :], nrm[0:n, :], 1e-24, None, ALU.max))
                    pool.tensor_tensor(inv[0:n, :], inv[0:n, :], nhalf[0:n, :], ALU.pow).then_inc(n_inv, 1)

                def cells(s):
                    n = SUBS[s][1]
                    pool.wait_ge(top_done, 3 * gi + s + 1)
                    for src, dst in ((topn, cand[0:n]), (idf, cexpert[0:n, s % 2])):
                        v = src[0:n, :, :].rearrange("p (h t) k -> p h t k", t=2)
                        o = 0
                        for r, m, w in CELLS:
                            d = dst[:, :, o:o + m * w].rearrange("p h (m w) -> p h m w", w=w)
                            ins = pool.tensor_tensor(
                                d, v[:, :, 0, r:r + m].unsqueeze(3).broadcast_to([n, H, m, w]),
                                v[:, :, 1, 0:w].unsqueeze(2).broadcast_to([n, H, m, w]), ALU.add)
                            o += m * w
                    ins.then_inc(cand_done, 1)

                def weights(s):
                    n = SUBS[s][1]
                    pool.wait_ge(w_raw, 3 * gi + s + 1)
                    pool.tensor_tensor(wn[0:n, :, :], cw_[0:n, :, :], spread(zr, n, H, NC), ALU.mult).then_inc(w_norm, 1)

                def onehot(s):
                    n = SUBS[s][1]
                    pool.wait_ge(pq_ready, 3 * gi + s + 1)
                    own_wait()
                    for p in range(P16):
                        ins = pool.tensor_scalar(ph[:, 0:n // 4, p, :], pi[:, 0:2 * n].rearrange("p (g t) -> p g t", t=8),
                                                 float(p), None, ALU.is_equal)
                    ins.then_inc(p_hot, 1)

                def terms(e0, e1):
                    if not moe:
                        return
                    m = gi - 1
                    for e in range(max(e0 - 1, 0), e1 - 1):
                        pool.wait_ge(ff_term, NE * m + e + 3)
                        pool.wait_ge(ff_acc, (NE + 1) * m + e + 1)
                        pool.tensor_tensor(acc[:, :], acc[:, :], term[:, e % 2, :], ALU.add).then_inc(ff_acc, 1)

                if abc:
                    ln(0)
                terms(0, 4)
                if abc:
                    attention(0)
                terms(4, 6)
                if abc:
                    ln(1)
                terms(6, 7)
                if abc:
                    pool.wait_ge(in_act, Q8 * gi + Q8)
                    v = act[:, :, :].rearrange("p q (g t) -> p (q g) t", t=8)
                    pool.tensor_tensor(v, v, blockmask[:, :].unsqueeze(1).broadcast_to([128, Q8 * N // 8, 8]),
                                       ALU.mult).then_inc(act_masked, 1)
                    front(0)
                terms(7, 9)
                if abc:
                    front(1)
                    cells(0)
                    weights(0)
                terms(9, 12)
                if abc:
                    cells(1)
                    onehot(0)
                    weights(1)
                    front(2)
                terms(12, 14)
                if abc:
                    cells(2)
                    onehot(1)
                terms(14, 15)
                if abc:
                    weights(2)
                    onehot(2)
                terms(15, 16)
                if abc:
                    ln(2)
                terms(16, 18)
                if abc:
                    attention(1)
                terms(18, 19)
                if abc:
                    ln(3)
                    pool.wait_ge(h_ready, 4 * gi + 4)
                    if moe:
                        pool.wait_ge(out_t, gi)
                    own_wait()
                    pool.tensor_copy(acc[:, :], hT[:, :]).then_inc(ff_acc, 1)
                    assert links[0] == P_LINKS, f"P_LINKS {links}"

            group(0, True, False)
            with pool.Fori(1, G) as g:
                group(g, True, True)
            group(G, False, True)

        @block.scalar
        def _(ae):
            ae.sem_inc(ff_gelu, 2)
            ae.sem_inc(out_copied, 1)
            ae.wait_ge(setup_pe, 1)
            ae.copy(cols[:, :], B0[:, 0:NROWS])
            ae.mul(hcols[:, :], B0[:, 0:NROWS], 0.5).then_inc(setup_a, 1)
            ae.wait_ge(setup_pe, 2)
            ae.copy(wtokT[:, :, :].rearrange("p j d -> p (j d)"), B1[:, :]).then_inc(setup_a, 1)
            ae.wait_ge(setup_pe, 4)
            ae.copy(wqkvT[:, :, :].rearrange("p j d -> p (j d)"), B3[:, 0:384])
            ae.copy(gateT[:, :], B3[:, 384:384 + E]).then_inc(setup_a, 1)
            ae.wait_ge(setup_pe, 6)
            for i in range(2):
                ins = ae.copy(dnT[:, 4 * i:4 * i + 4, :].rearrange("p q d -> p (q d)"), DN[i][:, :])
            ins.then_inc(setup_a, 1)
            ae.wait_ge(setup_a, 4)

            def group(gi, abc, moe):
                def gelus(e0, e1):
                    if not moe:
                        return
                    m = gi - 1
                    for e in range(e0, min(e1, NE)):
                        for f in range(FC):
                            ae.wait_ge(ff_up, (NE * m + e) * FC + f + 1)
                            if f == 0:
                                ae.wait_ge(ff_dn, NE * m + e + 1)
                            ae.activation(hid[:, e % 2, f, :], UP[f % 2][:, 0:N], ACT.Gelu,
                                          bias=col("b1", EORD[e] * FC + f)).then_inc(ff_gelu, 1)

                def tanh_half(dst, src, name, i=0):
                    return ae.activation(dst, src, ACT.Tanh, bias=hcol(name, i), scale=0.5)

                def exps(i):
                    ae.wait_ge(sc_shift, 2 * gi + i + 1)
                    ae.activation(prob[:, :], prob[:, :], ACT.Exp).then_inc(sc_exp, 1)

                def prob_turned(i):
                    ae.wait_ge(pt_mm, 2 * gi + i + 1)
                    ae.copy(probT[:, :], B0[0:L, 0:N]).then_inc(pt_out, 1)

                def front(s):
                    n = SUBS[s][1]
                    k = 3 * gi + s + 1
                    ae.wait_ge(q_biased, k)
                    ae.activation(sq[0:n, :], qc[0:n, :], ACT.Square).then_inc(q_sq, 1)
                    ae.wait_ge(z_t, k)
                    v = B1[:, :].rearrange("p (c n) -> p c n", n=128)[:, :, 0:n]
                    ae.activation(qnT[:, :, 0:n], v, ACT.Identity, bias=col("lnb"), scale=col("lng"))
                    ae.activation(sqT[:, :, 0:n], v, ACT.Square, bias=col("lnb"), scale=col("lng")).then_inc(q_out, 1)
                    ae.wait_ge(ks_mm, k)
                    ae.copy(nrm[0:n, :], B0[0:n, 0:2 * H]).then_inc(ks_out, 1)
                    if s > 0:
                        ae.wait_ge(top_done, k - 1)
                    ae.copy(sc[0:n, 0:H, :].rearrange("p c k -> p (c k)"), B2[0:n, :])
                    ae.copy(sc[0:n, H:2 * H, :].rearrange("p c k -> p (c k)"), B3[0:n, :]).then_inc(ks_out, 1)

                def cells_turned(s):
                    n = SUBS[s][1]
                    ae.wait_ge(cell_t, 3 * gi + s + 1)
                    ae.copy(wcell[:, 0:4 * n], B0[0:NK, 0:4 * n])
                    ae.copy(ecell[:, 0:4 * n], B1[0:NK, 0:4 * n]).then_inc(cell_out, 1)

                def cell_exps(s):
                    n = SUBS[s][1]
                    ae.wait_ge(cand_done, 3 * gi + s + 1)
                    ae.activation(cexp[0:n, :, :], cand[0:n, :, :], ACT.Exp).then_inc(cand_exp, 1)

                if abc:
                    ae.wait_ge(xt_done, 2 * gi + 1)
                    ae.copy(xT[:, 0, :], B0[:, 0:GB * XR]).then_inc(xt_copied, 1)
                    ae.wait_ge(tok_mm, gi + 1)
                    if moe:
                        ae.wait_ge(ff_acc, (NE + 1) * (gi - 1) + 1)
                    ae.activation(hT[:, :], B2[:, 0:N], ACT.Identity, bias=col("tok_b")).then_inc(h_ready, 1)
                gelus(0, 1)
                if abc:
                    ae.wait_ge(ln_b, 4 * gi + 1)
                    ae.copy(inT[:, :], B0[:, 0:N]).then_inc(ln_out, 1)
                gelus(1, 2)
                for i in range(2):
                    if abc:
                        ae.wait_ge(hw_mm, 4 * gi + 2 * i + 1)
                        ae.activation(tT[:, :], (B1, B3)[i][:, 0:N], ACT.Relu, bias=col("tb", i)).then_inc(hw_act, 1)
                        ae.wait_ge(hw_mm, 4 * gi + 2 * i + 2)
                        tanh_half(cT[:, :], (B2, B0)[i][:, 0:N], "cb", i).then_inc(hw_act, 1)
                    gelus(2 + i, 3 + i)
                if abc:
                    ae.wait_ge(s1_mm, gi + 1)
                    ae.activation(s1row[:, :], B1[0:1, 0:N], ACT.Identity, bias=ab[0:1, 0:1]).then_inc(s1_row, 1)
                    ae.wait_ge(v_mm, 2 * gi + 1)
                    ae.copy(vtok[:, :, :].rearrange("p b d -> p (b d)"), B2[0:L, :]).then_inc(v_out, 1)
                    exps(0)
                gelus(4, 5)
                if abc:
                    prob_turned(0)
                    ae.wait_ge(att_mm, 2 * gi + 1)
                    ae.copy(attT[:, :], B1[:, 0:N]).then_inc(att_out, 1)
                    ae.wait_ge(gate_mm, 2 * gi + 1)
                    tanh_half(tT[:, :], B2[:, 0:N], "ffb").then_inc(gate_act, 1)
                    ae.wait_ge(gate_mm, 2 * gi + 2)
                    tanh_half(cT[:, :], B3[:, 0:N], "frb").then_inc(gate_act, 1)
                gelus(5, 7)
                if abc:
                    ae.wait_ge(ln_b, 4 * gi + 2)
                    ae.copy(hnT[:, :], B1[:, 0:N]).then_inc(ln_out, 1)
                    for q in range(Q8):
                        ae.wait_ge(in_mm, Q8 * gi + q + 1)
                        ae.activation(act[:, q, :], (B2, B3)[q % 2][:, 0:N], ACT.Gelu).then_inc(in_act, 1)
                    front(0)
                gelus(7, 9)
                if abc:
                    front(1)
                    cell_exps(0)
                gelus(9, 11)
                if abc:
                    cells_turned(0)
                gelus(11, 12)
                if abc:
                    cell_exps(1)
                    front(2)
                gelus(12, 14)
                if abc:
                    cells_turned(1)
                    cell_exps(2)
                gelus(14, 15)
                if abc:
                    cells_turned(2)
                gelus(15, 17)
                if abc:
                    ae.wait_ge(qk_mm, 2 * gi + 1)
                    ae.activation(qT[:, :], B2[:, 0:N], ACT.Identity, bias=col("bq")).then_inc(qk_out, 1)
                    ae.wait_ge(qk_mm, 2 * gi + 2)
                    ae.activation(kT[:, :], B3[:, 0:N], ACT.Identity, bias=col("bk")).then_inc(qk_out, 1)
                    ae.wait_ge(v_mm, 2 * gi + 2)
                    ae.copy(vtok[:, :, :].rearrange("p b d -> p (b d)"), B1[0:L, :]).then_inc(v_out, 1)
                    exps(1)
                gelus(17, 18)
                if abc:
                    prob_turned(1)
                if moe:
                    ae.wait_ge(out_t, gi)
                    ae.wait_ge(out_done, 16 * NSUB * (gi - 1) + 16)
                    for s, (o, n) in enumerate(SUBS):
                        ins = ae.copy(otile[0:n, s, :], DN[0][0:n, 128 * s:128 * s + 128])
                    ins.then_inc(out_copied, 1)
                if abc:
                    ae.wait_ge(ln_b, 4 * gi + 4)
                    ae.copy(xd[:, :], B1[:, 0:N]).then_inc(ln_out, 1)
                    for i in range(2):
                        ae.wait_ge(lg_shift, 2 * gi + i + 1)
                        ae.activation(ge[:, :, :], ge[:, :, :], ACT.Exp).then_inc(lg_exp, 1)
                    ae.wait_ge(comb_t, gi + 1)
                    if moe:
                        ae.wait_ge(comb_out, 16 * gi)
                    ae.copy(combT[:, :], B2[0:E, 0:N]).then_inc(comb_copied, 1)

            group(0, True, False)
            with ae.Fori(1, G) as g:
                group(g, True, True)
            group(G, False, True)

        @block.vector
        def _(dve):
            dve.sem_inc(ff_dn, 2)
            dve.sem_inc(ff_term, 2)
            chain = [0]

            def set_link(ins):
                chain[0] += 1
                ins.then_inc(v_set, 1)
                dve.wait_ge(v_set, chain[0])

            dve.wait_ge(wts_in, N_WTS[0])
            set_link(dve.tensor_tensor(sq[0:PK, 0:2 * HALF], keys[:, 0:2, :].rearrange("p c k -> p (c k)"),
                                       keys[:, 0:2, :].rearrange("p c k -> p (c k)"), ALU.mult))
            set_link(dve.tensor_reduce(kn[:, :], sq[0:PK, 0:2 * HALF].rearrange("p (c k) -> p c k", k=HALF), AX, ALU.add))
            dve.tensor_scalar(kn[:, :], kn[:, :], 1e-24, None, ALU.max).then_inc(setup_v, 1)
            dve.wait_ge(setup_pe, 3)
            set_link(dve.tensor_copy(wqcT[:, :], B2[:, :]))
            for t in (wqcT, bqc):
                set_link(dve.tensor_reduce(bqm[:, :], heads(t, 128), AX, ALU.add))
                set_link(dve.tensor_scalar(bqm[:, :], bqm[:, :], 1.0 / QD, None, ALU.mult))
                set_link(dve.tensor_tensor(heads(t, 128), heads(t, 128), spread(bqm, 128, H, QD), ALU.subtract))
            dve.sem_inc(setup_v, 1)
            dve.tensor_copy(merge16[:, :, :], merge[:, :, :])
            dve.wait_ge(setup_p, 1)
            dve.wait_ge(setup_pe, 5)
            for c in range(4):
                ins = dve.tensor_copy(keysBD[HALF * c:HALF * c + HALF, PK * c:PK * c + PK],
                                      UP[0][HALF * c:HALF * c + HALF, 0:PK])
            ins.then_inc(setup_v, 1)
            dve.wait_ge(setup_v, 3)

            def group(gi, abc, moe):
                m = gi - 1
                links = [0]

                def link(ins):
                    links[0] += 1
                    ins.then_inc(v_link, 1)
                    dve.wait_ge(v_link, gi * V_LINKS + links[0])

                def own_wait():
                    dve.sem_inc(v_met, 1)

                def ln(i):
                    b = B3 if i == 0 else B0
                    dve.wait_ge(ln_t, 4 * gi + i + 1)
                    for s, (o, n) in enumerate(SUBS):
                        ins = dve.bn_stats(bn[0:n, s, :], b[0:n, 128 * s:128 * s + 128])
                    link(ins)
                    own_wait()
                    for s, (o, n) in enumerate(SUBS):
                        ins = dve.bn_aggr(mv[0:n, s, :], bn[0:n, s, :])
                    ins.then_inc(ln_mv, 1)
                    dve.wait_ge(ln_rstd, 4 * gi + i + 1)
                    for s, (o, n) in enumerate(SUBS):
                        ins = dve.tensor_scalar(xn[0:n, s, :], b[0:n, 128 * s:128 * s + 128], mv[0:n, s, 0:1],
                                                rstd[0:n, s:s + 1], ALU.subtract, ALU.mult)
                    ins.then_inc(ln_xn, 1)

                def terms(e0, e1):
                    if not moe:
                        return
                    for e in range(max(e0 - 1, 0), e1 - 1):
                        x = NE * m + e
                        dve.wait_ge(ff_dn, x + 3)
                        dve.wait_ge(ff_acc, (NE + 1) * m + max(e, 1))
                        b = DN[e % 2][:, 0:N]
                        if EORD[e] >= E:
                            ins = dve.tensor_scalar(term[:, e % 2, :], b, col("b2", EORD[e]), 1.0 / SH, ALU.add, ALU.mult)
                        else:
                            r = EORD[e] // 4
                            if EORD[e] % 4 == 0:
                                dve.wait_ge(comb_in[r % 2], 16 * (E // 8 * m + r // 2 + 1))
                            ins = dve.scalar_tensor_tensor(term[:, e % 2, :], b, col("b2", EORD[e]),
                                                           combB[:, r % 2, EORD[e] % 4, :], ALU.add, ALU.mult)
                        ins.then_inc(ff_term, 1)

                def attention(i):
                    dve.wait_ge(sc_mm, 2 * gi + i + 1)
                    s = B3[0:L, 0:N].rearrange("p (b j) -> p b j", j=L)
                    p = prob[:, :].rearrange("p (b j) -> p b j", j=L)
                    link(dve.tensor_reduce(amax[:, :], s, AX, ALU.max))
                    if i == 0:
                        link(dve.tensor_scalar(amax[:, :], amax[:, :], 0.0, None, ALU.max))
                        dve.scalar_tensor_tensor(p, s, 0.0, spread(amax, L, GB, L), ALU.max,
                                                 ALU.subtract).then_inc(sc_shift, 1)
                    else:
                        dve.tensor_tensor(p, s, spread(amax, L, GB, L), ALU.subtract).then_inc(sc_shift, 1)
                    dve.wait_ge(sc_exp, 2 * gi + i + 1)
                    link(dve.tensor_reduce(asum[:, :], p, AX, ALU.add))
                    dve.reciprocal(arec[:, :], asum[:, :]).then_inc(sc_rec, 1)

                def front(s):
                    n = SUBS[s][1]
                    k = 3 * gi + s + 1
                    dve.wait_ge(q_mm, k)
                    dve.tensor_tensor(qc[0:n, :], B0[0:n, :], bqc[0:n, :], ALU.add).then_inc(q_biased, 1)
                    dve.wait_ge(q_sq, k)
                    dve.tensor_reduce(qv[0:n, :], heads(sq, n), AX, ALU.add).then_inc(q_var, 1)
                    dve.wait_ge(q_rstd, k)
                    dve.tensor_tensor(heads(qc, n), heads(qc, n), spread(qr, n, H, QD), ALU.mult).then_inc(q_z, 1)

                def search(s):
                    n = SUBS[s][1]
                    k = 3 * gi + s + 1
                    dve.wait_ge(ks_out, 2 * k)
                    own_wait()
                    for c in range(2 * H):
                        ins = dve.max(top[0:n, c, 0:8], sc[0:n, c, :])
                    link(ins)
                    own_wait()
                    for c in range(2 * H):
                        ins = dve.max_index(idx[0:n, c, 0:8], top[0:n, c, 0:8], sc[0:n, c, :])
                    link(ins)
                    own_wait()
                    for c in range(2 * H):
                        ins = dve.match_replace(sc[0:n, c, :], top[0:n, c, 0:8], sc[0:n, c, :], TAKEN)
                    link(ins)
                    own_wait()
                    for c in range(2 * H):
                        ins = dve.max(top[0:n, c, 8:16], sc[0:n, c, :])
                    link(ins)
                    own_wait()
                    for c in range(2 * H):
                        ins = dve.max_index(idx[0:n, c, 8:16], top[0:n, c, 8:16], sc[0:n, c, :])
                    link(ins)
                    dve.wait_ge(n_inv, k)
                    dve.tensor_tensor(topn[0:n], top[0:n], spread(inv, n, 2 * H, K), ALU.mult)
                    dve.tensor_copy(idf[0:n], idx[0:n]).then_inc(top_done, 1)

                def pick(s):
                    n = SUBS[s][1]
                    k = 3 * gi + s + 1
                    dve.wait_ge(cand_done, k)
                    own_wait()
                    for h in range(H):
                        ins = dve.max(best[0:n, h, 0:8], cand[0:n, h, :])
                    link(ins)
                    own_wait()
                    for h in range(H):
                        ins = dve.match_replace(cand2[0:n, h, :], best[0:n, h, 0:8], cand[0:n, h, :], TAKEN)
                    link(ins)
                    own_wait()
                    for h in range(H):
                        ins = dve.max(best[0:n, h, 8:16], cand2[0:n, h, :])
                    link(ins)
                    own_wait()
                    for h in range(H):
                        ins = dve.match_replace(cand2[0:n, h, :], best[0:n, h, 8:16], cand2[0:n, h, :], TAKEN)
                    link(ins)
                    dve.wait_ge(cand_exp, k)
                    dve.scalar_tensor_tensor(epick[0:n].rearrange("p h k -> p (h k)"),
                                             cand2[0:n].rearrange("p h k -> p (h k)"), TAKEN / 10,
                                             cexpert[0:n, s % 2].rearrange("p h k -> p (h k)"), ALU.is_lt, ALU.mult)
                    link(dve.scalar_tensor_tensor(cw_[0:n].rearrange("p h k -> p (h k)"),
                                                  cand2[0:n].rearrange("p h k -> p (h k)"), TAKEN / 10,
                                                  cexp[0:n].rearrange("p h k -> p (h k)"), ALU.is_lt, ALU.mult))
                    link(dve.tensor_reduce(z[0:n], cw_[0:n], AX, ALU.add))
                    link(dve.tensor_scalar(z[0:n], z[0:n], 1.0 / WSCALE, None, ALU.mult))
                    dve.reciprocal(zr[0:n], z[0:n]).then_inc(w_raw, 1)

                def hot(s):
                    n = SUBS[s][1]
                    k = 3 * gi + s + 1
                    w = 2 * n
                    dve.wait_ge(slots_mm, k)
                    dve.tensor_scalar(pi[:, 0:w], B0[0:NS, w:2 * w], 0.125, -0.4375, ALU.mult, ALU.add)
                    link(dve.tensor_copy(whi[:, 0:w], B0[0:NS, 0:w]))
                    dve.scalar_tensor_tensor(qi[:, 0:w], pi[:, 0:w], -8.0, B0[0:NS, w:2 * w], ALU.mult, ALU.add)
                    dve.tensor_tensor(wlo[:, 0:w], B0[0:NS, 0:w], whi[:, 0:w], ALU.subtract).then_inc(pq_ready, 1)
                    dve.wait_ge(pq_ready, k)
                    for q in range(Q8):
                        ins = dve.tensor_scalar(qh[:, q, 0:w], qi[:, 0:w], float(q), None, ALU.is_equal)
                    link(ins)
                    for part, src in enumerate((whi, wlo)):
                        ins = dve.tensor_tensor(qw[:, part, :, 0:w], qh[:, :, 0:w],
                                                src[:, 0:w].unsqueeze(1).broadcast_to([NS, Q8, w]), ALU.mult)
                    ins.then_inc(q_hot, 1)

                def own_blocks(s):
                    o, n = SUBS[s]
                    if s == 0:
                        dve.wait_ge(act_masked, gi + 1)
                    dve.wait_ge(pq_mm, 3 * gi + s + 1)
                    for i, b in enumerate((B2, B3)):
                        g = min(8, n // 8 - 8 * i)
                        t = slice(o + 64 * i, o + 64 * i + 8 * g)
                        ins = dve.tensor_tensor(
                            act[:, :, t].rearrange("p q (g t) -> p q g t", t=8),
                            b[:, 0:64 * g].rearrange("p (g q t) -> p q g t", q=Q8, t=8),
                            act[:, :, t].rearrange("p q (g t) -> p q g t", t=8), ALU.mult)
                    ins.then_inc(peer_x, 1)

                if abc:
                    dve.wait_ge(xt_done, 2 * gi + 2)
                    dve.tensor_copy(xT[:, 1, :], B1[:, 0:GB * XR]).then_inc(xt_copied, 1)
                    ln(0)
                terms(0, 2)
                for i in range(2):
                    if abc:
                        dve.wait_ge(hw_act, 4 * gi + 2 * i + 2)
                        src, dst = ((inT, x1T), (x1T, x2T))[i]
                        link(dve.tensor_tensor(dT[:, :], tT[:, :], src[:, :], ALU.subtract))
                        link(dve.scalar_tensor_tensor(dT[:, :], cT[:, :], 1.0, dT[:, :], ALU.add, ALU.mult))
                        dve.scalar_tensor_tensor(dst[:, :], dT[:, :], 0.5, src[:, :], ALU.mult, ALU.add).then_inc(hw_x, 1)
                        if i == 1:
                            dve.wait_ge(hw_x, 2 * gi + 2)
                            dve.tensor_scalar(uT[:, :], x2T[:, :], col("aw", 2), col("aw", 1), ALU.mult,
                                              ALU.add).then_inc(u_ready, 1)
                    terms(2 + i, 3 + i)
                if abc:
                    attention(0)
                terms(4, 5)
                if abc:
                    dve.wait_ge(gate_act, 2 * gi + 2)
                    dve.scalar_tensor_tensor(dT[:, :], cT[:, :], 1.0, inT[:, :], ALU.add, ALU.mult)
                    link(dve.tensor_scalar(tT[:, :], tT[:, :], 0.5, 0.5, ALU.mult, ALU.add))
                    dve.scalar_tensor_tensor(x1T[:, :], dT[:, :], 0.5, hT[:, :], ALU.mult, ALU.add)
                    link(dve.tensor_tensor(x2T[:, :], tT[:, :], tT[:, :], ALU.mult))
                    dve.tensor_tensor(hT[:, :], x1T[:, :], x2T[:, :], ALU.add).then_inc(h_ready, 1)
                terms(5, 6)
                if abc:
                    ln(1)
                terms(6, 7)
                if abc:
                    front(0)
                    search(0)
                terms(7, 9)
                if abc:
                    front(1)
                    pick(0)
                    search(1)
                terms(9, 12)
                if abc:
                    hot(0)
                    pick(1)
                    own_blocks(0)
                    front(2)
                    search(2)
                terms(12, 14)
                if abc:
                    hot(1)
                    pick(2)
                    own_blocks(1)
                terms(14, 15)
                if abc:
                    hot(2)
                    own_blocks(2)
                terms(15, 16)
                if abc:
                    dve.wait_ge(up_mm, gi + 1)
                    dve.scalar_tensor_tensor(hT[:, :], B0[:, 0:N], 1.0 / WSCALE, hT[:, :], ALU.mult,
                                             ALU.add).then_inc(h_ready, 1)
                    ln(2)
                    dve.wait_ge(ln_b, 4 * gi + 3)
                    dve.tensor_tensor(inT[:, :].rearrange("p (b l) -> p b l", l=L),
                                      B1[:, 0:N].rearrange("p (b l) -> p b l", l=L),
                                      posT[:, :].unsqueeze(1).broadcast_to([128, GB, L]), ALU.add).then_inc(ln_out, 1)
                terms(16, 17)
                if abc:
                    attention(1)
                terms(17, 18)
                if abc:
                    dve.wait_ge(att_mm, 2 * gi + 2)
                    dve.scalar_tensor_tensor(hT[:, :], B1[:, 0:N], col("bv"), hT[:, :], ALU.add,
                                             ALU.add).then_inc(h_ready, 1)
                terms(18, 19)
                if abc:
                    ln(3)
                    dve.wait_ge(lg_mm, gi + 1)
                    for s, (o, n) in enumerate(SUBS):
                        ins = dve.tensor_copy(lg[0:n, s, 0:E], B3[0:n, E * s:E * s + E])
                    link(ins)
                    link(dve.tensor_reduce(gs[:, :], lg[:, :, 0:E], AX, ALU.max))
                    dve.tensor_tensor(ge[:, :, :], lg[:, :, 0:E], spread(gs, 128, NSUB, E),
                                      ALU.subtract).then_inc(lg_shift, 1)
                    dve.wait_ge(lg_exp, 2 * gi + 1)
                    link(dve.tensor_reduce(gs[:, :], ge[:, :, :], AX, ALU.add))
                    link(dve.reciprocal(gr[:, :], gs[:, :]))
                    link(dve.tensor_tensor(lg[:, :, 0:E], ge[:, :, :], spread(gr, 128, NSUB, E), ALU.mult))
                    own_wait()
                    for s, (o, n) in enumerate(SUBS):
                        ins = dve.max(m8[0:n, s, :], lg[0:n, s, :])
                    link(ins)
                    dve.tensor_tensor(ge[:, :, :], lg[:, :, 0:E], m8[:, :, 0:1].broadcast_to([128, NSUB, E]),
                                      ALU.subtract).then_inc(lg_shift, 1)
                    link(dve.tensor_copy(t8[:, :, 0:TOPK], m8[:, :, 0:TOPK]))
                    own_wait()
                    for s, (o, n) in enumerate(SUBS):
                        ins = dve.match_replace(lg2[0:n, s, :], t8[0:n, s, :], lg[0:n, s, :], TAKEN)
                    link(ins)
                    dve.wait_ge(lg_exp, 2 * gi + 2)
                    link(dve.scalar_tensor_tensor(comb[:, :, :], lg2[:, :, 0:E], TAKEN / 10, ge[:, :, :],
                                                  ALU.is_lt, ALU.mult))
                    link(dve.tensor_reduce(gs[:, :], comb[:, :, :], AX, ALU.add))
                    link(dve.reciprocal(gr[:, :], gs[:, :]))
                    dve.tensor_tensor(comb[:, :, :], comb[:, :, :], spread(gr, 128, NSUB, E),
                                      ALU.mult).then_inc(comb_ready, 1)
                    assert links[0] == V_LINKS, f"V_LINKS {links}"

            group(0, True, False)
            with dve.Fori(1, G) as g:
                group(g, True, True)
            group(G, False, True)


_INS = ['x', 'L0_tok_W', 'L0_tok_b', 'L0_attn_tW', 'L0_attn_tb', 'L0_attn_cW', 'L0_attn_cb', 'L0_attn_aW',
        'L0_attn_ab', 'L0_attn_frW', 'L0_attn_frb', 'L0_attn_ffW', 'L0_attn_ffb', 'L0_ffn_Wq', 'L0_ffn_bq',
        'L0_ffn_ln_g', 'L0_ffn_ln_b', 'L0_ffn_keys0', 'L0_ffn_keys1', 'L0_ffn_expert_down',
        'L0_ffn_expert_up', 'L1_attn_Wq', 'L1_attn_bq', 'L1_attn_Wk', 'L1_attn_bk', 'L1_attn_Wv',
        'L1_attn_bv', 'L1_ffn_gate_w', 'L1_ffn_re_w1', 'L1_ffn_re_b1', 'L1_ffn_re_w2', 'L1_ffn_re_b2',
        'L1_ffn_se_w1', 'L1_ffn_se_b1', 'L1_ffn_se_w2', 'L1_ffn_se_b2']


def merge_table():
    def area(a, b):
        return sum(max([c + 1 for r, c in (a, b) if r >= row], default=0) for row in range(K))

    grid = [(r + i, c) for r, m, w in CELLS for i in range(m) for c in range(w)]
    slot = {}
    for cell in sorted(grid, key=lambda x: (x[0] + 1) * (x[1] + 1)):
        if area(cell, cell) > K:
            slot[cell] = 0
            continue
        used = {s for other, s in slot.items() if area(cell, other) <= K}
        slot[cell] = min(set(range(len(grid))) - used)
    assert max(slot.values()) < SLOTS
    table = np.zeros((2 * NC, 2, 4 * SLOTS), np.float32)
    for pair in range(2):
        for head in range(2):
            for i, cell in enumerate(grid):
                table[head * NC + i, pair, (2 * pair + head) * SLOTS + slot[cell]] = 1.0
    return table


def shape_constants():
    pos = np.arange(L, dtype=np.float32)[:, None]
    div = np.exp(np.arange(0, D, 2, dtype=np.float32) * np.float32(-np.log(np.float32(10000.0)) / D))
    ang = (pos * div.astype(np.float32)).astype(np.float32)
    mask = np.tile(np.eye(8, dtype=np.float32), (P16, 1))
    return {"c_ident": np.eye(128, dtype=np.float32),
            "c_posT": np.ascontiguousarray(np.concatenate([np.sin(ang), np.cos(ang)], axis=-1).T.astype(np.float32)),
            "c_blockmask": mask,
            "c_merge": merge_table(),
            "c_halfones": np.repeat(np.eye(4, dtype=np.float32), HALF, axis=0)}


def kernel(**inputs):
    import concourse.bacc as bacc
    from concourse.bass_utils import run_bass_kernel_spmd

    nc = bacc.Bacc("TRN2", target_bir_lowering=False, num_devices=1)
    arrays, aps = {}, {}
    for name, v in [(n, inputs[n]) for n in _INS] + list(shape_constants().items()):
        v = np.ascontiguousarray(v)
        arrays[f"in_{name}_dram"] = v
        aps[name] = nc.dram_tensor(f"in_{name}_dram", v.shape, mybir.dt.from_np(v.dtype), kind="ExternalInput").ap()
    out = nc.dram_tensor("out_0_dram", (NB, L, D), F32, kind="ExternalOutput").ap()
    build(nc, aps, out)
    r = run_bass_kernel_spmd(nc, [arrays], core_ids=[0])
    return r.results[0]["out_0_dram"]
```

```python
from contextlib import ExitStack

import numpy as np

import concourse.bass as bass
from concourse import mybir

F32 = mybir.dt.float32
F16 = mybir.dt.float16
U16 = mybir.dt.uint16
I16 = mybir.dt.int16
ALU = mybir.AluOpType
ACT = mybir.ActivationFunctionType
AX = mybir.AxisListType.X

D = 128
NB, T, C = 32, 750, 32
PL, PS = 16, 8
L = (T - PL) // PS + 1
GB = 4
G = NB // GB
N = GB * L
SUBS = [(0, 128), (128, 128), (256, N - 256)]
NSUB = len(SUBS)
XR = L + 1
H, QD, PK, K = 8, 64, 64, 16
HALF = QD // 2
HP = H // 2
CELLS = [(0, 1, 16), (1, 1, 8), (2, 2, 5), (4, 4, 3), (8, 8, 1)]
SLOTS = 24
NC = sum(n * w for _, n, w in CELLS)
P16, Q8 = 16, 8
E, SH, F, TOPK = 16, 2, 512, 4
FC = F // 128
NE = E + SH
EPS = 1e-5
TAKEN = -1e30

ROWS = [("b1", NE * FC), ("b2", NE), ("tok_b", 1), ("tb", 2), ("cb", 2), ("aw", 3), ("frb", 1),
        ("ffb", 1), ("lng", 1), ("lnb", 1), ("bq", 1), ("bk", 1), ("bv", 1)]
COL, NROWS = {}, 0
for _name, _n in ROWS:
    COL[_name] = NROWS
    NROWS += _n

EORD = list(range(E, NE)) + list(range(E))
WSCALE = 1024.0
V_LINKS, P_LINKS = (11, 57), (2, 8)
A, B = 0, 1

STEPS = (NE + 1) * FC
AT = dict(z0=1, k0=3, q1=5, z1=9, k1=10, s1c=11, c0=13, z2=16, t0=18, u0=26, k2=28, s2c=29, c1=31, t1=36,
          u1=44, c2=49, t2=55, u2=62, up=63, ln0=64, back0=66, qk=67, hw1=69, e1=70, s1=71, e0=73, lnB1=74)


def build(nc, a, out):
    ctx = ExitStack()
    with ctx:
        def sb(name, shape, dt=F32):
            return ctx.enter_context(nc.sbuf_tensor(name, shape, dt))

        def sem(name):
            return ctx.enter_context(nc.semaphore(name))

        bank = [ctx.enter_context(nc.psum_tensor(f"bank{i}", [128, 512], F32)) for i in range(8)]
        B0, B1, B2, B3 = bank[:4]
        UP, DN = bank[4:6], bank[6:8]
        comb_dram = nc.dram_tensor("comb_dram", [G, E, N], F32, kind="Internal").ap()

        ident = sb("ident", [128, 128])
        posT = sb("posT", [128, L])
        blockmask = sb("blockmask", [128, 8])
        halfones = sb("halfones", [128, 4])
        ones = sb("ones", [1, 128])
        nhalf = sb("nhalf", [128, 16])
        rows = sb("rows", [NROWS, 128])
        cols = sb("cols", [128, NROWS])
        hcols = sb("hcols", [128, NROWS])
        ab = sb("ab", [1, 1])
        wtokT = sb("wtokT", [128, 4, 128])
        wqcT = sb("wqcT", [128, 512])
        wqkvT = sb("wqkvT", [128, 3, 128])
        gateT = sb("gateT", [128, E])
        bqc = sb("bqc", [128, 512])
        bqm = sb("bqm", [128, H])
        tw = sb("tw", [128, 2, 128])
        cw = sb("cw", [128, 2, 128])
        ffw = sb("ffw", [128, 2, 128])
        frw = sb("frw", [128, 2, 128])
        keys = sb("keys", [PK, 4, HALF])
        keys2 = sb("keys2", [PK, 4, HALF])
        kn = sb("kn", [PK, 2])
        keysBD = sb("keysBD", [128, 256])
        merge = sb("merge", [2 * NC, 2, 4 * SLOTS])
        merge16 = sb("merge16", [2 * NC, 2, 4 * SLOTS], F16)
        dnT = sb("dnT", [128, Q8, 128])
        upR = sb("upR", [128, Q8, 128])
        w1 = sb("w1", [128, NE, F])
        w2 = sb("w2", [128, NE, FC, 128])

        xin = sb("xin", [XR, GB, 2, 128])
        hT = sb("hT", [128, N])
        shared = sb("shared", [128, 2 * GB * XR + 11 * N + GB * 128])
        xT = shared[:, 0:2 * GB * XR].rearrange("p (s r) -> p s r", s=2)
        at = 2 * GB * XR
        vtokB = shared[0:L, at:at + GB * 128].rearrange("p (b d) -> p b d", b=GB)
        at += GB * 128
        tT, cT, dT, x1T, x2T, uT, attT, qT, kT, probs, probsT = (shared[:, at + i * N:at + (i + 1) * N] for i in range(11))
        prob, probT = (dT[0:L, :], probs[0:L, :]), (x1T[0:L, :], probsT[0:L, :])
        bn = [sb(f"bn{i}", [128, NSUB, 6]) for i in range(2)]
        mv = [sb(f"mv{i}", [128, NSUB, 2]) for i in range(2)]
        rstd = [sb(f"rstd{i}", [128, NSUB]) for i in range(2)]
        inT = sb("inT", [128, N])
        hAT = sb("hAT", [128, N])
        s1row = sb("s1row", [1, N])
        amax = [sb(f"amax{i}", [L, GB]) for i in range(2)]
        asum = [sb(f"asum{i}", [L, GB]) for i in range(2)]
        arec = [sb(f"arec{i}", [L, GB]) for i in range(2)]
        hnT = sb("hnT", [128, N])
        act = sb("act", [128, Q8, N])
        act_raw = act[:, 0:5, :].rearrange("p q n -> p (q n)")[:, 0:12 * 128].rearrange("p (j n) -> p j n", n=128)
        dnraw = act[:, 5:8, :].rearrange("p q n -> p (q n)")[:, 0:Q8 * 128].rearrange("p (j n) -> p j n", n=128)
        qc = sb("qc", [128, 512])
        sq = sb("sq", [128, 512])
        qv = sb("qv", [128, H])
        qr = sb("qr", [128, H])
        qnT = sb("qnT", [128, HP, 128])
        sqT = sb("sqT", [128, HP, 128])
        sc = sb("sc", [128, 2 * H, PK])
        nrm = sb("nrm", [128, 2 * H])
        inv = sb("inv", [128, 2, 2 * H])
        top = sb("top", [128, 2 * H, K])
        topn = sb("topn", [128, 2 * H, K])
        idx = sb("idx", [128, 2 * H, K], U16)
        idf = sb("idf", [128, 2 * H, K])
        cand = sb("cand", [128, H, NC])
        cand2 = sb("cand2", [128, H, NC])
        best = sb("best", [128, H, K])
        cexp = sb("cexp", [128, H, NC])
        cexpert = sb("cexpert", [128, 2, H, NC])
        cw_ = sb("cw_", [128, H, NC])
        z = sb("z", [128, H])
        zr = sb("zr", [128, H])
        NK = 2 * NC
        NS = 4 * SLOTS
        epick = sb("epick", [128, H, NC])
        xn = [t[:, 0:NSUB * 128].rearrange("p (s d) -> p s d", s=NSUB) for t in (sq, qc)]
        inA = sqT[:, :, :].rearrange("p c n -> p (c n)")[:, 0:N]
        vtok = (sc[0:L, 0:GB * 128 // PK, :].rearrange("p c k -> p (c k)").rearrange("p (b d) -> p b d", b=GB), vtokB)
        wcell = sq[0:NK, :]
        ecell = sb("ecell", [NK, 512], F16)
        pi = sb("pi", [NS, 256], I16)
        qi = sb("qi", [NS, 256], F16)
        whi = sb("whi", [NS, 256], F16)
        wlo = sb("wlo", [NS, 256], F16)
        hot16 = shared[0:NS, 0:5120].bitcast(F16)
        ph = hot16[:, 0:P16 * 256].rearrange("p (g k t) -> p g k t", k=P16, t=8)
        qh = hot16[:, P16 * 256:(P16 + Q8) * 256].rearrange("p (k n) -> p k n", k=Q8)
        qw = hot16[:, (P16 + Q8) * 256:(P16 + 3 * Q8) * 256].rearrange("p (h k n) -> p h k n", h=2, k=Q8)
        lg = sb("lg", [128, NSUB, E + 4])
        lg2 = sb("lg2", [128, NSUB, E + 4])
        ge = sb("ge", [128, NSUB, E])
        gs_ = sb("gs_", [128, NSUB])
        gr = sb("gr", [128, NSUB])
        m8 = sb("m8", [128, NSUB, 8])
        t8 = sb("t8", [128, NSUB, 8])
        comb = sb("comb", [128, NSUB, E])
        combT = sb("combT", [E, N])
        combB = sb("combB", [128, 2, 4, N])
        xd = sb("xd", [128, N])
        hid = sb("hid", [128, 2, FC, N])
        term = sb("term", [128, 2, N])
        acc = sb("acc", [128, N])
        otile = sb("otile", [128, NSUB, 128])

        x_in, const_in, wts_in, exp_in, peer_in = (sem("x_in"), sem("const_in"), sem("wts_in"), sem("exp_in"),
                                                   sem("peer_in"))
        setup_v, setup_p, setup_pe, setup_a, v_set = (sem("setup_v"), sem("setup_p"), sem("setup_pe"),
                                                      sem("setup_a"), sem("v_set"))
        comb_out, out_done = sem("comb_out"), sem("out_done")
        comb_in = [sem("comb_in_even"), sem("comb_in_odd")]
        def sems(name):
            return sem(name + "_A"), sem(name + "_B")

        v_link, p_link = sems("v_link"), sems("p_link")
        v_met, p_met = sem("v_met"), sem("p_met")
        xt_done, xt_copied, tok_mm = sem("xt_done"), sem("xt_copied"), sem("tok_mm")
        h_ready = sems("h_ready")
        ln_t, ln_mv, ln_rstd, ln_xn, ln_b, ln_out = (sems("ln_t"), sems("ln_mv"), sems("ln_rstd"), sems("ln_xn"),
                                                     sems("ln_b"), sems("ln_out"))
        hw_mm, hw_act, hw_x, u_ready = sem("hw_mm"), sem("hw_act"), sem("hw_x"), sem("u_ready")
        s1_mm, s1_row, gate_mm, gate_act = sem("s1_mm"), sem("s1_row"), sem("gate_mm"), sem("gate_act")
        qk_mm, qk_out, v_mm, v_out = sem("qk_mm"), sem("qk_out"), sems("v_mm"), sems("v_out")
        sc_mm, sc_shift, sc_exp, sc_rec, prob_ready = (sems("sc_mm"), sems("sc_shift"), sems("sc_exp"),
                                                       sems("sc_rec"), sems("prob_ready"))
        pt_mm, pt_out, att_mm, att_out = sems("pt_mm"), sems("pt_out"), sems("att_mm"), sem("att_out")
        in_mm, in_act, act_masked = sem("in_mm"), sem("in_act"), sem("act_masked")
        q_mm, q_biased, q_sq, q_var, q_rstd, q_z = (sem("q_mm"), sem("q_biased"), sem("q_sq"), sem("q_var"),
                                                    sem("q_rstd"), sem("q_z"))
        z_t, q_out, ks_mm, ks_out, n_inv = sem("z_t"), sem("q_out"), sem("ks_mm"), sem("ks_out"), sem("n_inv")
        top_done, cand_done, cand_exp, w_raw, w_norm = (sem("top_done"), sem("cand_done"), sem("cand_exp"),
                                                        sem("w_raw"), sem("w_norm"))
        cell_t, cell_out, slots_mm, pq_ready, e_picked, q_hot, pq_mm, peer_x, up_mm = (
            sem("cell_t"), sem("cell_out"), sem("slots_mm"), sem("pq_ready"), sem("e_picked"), sem("q_hot"), sem("pq_mm"), sem("peer_x"), sem("up_mm"))
        lg_mm, lg_shift, lg_exp, comb_ready, comb_t, comb_copied = (
            sem("lg_mm"), sem("lg_shift"), sem("lg_exp"), sem("comb_ready"), sem("comb_t"), sem("comb_copied"))
        ff_up, ff_gelu, ff_dn, ff_term, ff_acc = (sem("ff_up"), sem("ff_gelu"), sem("ff_dn"), sem("ff_term"),
                                                  sem("ff_acc"))
        out_t, out_copied = sem("out_t"), sem("out_copied")

        out_v = out.rearrange("(g b) l d -> g (b l) d", b=GB)
        x_v = a["x"].rearrange("(g b) t c -> g b (t c)", b=GB)

        def col(name, i=0):
            return cols[:, COL[name] + i:COL[name] + i + 1]

        def hcol(name, i=0):
            return hcols[:, COL[name] + i:COL[name] + i + 1]

        def of_group(v, gi):
            if isinstance(gi, int):
                return v[gi]
            return v[bass.ds(gi, 1)].rearrange("o a b -> (o a) b")

        def heads(t, n):
            return t[0:n, :].rearrange("p (h k) -> p h k", h=H)

        def spread(t, n, h, k):
            return t[0:n, 0:h].unsqueeze(2).broadcast_to([n, h, k])

        LN_IN, LN_BACK = ((B1, B0), (B3, B3)), ((B0, B1), (B2, B2))

        block = ctx.enter_context(nc.Block())
        N_CONST, N_WTS = [0], [0]

        @block.sync
        def _(sp):
            def load_x(gi):
                src = of_group(x_v, gi)
                sp.dma_start(xin[:, :, :, :].rearrange("p b s k -> p b (s k)"),
                             src[:, 0:XR * 256].rearrange("b (p k) -> p b k", k=256)).then_inc(x_in, 16)

            def const(dst, src):
                N_CONST[0] += 16
                sp.dma_start(dst, src).then_inc(const_in, 16)

            def wts(dst, src):
                N_WTS[0] += 16
                sp.dma_start(dst, src).then_inc(wts_in, 16)

            sp.sem_inc(out_done, 16)
            load_x(0)
            const(ident[:, :], a["c_ident"])
            for name, src in (("tok_b", "L0_tok_b"), ("tb", "L0_attn_tb"), ("cb", "L0_attn_cb"),
                              ("aw", "L0_attn_aW"), ("frb", "L0_attn_frb"), ("ffb", "L0_attn_ffb"),
                              ("bq", "L1_attn_bq"), ("bk", "L1_attn_bk"), ("bv", "L1_attn_bv")):
                v = a[src]
                v = v.rearrange("(o d) -> o d", d=128) if len(v.shape) == 1 else v
                const(rows[COL[name]:COL[name] + v.shape[0], :], v)
            for name, src in (("lng", "L0_ffn_ln_g"), ("lnb", "L0_ffn_ln_b")):
                for i in range(2):
                    const(rows[COL[name]:COL[name] + 1, 64 * i:64 * i + 64],
                          a[src].rearrange("(o d) -> o d", o=1))
            const(rows[0:E * FC, :], a["L1_ffn_re_b1"].rearrange("e (c f) -> (e c) f", f=128))
            const(rows[E * FC:NE * FC, :], a["L1_ffn_se_b1"].rearrange("e (c f) -> (e c) f", f=128))
            const(rows[COL["b2"]:COL["b2"] + E, :], a["L1_ffn_re_b2"])
            const(rows[COL["b2"] + E:COL["b2"] + NE, :], a["L1_ffn_se_b2"])
            const(ab[:, :], a["L0_attn_ab"].rearrange("(o d) -> o d", o=1))
            const(act_raw[:, 0:4, :], a["L0_tok_W"].rearrange("d (j k) -> d j k", k=128))
            const(act_raw[:, 4:8, :], a["L0_ffn_Wq"].rearrange("(j r) d -> r j d", r=128))
            wts(tw[:, :, :], a["L0_attn_tW"].rearrange("i d n -> d i n"))
            wts(cw[:, :, :], a["L0_attn_cW"].rearrange("i d n -> d i n"))
            wts(ffw[:, :, :], a["L0_attn_ffW"].rearrange("(i d) n -> d i n", d=128))
            wts(frw[:, :, :], a["L0_attn_frW"].rearrange("(i d) n -> d i n", d=128))
            for i in range(4):
                wts(keys[:, i, :], a[f"L0_ffn_keys{i % 2}"])
            wts(bqc[:, :], a["L0_ffn_bq"].rearrange("(o n) -> o n", o=1).broadcast_to([128, 512]))
            wts(posT[:, :], a["c_posT"])
            wts(blockmask[:, :], a["c_blockmask"])
            wts(halfones[:, :], a["c_halfones"])
            wts(merge[:, :, :], a["c_merge"])
            for i, name in enumerate(("L1_attn_Wq", "L1_attn_Wk", "L1_attn_Wv")):
                wts(act_raw[:, 8 + i, :], a[name])
            wts(act_raw[0:E, 11, :], a["L1_ffn_gate_w"])
            for dst, name in ((dnraw, "L0_ffn_expert_down"), (upR, "L0_ffn_expert_up")):
                v = a[name][0:128, :].rearrange("(p q) d -> p (q d)", q=Q8)
                for p in range(P16):
                    sp.dma_start(dst[8 * p:8 * p + 8, :, :].rearrange("t q d -> t (q d)"),
                                 v[p:p + 1, :].broadcast_to([8, Q8 * 128])).then_inc(peer_in, 16)
            for e0, e1 in ((0, 4), (4, 8), (8, 12), (12, 16)):
                sp.dma_start(w1[:, e0:e1, :], a["L1_ffn_re_w1"][e0:e1].rearrange("e d f -> d e f")).then_inc(exp_in, 16)
                sp.dma_start(w2[:, e0:e1, :, :].rearrange("p e c d -> p (e c) d"),
                             a["L1_ffn_re_w2"][e0:e1].rearrange("e (c p) d -> p (e c) d", p=128)).then_inc(exp_in, 16)
            sp.dma_start(w1[:, E:NE, :], a["L1_ffn_se_w1"].rearrange("e d f -> d e f")).then_inc(exp_in, 16)
            sp.dma_start(w2[:, E:NE, :, :].rearrange("p e c d -> p (e c) d"),
                         a["L1_ffn_se_w2"].rearrange("e (c p) d -> p (e c) d", p=128)).then_inc(exp_in, 16)

            def next_x(gi):
                sp.wait_ge(xt_done, 2 * gi)
                load_x(gi)

            def store(m):
                sp.wait_ge(out_copied, m + 2)
                dst = of_group(out_v, m)
                for s, (o, n) in enumerate(SUBS):
                    sp.dma_start(dst[o:o + n, :], otile[0:n, s, :]).then_inc(out_done, 16)

            def gates(m):
                sp.wait_ge(comb_copied, m + 1)
                mem = of_group(comb_dram, m)
                sp.dma_start(mem, combT[:, :]).then_inc(comb_out, 16)
                sp.wait_ge(comb_out, 16 * m + 16)
                for r in range(E // 4):
                    sp.wait_ge(ff_term, NE * m + 2 + (SH + 4 * (r - 1) if r > 1 else 0))
                    sp.dma_start(combB[:, r % 2, :, :].rearrange("p e n -> p (e n)"),
                                 mem[4 * r:4 * r + 4, :].rearrange("(o e) n -> o (e n)", o=1).broadcast_to([128, 4 * N])
                                 ).then_inc(comb_in[r % 2], 16)

            next_x(1)
            next_x(2)
            gates(0)
            with sp.Fori(1, G - 2) as g:
                next_x(g + 2)
                store(g - 1)
                gates(g)
            store(G - 3)
            gates(G - 2)
            store(G - 2)
            gates(G - 1)
            store(G - 1)
            sp.wait_ge(out_done, 16 * NSUB * G + 16)

        @block.tensor
        def _(pe):
            def mm(o, lhsT, rhs, start=True, stop=True):
                return pe.matmul(o, lhsT, rhs, start=start, stop=stop)

            def tr(o, src):
                n = src.shape[0]
                return pe.transpose(o, src, ident[0:n, 0:n])

            pe.wait_ge(const_in, N_CONST[0])
            tr(B0[:, 0:NROWS], rows[:, :]).then_inc(setup_pe, 1)
            for j in range(4):
                ins = tr(B1[:, 128 * j:128 * j + 128], act_raw[:, j, :])
            ins.then_inc(setup_pe, 1)
            for j in range(4):
                ins = tr(B2[:, 128 * j:128 * j + 128], act_raw[:, 4 + j, :])
            ins.then_inc(setup_pe, 1)
            pe.wait_ge(wts_in, N_WTS[0])
            for j in range(3):
                tr(B3[:, 128 * j:128 * j + 128], act_raw[:, 8 + j, :])
            tr(B3[:, 384:384 + E], act_raw[0:E, 11, :]).then_inc(setup_pe, 1)
            pe.wait_ge(setup_p, 3)
            tr(UP[0][:, 0:PK], keys2[:, :, :].rearrange("p c k -> p (c k)")).then_inc(setup_pe, 1)
            pe.wait_ge(setup_a, 3)
            pe.wait_ge(setup_v, 2)

            def setup_experts():
                pe.wait_ge(peer_in, 16 * 2 * P16)
                for q in range(Q8):
                    ins = tr(DN[q // 4][:, 128 * (q % 4):128 * (q % 4) + 128], dnraw[:, q, :])
                ins.then_inc(setup_pe, 1)
                pe.wait_ge(setup_a, 4)
                pe.wait_ge(setup_v, 3)

            def group(gi, peer, nxt, moe):
                m, gj = gi - 1, gi + 1
                done = [0]

                def moe_to(upto):
                    if not moe:
                        return
                    if done[0] == 0:
                        pe.wait_ge(exp_in, 160)
                    for step in range(done[0], upto):
                        e, f = step // FC, step % FC
                        if e < NE:
                            pe.wait_ge(ff_gelu, NE * FC * m + step + 1)
                            mm(UP[f % 2][:, 0:N], w1[:, EORD[e], 128 * f:128 * f + 128], xd[:, :]).then_inc(ff_up, 1)
                        if e > 0:
                            x = NE * m + e
                            if f == 0:
                                pe.wait_ge(ff_term, x)
                                if e == 1:
                                    pe.wait_ge(out_copied, m + 1)
                            pe.wait_ge(ff_gelu, (x - 1) * FC + f + 3)
                            ins = mm(DN[(e - 1) % 2][:, 0:N], w2[:, EORD[e - 1], f, :], hid[:, (e - 1) % 2, f, :],
                                     start=(f == 0), stop=(f == FC - 1))
                            if f == FC - 1:
                                ins.then_inc(ff_dn, 1)
                    done[0] = upto

                def gs(st):
                    return (gj, gi)[st]

                def ln_in(st, i):
                    pe.wait_ge(h_ready[st], 2 * gs(st) + i + 1)
                    h = (hAT, hT)[st]
                    for s, (o, n) in enumerate(SUBS):
                        ins = tr(LN_IN[st][i][0:n, 128 * s:128 * s + 128], h[:, o:o + n])
                    ins.then_inc(ln_t[st], 1)

                def ln_back(st, i):
                    pe.wait_ge(ln_xn[st], 2 * gs(st) + i + 1)
                    for s, (o, n) in enumerate(SUBS):
                        ins = tr(LN_BACK[st][i][:, o:o + n], xn[st][0:n, s, :])
                    ins.then_inc(ln_b[st], 1)

                def turn_probs(st):
                    pe.wait_ge(v_out[st], gs(st) + 1)
                    pe.wait_ge(prob_ready[st], gs(st) + 1)
                    for b in range(GB):
                        ins = tr((B0, B3)[st][0:L, L * b:L * b + L], prob[st][:, L * b:L * b + L])
                    ins.then_inc(pt_mm[st], 1)

                def probs_times_values(st):
                    pe.wait_ge(pt_out[st], gs(st) + 1)
                    for b in range(GB):
                        ins = mm((B1, B2)[st][:, L * b:L * b + L], vtok[st][:, b, :], probT[st][:, L * b:L * b + L])
                    ins.then_inc(att_mm[st], 1)

                def queries(s):
                    o, n = SUBS[s]
                    k = 3 * gi + s + 1
                    if s > 0:
                        pe.wait_ge(ks_out, 2 * (k - 1) - 1)
                    mm(B0[0:n, :], hnT[:, o:o + n], wqcT[:, :]).then_inc(q_mm, 1)

                def turn_queries(s):
                    n = SUBS[s][1]
                    pe.wait_ge(q_z, 3 * gi + s + 1)
                    for c in range(HP):
                        ins = tr(B1[:, 128 * c:128 * c + n], qc[0:n, 128 * c:128 * c + 128])
                    ins.then_inc(z_t, 1)

                def key_scores(s):
                    n = SUBS[s][1]
                    k = 3 * gi + s + 1
                    pe.wait_ge(q_out, k)
                    if s == 0:
                        pe.wait_ge(in_act, Q8 * gi + Q8)
                    elif s == 1:
                        pe.wait_ge(ks_out, 2 * (k - 1))
                    else:
                        pe.wait_ge(peer_x, 3 * gi + 1)
                    for c in range(HP):
                        mm(B0[0:n, 4 * c:4 * c + 4], sqT[:, c, 0:n], halfones[:, :])
                        ins = mm((B2, B3)[c // 2][0:n, 256 * (c % 2):256 * (c % 2) + 256], qnT[:, c, 0:n], keysBD[:, :])
                    ins.then_inc(ks_mm, 1)

                def turn_cells(s):
                    n = SUBS[s][1]
                    k = 3 * gi + s + 1
                    pe.wait_ge(w_norm, k)
                    pe.wait_ge(e_picked, k)
                    if s == 0:
                        pe.wait_ge(q_biased, k + 2)
                        pe.wait_ge(q_out, k + 2)
                    elif s == 1:
                        pe.wait_ge(ks_out, 2 * (k + 1))
                    for c in range(HP):
                        tr(B0[0:NK, n * c:n * c + n], cw_[0:n, 2 * c:2 * c + 2, :].rearrange("p h k -> p (h k)"))
                        ins = tr(B1[0:NK, n * c:n * c + n],
                                 epick[0:n, 2 * c:2 * c + 2, :].rearrange("p h k -> p (h k)"))
                    ins.then_inc(cell_t, 1)

                def slots(s):
                    n = SUBS[s][1]
                    pe.wait_ge(cell_out, 3 * gi + s + 1)
                    for i in range(2):
                        for c in range(2):
                            mm(B0[0:NS, i * n:i * n + n], merge[:, c, :], wcell[:, (2 * i + c) * n:(2 * i + c + 1) * n],
                               start=(c == 0), stop=(c == 1))
                        for c in range(2):
                            ins = mm(B0[0:NS, (2 + i) * n:(3 + i) * n], merge16[:, c, :],
                                     ecell[:, (2 * i + c) * n:(2 * i + c + 1) * n], start=(c == 0), stop=(c == 1))
                    ins.then_inc(slots_mm, 1)

                def sums(s):
                    n = SUBS[s][1]
                    k = 3 * gi + s + 1
                    pe.wait_ge(q_hot, k)
                    if s < 2:
                        pe.wait_ge(ks_out, 2 * (k + 1))
                    else:
                        pe.wait_ge(peer_x, k - 1)
                    for t in range(n // 8):
                        for c in range(2):
                            x = n * c + 8 * t
                            for part in range(2):
                                ins = mm((B2, B3)[t // 8][:, 64 * (t % 8):64 * (t % 8) + 64],
                                         ph[:, x // 8, :, :].rearrange("p k t -> p (k t)"),
                                         qw[:, part, :, x:x + 8], start=(c == 0 and part == 0),
                                         stop=(c == 1 and part == 1))
                    ins.then_inc(pq_mm, 1)

                def expert_inputs(q0, q1):
                    for q in range(q0, q1):
                        if q >= 2:
                            pe.wait_ge(in_act, Q8 * gi + q - 1)
                        mm((B2, B3)[q % 2][:, 0:N], dnT[:, q, :], hnT[:, :]).then_inc(in_mm, 1)

                if peer:
                    pe.wait_ge(ln_out[A], 2 * gi + 2)
                    queries(0)
                    if moe:
                        pe.wait_ge(comb_copied, gi)
                    expert_inputs(0, 4)
                    moe_to(AT["z0"])
                    turn_queries(0)
                    expert_inputs(4, 8)
                    moe_to(AT["k0"])
                    key_scores(0)
                    queries(1)
                    moe_to(AT["z1"])
                    turn_queries(1)
                    moe_to(AT["k1"])
                    key_scores(1)
                    queries(2)
                    moe_to(AT["z2"])
                    turn_queries(2)
                    moe_to(AT["t0"])
                    turn_cells(0)
                    moe_to(AT["t0"] + 1)
                    slots(0)
                    moe_to(AT["u0"])
                    sums(0)
                    moe_to(AT["k2"])
                    key_scores(2)
                    moe_to(AT["t1"])
                    turn_cells(1)
                    moe_to(AT["t1"] + 1)
                    slots(1)
                    moe_to(AT["u1"])
                    sums(1)
                    moe_to(AT["t2"])
                    turn_cells(2)
                    moe_to(AT["t2"] + 1)
                    slots(2)
                    moe_to(AT["u2"])
                    sums(2)
                if nxt:
                    pe.wait_ge(x_in, 16 * gj + 16)
                    for s in range(2):
                        for b in range(GB):
                            ins = tr((B0, B1)[s][:, XR * b:XR * b + XR], xin[:, b, s, :])
                        ins.then_inc(xt_done, 1)
                moe_to(AT["up"])
                if peer:
                    pe.wait_ge(peer_x, 3 * gi + 3)
                    for q in range(Q8):
                        ins = mm(B2[:, 0:N], upR[:, q, :], act[:, q, :], start=(q == 0), stop=(q == Q8 - 1))
                    ins.then_inc(up_mm, 1)
                if nxt:
                    pe.wait_ge(xt_copied, 2 * gj + 2)
                    for j in range(4):
                        v = xT[:, j % 2, :].rearrange("p (b r) -> p b r", r=XR)[:, :, j // 2:j // 2 + L]
                        ins = mm(B0[:, 0:N], wtokT[:, j, :], v, start=(j == 0), stop=(j == 3))
                    ins.then_inc(tok_mm, 1)
                if peer:
                    ln_in(B, 0)
                moe_to(AT["ln0"])
                if nxt:
                    ln_in(A, 0)
                moe_to(AT["back0"])
                if peer:
                    ln_back(B, 0)
                if nxt:
                    ln_back(A, 0)
                moe_to(AT["qk"])
                if peer:
                    pe.wait_ge(ln_out[B], 2 * gi + 1)
                    mm(B3[:, 0:N], wqkvT[:, 0, :], inT[:, :]).then_inc(qk_mm, 1)
                    mm(B2[:, 0:N], wqkvT[:, 1, :], inT[:, :]).then_inc(qk_mm, 1)
                if nxt:
                    pe.wait_ge(ln_out[A], 2 * gj + 1)
                    mm(B1[:, 0:N], tw[:, 0, :], inA[:, :]).then_inc(hw_mm, 1)
                    mm(B0[:, 0:N], cw[:, 0, :], inA[:, :]).then_inc(hw_mm, 1)
                if peer:
                    pe.wait_ge(qk_out, 2 * gi + 1)
                    for b in range(GB):
                        ins = mm(B3[0:L, 128 * b:128 * b + 128], inT[:, L * b:L * b + L], wqkvT[:, 2, :])
                    ins.then_inc(v_mm[B], 1)
                    pe.wait_ge(qk_out, 2 * gi + 2)
                    for b in range(GB):
                        t = slice(L * b, L * b + L)
                        ins = mm(B2[0:L, t], qT[:, t], kT[:, t])
                    ins.then_inc(sc_mm[B], 1)
                moe_to(AT["hw1"])
                if nxt:
                    pe.wait_ge(hw_x, 2 * gj + 1)
                    mm(B1[:, 0:N], tw[:, 1, :], x1T[:, :]).then_inc(hw_mm, 1)
                    mm(B0[:, 0:N], cw[:, 1, :], x1T[:, :]).then_inc(hw_mm, 1)
                moe_to(AT["s1"])
                if nxt:
                    pe.wait_ge(hw_x, 2 * gj + 2)
                    mm(B1[0:1, 0:N], col("aw", 0), x2T[:, :]).then_inc(s1_mm, 1)
                    for b in range(GB):
                        ins = tr(B0[0:L, 128 * b:128 * b + 128], x2T[:, L * b:L * b + L])
                    ins.then_inc(v_mm[A], 1)
                if peer:
                    turn_probs(B)
                if nxt:
                    pe.wait_ge(u_ready, gj + 1)
                    pe.wait_ge(s1_row, gj + 1)
                    for b in range(GB):
                        t = slice(L * b, L * b + L)
                        mm(B1[0:L, t], uT[:, t], x2T[:, t], stop=False)
                        ins = mm(B1[0:L, t], s1row[0:1, t], ones[0:1, 0:L], start=False)
                    ins.then_inc(sc_mm[A], 1)
                if peer:
                    probs_times_values(B)
                moe_to(AT["lnB1"])
                if peer:
                    ln_in(B, 1)
                moe_to(STEPS)
                if nxt:
                    turn_probs(A)
                if moe:
                    pe.wait_ge(ff_acc, (NE + 1) * gi)
                    for s, (o, n) in enumerate(SUBS):
                        ins = tr(DN[0][0:n, 128 * s:128 * s + 128], acc[:, o:o + n])
                    ins.then_inc(out_t, 1)
                if peer:
                    ln_back(B, 1)
                if nxt:
                    probs_times_values(A)
                if peer:
                    pe.wait_ge(ln_out[B], 2 * gi + 2)
                    for s, (o, n) in enumerate(SUBS):
                        ins = mm(B3[0:n, E * s:E * s + E], xd[:, o:o + n], gateT[:, :])
                    ins.then_inc(lg_mm, 1)
                if nxt:
                    pe.wait_ge(att_out, gj + 1)
                    for w, b in ((ffw, B0), (frw, B1)):
                        mm(b[:, 0:N], w[:, 0, :], inA[:, :], stop=False)
                        mm(b[:, 0:N], w[:, 1, :], attT[:, :], start=False).then_inc(gate_mm, 1)
                    ln_in(A, 1)
                if peer:
                    pe.wait_ge(comb_ready, gi + 1)
                    for s, (o, n) in enumerate(SUBS):
                        ins = tr(B2[0:E, o:o + n], comb[0:n, s, :])
                    ins.then_inc(comb_t, 1)
                if nxt:
                    ln_back(A, 1)

            group(-1, False, True, False)
            setup_experts()
            group(0, True, True, False)
            with pe.Fori(1, G - 1) as g:
                group(g, True, True, True)
            group(G - 1, True, False, True)
            group(G, False, False, True)

        @block.gpsimd
        def _(pool):
            pool.memset(ones[:, :], 1.0)
            pool.memset(nhalf[:, :], -0.5)
            pool.memset(keysBD[:, :], 0.0)
            for i in range(2):
                pool.memset(mv[i][:, :, :], 1.0)
            pool.memset(lg[:, :, :], -1.0)
            pool.memset(m8[:, :, :], -1.0)
            pool.memset(lg2[:, :, :], TAKEN)
            pool.memset(ge[:, :, :], 0.0)
            pool.memset(t8[:, :, :], -1.0).then_inc(setup_p, 1)
            pool.wait_ge(setup_p, 1)
            pool.wait_ge(setup_v, 1)
            pool.tensor_tensor(kn[:, :], kn[:, :], nhalf[0:PK, 0:2], ALU.pow).then_inc(setup_p, 1)
            pool.wait_ge(setup_p, 2)
            for i in range(2):
                ins = pool.tensor_tensor(keys2[:, 2 * i:2 * i + 2, :], keys[:, 2 * i:2 * i + 2, :],
                                         spread(kn, PK, 2, HALF), ALU.mult)
            ins.then_inc(setup_p, 1)

            def group(gi, peer, nxt, moe):
                m, gj = gi - 1, gi + 1
                links, added = [0, 0], [0]

                def gs(st):
                    return (gj, gi)[st]

                def link(st, ins):
                    links[st] += 1
                    ins.then_inc(p_link[st], 1)
                    pool.wait_ge(p_link[st], gs(st) * P_LINKS[st] + links[st])

                def own_wait():
                    pool.sem_inc(p_met, 1)

                def moe_to(upto):
                    if not moe:
                        return
                    for e in range(added[0], upto // FC - 1):
                        pool.wait_ge(ff_term, NE * m + e + 3)
                        pool.wait_ge(ff_acc, (NE + 1) * m + e + 1)
                        pool.tensor_tensor(acc[:, :], acc[:, :], term[:, e % 2, :], ALU.add).then_inc(ff_acc, 1)
                        added[0] = e + 1

                def ln(st, i):
                    pool.wait_ge(ln_mv[st], 2 * gs(st) + i + 1)
                    own_wait()
                    link(st, pool.tensor_scalar(rstd[st][:, :], mv[st][:, :, 1], EPS, None, ALU.add))
                    pool.tensor_tensor(rstd[st][:, :], rstd[st][:, :], nhalf[:, 0:NSUB], ALU.pow).then_inc(ln_rstd[st], 1)

                def attention(st):
                    pool.wait_ge(sc_rec[st], gs(st) + 1)
                    v = prob[st][:, :].rearrange("p (b j) -> p b j", j=L)
                    pool.tensor_tensor(v, v, spread(arec[st], L, GB, L), ALU.mult).then_inc(prob_ready[st], 1)

                def mask_inputs(q0, q1):
                    pool.wait_ge(in_act, Q8 * gi + q1)
                    v = act[:, q0:q1, :].rearrange("p q (g t) -> p (q g) t", t=8)
                    pool.tensor_tensor(v, v, blockmask[:, :].unsqueeze(1).broadcast_to([128, (q1 - q0) * N // 8, 8]),
                                       ALU.mult).then_inc(act_masked, 1)

                def query_norm(s):
                    n = SUBS[s][1]
                    pool.wait_ge(q_var, 3 * gi + s + 1)
                    own_wait()
                    link(B, pool.tensor_scalar(qr[0:n, :], qv[0:n, :], 1.0 / QD, EPS, ALU.mult, ALU.add))
                    pool.tensor_tensor(qr[0:n, :], qr[0:n, :], nhalf[0:n, 0:H], ALU.pow).then_inc(q_rstd, 1)

                def half_norms(s):
                    n = SUBS[s][1]
                    pool.wait_ge(ks_out, 2 * (3 * gi + s + 1) - 1)
                    own_wait()
                    link(B, pool.tensor_scalar(inv[0:n, s % 2, :], nrm[0:n, :], 1e-24, None, ALU.max))
                    pool.tensor_tensor(inv[0:n, s % 2, :], inv[0:n, s % 2, :], nhalf[0:n, :], ALU.pow).then_inc(n_inv, 1)

                def cells(s):
                    n = SUBS[s][1]
                    pool.wait_ge(top_done, 3 * gi + s + 1)
                    for src, dst in ((topn, cand[0:n]), (idf, cexpert[0:n, s % 2])):
                        v = src[0:n, :, :].rearrange("p (h t) k -> p h t k", t=2)
                        o = 0
                        for r, k, w in CELLS:
                            d = dst[:, :, o:o + k * w].rearrange("p h (m w) -> p h m w", w=w)
                            ins = pool.tensor_tensor(
                                d, v[:, :, 0, r:r + k].unsqueeze(3).broadcast_to([n, H, k, w]),
                                v[:, :, 1, 0:w].unsqueeze(2).broadcast_to([n, H, k, w]), ALU.add)
                            o += k * w
                        ins.then_inc(cand_done, 1)

                def weights(s):
                    n = SUBS[s][1]
                    pool.wait_ge(w_raw, 3 * gi + s + 1)
                    pool.tensor_tensor(cw_[0:n, :, :], cw_[0:n, :, :], spread(zr, n, H, NC), ALU.mult).then_inc(w_norm, 1)

                if peer:
                    query_norm(0)
                    mask_inputs(0, 4)
                    half_norms(0)
                    query_norm(1)
                    moe_to(AT["z1"])
                    mask_inputs(4, 8)
                    half_norms(1)
                    moe_to(AT["c0"])
                    cells(0)
                    query_norm(2)
                    moe_to(AT["t0"])
                    weights(0)
                    moe_to(AT["k2"])
                    half_norms(2)
                    cells(1)
                    moe_to(AT["t1"])
                    weights(1)
                    moe_to(AT["c2"])
                    cells(2)
                    moe_to(AT["t2"])
                    weights(2)
                moe_to(AT["up"])
                if peer:
                    ln(B, 0)
                if nxt:
                    ln(A, 0)
                moe_to(AT["s1"])
                if peer:
                    attention(B)
                if nxt:
                    attention(A)
                moe_to(AT["lnB1"])
                if peer:
                    ln(B, 1)
                moe_to(STEPS)
                if peer:
                    pool.wait_ge(h_ready[B], 2 * gi + 2)
                    if moe:
                        pool.wait_ge(out_t, gi)
                    own_wait()
                    pool.tensor_copy(acc[:, :], hT[:, :]).then_inc(ff_acc, 1)
                if nxt:
                    ln(A, 1)
                assert links == [nxt * P_LINKS[A], peer * P_LINKS[B]], f"P_LINKS {links}"

            group(-1, False, True, False)
            group(0, True, True, False)
            with pool.Fori(1, G - 1) as g:
                group(g, True, True, True)
            group(G - 1, True, False, True)
            group(G, False, False, True)

        @block.scalar
        def _(ae):
            ae.sem_inc(ff_gelu, 2)
            ae.sem_inc(out_copied, 1)
            ae.wait_ge(setup_pe, 1)
            ae.copy(cols[:, :], B0[:, 0:NROWS])
            ae.mul(hcols[:, :], B0[:, 0:NROWS], 0.5).then_inc(setup_a, 1)
            ae.wait_ge(setup_pe, 2)
            ae.copy(wtokT[:, :, :].rearrange("p j d -> p (j d)"), B1[:, :]).then_inc(setup_a, 1)
            ae.wait_ge(setup_pe, 4)
            ae.copy(wqkvT[:, :, :].rearrange("p j d -> p (j d)"), B3[:, 0:384])
            ae.copy(gateT[:, :], B3[:, 384:384 + E]).then_inc(setup_a, 1)
            ae.wait_ge(setup_a, 3)

            def group(gi, peer, nxt, moe):
                m, gj = gi - 1, gi + 1
                done = [0]

                def moe_to(upto):
                    if not moe:
                        return
                    for step in range(done[0], min(upto, NE * FC)):
                        e, f = step // FC, step % FC
                        ae.wait_ge(ff_up, NE * FC * m + step + 1)
                        if f == 0:
                            ae.wait_ge(ff_dn, NE * m + e + 1)
                        ae.activation(hid[:, e % 2, f, :], UP[f % 2][:, 0:N], ACT.Gelu,
                                      bias=col("b1", EORD[e] * FC + f)).then_inc(ff_gelu, 1)
                    done[0] = upto

                def gs(st):
                    return (gj, gi)[st]

                def tanh_half(dst, src, name, i=0):
                    return ae.activation(dst, src, ACT.Tanh, bias=hcol(name, i), scale=0.5)

                def exps(st):
                    ae.wait_ge(sc_shift[st], gs(st) + 1)
                    ae.activation(prob[st][:, :], prob[st][:, :], ACT.Exp).then_inc(sc_exp[st], 1)

                def prob_turned(st):
                    ae.wait_ge(pt_mm[st], gs(st) + 1)
                    ae.copy(probT[st][:, :], (B0, B3)[st][0:L, 0:N]).then_inc(pt_out[st], 1)

                def values(st):
                    ae.wait_ge(v_mm[st], gs(st) + 1)
                    ae.copy(vtok[st][:, :, :].rearrange("p b d -> p (b d)"), (B0, B3)[st][0:L, :]).then_inc(v_out[st], 1)

                def normed(st, i, dst):
                    ae.wait_ge(ln_b[st], 2 * gs(st) + i + 1)
                    ae.copy(dst[:, :], LN_BACK[st][i][:, 0:N]).then_inc(ln_out[st], 1)

                def query_squares(s):
                    n = SUBS[s][1]
                    ae.wait_ge(q_biased, 3 * gi + s + 1)
                    ae.activation(sq[0:n, :], qc[0:n, :], ACT.Square).then_inc(q_sq, 1)

                def turned_queries(s):
                    n = SUBS[s][1]
                    ae.wait_ge(z_t, 3 * gi + s + 1)
                    v = B1[:, :].rearrange("p (c n) -> p c n", n=128)[:, :, 0:n]
                    ae.activation(qnT[:, :, 0:n], v, ACT.Identity, bias=col("lnb"), scale=col("lng"))
                    ae.activation(sqT[:, :, 0:n], v, ACT.Square, bias=col("lnb"), scale=col("lng")).then_inc(q_out, 1)

                def norms(s):
                    n = SUBS[s][1]
                    k = 3 * gi + s + 1
                    ae.wait_ge(ks_mm, k)
                    if s > 0:
                        ae.wait_ge(n_inv, k - 1)
                    ae.copy(nrm[0:n, :], B0[0:n, 0:2 * H]).then_inc(ks_out, 1)

                def scores(s):
                    n = SUBS[s][1]
                    if s > 0:
                        ae.wait_ge(top_done, 3 * gi + s)
                    ae.copy(sc[0:n, 0:H, :].rearrange("p c k -> p (c k)"), B2[0:n, :])
                    ae.copy(sc[0:n, H:2 * H, :].rearrange("p c k -> p (c k)"), B3[0:n, :]).then_inc(ks_out, 1)

                def cells_turned(s):
                    n = SUBS[s][1]
                    ae.wait_ge(cell_t, 3 * gi + s + 1)
                    ae.copy(wcell[:, 0:4 * n], B0[0:NK, 0:4 * n])
                    ae.copy(ecell[:, 0:4 * n], B1[0:NK, 0:4 * n]).then_inc(cell_out, 1)

                def cell_exps(s):
                    n = SUBS[s][1]
                    ae.wait_ge(cand_done, 2 * (3 * gi + s) + 1)
                    ae.activation(cexp[0:n, :, :], cand[0:n, :, :], ACT.Exp).then_inc(cand_exp, 1)

                def expert_inputs(q0, q1):
                    for q in range(q0, q1):
                        ae.wait_ge(in_mm, Q8 * gi + q + 1)
                        ae.activation(act[:, q, :], (B2, B3)[q % 2][:, 0:N], ACT.Gelu).then_inc(in_act, 1)

                if peer:
                    expert_inputs(0, 1)
                    query_squares(0)
                    expert_inputs(1, 4)
                    moe_to(AT["z0"])
                    turned_queries(0)
                    expert_inputs(4, 8)
                    moe_to(AT["k0"])
                    norms(0)
                    scores(0)
                    moe_to(AT["q1"])
                    query_squares(1)
                    moe_to(AT["z1"])
                    turned_queries(1)
                    moe_to(AT["k1"])
                    norms(1)
                    moe_to(AT["s1c"])
                    scores(1)
                    query_squares(2)
                    moe_to(AT["c0"])
                    cell_exps(0)
                    moe_to(AT["z2"])
                    turned_queries(2)
                    moe_to(AT["t0"])
                    cells_turned(0)
                    moe_to(AT["k2"])
                    norms(2)
                    moe_to(AT["s2c"])
                    scores(2)
                    moe_to(AT["c1"])
                    cell_exps(1)
                    moe_to(AT["t1"])
                    cells_turned(1)
                    moe_to(AT["c2"])
                    cell_exps(2)
                    moe_to(AT["t2"])
                    cells_turned(2)
                    moe_to(AT["u2"])
                if nxt:
                    ae.wait_ge(xt_done, 2 * gj + 1)
                    ae.copy(xT[:, 0, :], B0[:, 0:GB * XR]).then_inc(xt_copied, 1)
                moe_to(AT["up"])
                if nxt:
                    ae.wait_ge(tok_mm, gj + 1)
                    if peer:
                        ae.wait_ge(h_ready[B], 2 * gi + 1)
                    ae.activation(hAT[:, :], B0[:, 0:N], ACT.Identity, bias=col("tok_b")).then_inc(h_ready[A], 1)
                moe_to(AT["back0"])
                if nxt:
                    normed(A, 0, inA)
                moe_to(AT["qk"])
                if peer:
                    ae.wait_ge(qk_mm, 2 * gi + 1)
                    ae.activation(qT[:, :], B3[:, 0:N], ACT.Identity, bias=col("bq")).then_inc(qk_out, 1)
                    ae.wait_ge(qk_mm, 2 * gi + 2)
                    ae.activation(kT[:, :], B2[:, 0:N], ACT.Identity, bias=col("bk")).then_inc(qk_out, 1)
                for i in range(2):
                    if nxt:
                        ae.wait_ge(hw_mm, 4 * gj + 2 * i + 1)
                        ae.activation(tT[:, :], B1[:, 0:N], ACT.Relu, bias=col("tb", i)).then_inc(hw_act, 1)
                        ae.wait_ge(hw_mm, 4 * gj + 2 * i + 2)
                        tanh_half(cT[:, :], B0[:, 0:N], "cb", i).then_inc(hw_act, 1)
                    if peer and i == 0:
                        values(B)
                    moe_to(AT[("hw1", "e1")[i]])
                if peer:
                    exps(B)
                moe_to(AT["s1"])
                if nxt:
                    ae.wait_ge(s1_mm, gj + 1)
                    ae.activation(s1row[:, :], B1[0:1, 0:N], ACT.Identity, bias=ab[0:1, 0:1]).then_inc(s1_row, 1)
                    values(A)
                if peer:
                    prob_turned(B)
                moe_to(AT["e0"])
                if nxt:
                    exps(A)
                moe_to(STEPS)
                if nxt:
                    prob_turned(A)
                if moe:
                    ae.wait_ge(out_t, gi)
                    ae.wait_ge(out_done, 16 * NSUB * (gi - 1) + 16)
                    for s, (o, n) in enumerate(SUBS):
                        ins = ae.copy(otile[0:n, s, :], DN[0][0:n, 128 * s:128 * s + 128])
                    ins.then_inc(out_copied, 1)
                if peer:
                    normed(B, 1, xd)
                if nxt:
                    ae.wait_ge(att_mm[A], gj + 1)
                    ae.copy(attT[:, :], B1[:, 0:N]).then_inc(att_out, 1)
                    ae.wait_ge(gate_mm, 2 * gj + 1)
                    tanh_half(tT[:, :], B0[:, 0:N], "ffb").then_inc(gate_act, 1)
                    ae.wait_ge(gate_mm, 2 * gj + 2)
                    tanh_half(cT[:, :], B1[:, 0:N], "frb").then_inc(gate_act, 1)
                if peer:
                    for i in range(2):
                        ae.wait_ge(lg_shift, 2 * gi + i + 1)
                        ae.activation(ge[:, :, :], ge[:, :, :], ACT.Exp).then_inc(lg_exp, 1)
                    ae.wait_ge(comb_t, gi + 1)
                    if moe:
                        ae.wait_ge(comb_out, 16 * gi)
                    ae.copy(combT[:, :], B2[0:E, 0:N]).then_inc(comb_copied, 1)
                if nxt:
                    normed(A, 1, hnT)

            group(-1, False, True, False)
            ae.wait_ge(setup_pe, 6)
            for i in range(2):
                ins = ae.copy(dnT[:, 4 * i:4 * i + 4, :].rearrange("p q d -> p (q d)"), DN[i][:, :])
            ins.then_inc(setup_a, 1)
            group(0, True, True, False)
            with ae.Fori(1, G - 1) as g:
                group(g, True, True, True)
            group(G - 1, True, False, True)
            group(G, False, False, True)

        @block.vector
        def _(dve):
            dve.sem_inc(ff_dn, 2)
            dve.sem_inc(ff_term, 2)
            chain = [0]

            def set_link(ins):
                chain[0] += 1
                ins.then_inc(v_set, 1)
                dve.wait_ge(v_set, chain[0])

            dve.wait_ge(wts_in, N_WTS[0])
            set_link(dve.tensor_tensor(sq[0:PK, 0:2 * HALF], keys[:, 0:2, :].rearrange("p c k -> p (c k)"),
                                       keys[:, 0:2, :].rearrange("p c k -> p (c k)"), ALU.mult))
            set_link(dve.tensor_reduce(kn[:, :], sq[0:PK, 0:2 * HALF].rearrange("p (c k) -> p c k", k=HALF), AX, ALU.add))
            dve.tensor_scalar(kn[:, :], kn[:, :], 1e-24, None, ALU.max).then_inc(setup_v, 1)
            dve.wait_ge(setup_pe, 3)
            set_link(dve.tensor_copy(wqcT[:, :], B2[:, :]))
            for t in (wqcT, bqc):
                set_link(dve.tensor_reduce(bqm[:, :], heads(t, 128), AX, ALU.add))
                set_link(dve.tensor_scalar(bqm[:, :], bqm[:, :], 1.0 / QD, None, ALU.mult))
                set_link(dve.tensor_tensor(heads(t, 128), heads(t, 128), spread(bqm, 128, H, QD), ALU.subtract))
            dve.sem_inc(setup_v, 1)
            dve.tensor_copy(merge16[:, :, :], merge[:, :, :])
            dve.wait_ge(setup_p, 1)
            dve.wait_ge(setup_pe, 5)
            for c in range(4):
                ins = dve.tensor_copy(keysBD[HALF * c:HALF * c + HALF, PK * c:PK * c + PK],
                                      UP[0][HALF * c:HALF * c + HALF, 0:PK])
            ins.then_inc(setup_v, 1)
            dve.wait_ge(setup_v, 3)

            def group(gi, peer, nxt, moe):
                m, gj = gi - 1, gi + 1
                links, done = [0, 0], [0]

                def gs(st):
                    return (gj, gi)[st]

                def link(st, ins):
                    links[st] += 1
                    ins.then_inc(v_link[st], 1)
                    dve.wait_ge(v_link[st], gs(st) * V_LINKS[st] + links[st])

                def own_wait():
                    dve.sem_inc(v_met, 1)

                def moe_to(upto):
                    if not moe:
                        return
                    for e in range(done[0], upto // FC - 1):
                        x = NE * m + e
                        dve.wait_ge(ff_dn, x + 3)
                        dve.wait_ge(ff_acc, (NE + 1) * m + max(e, 1))
                        b = DN[e % 2][:, 0:N]
                        if EORD[e] >= E:
                            ins = dve.tensor_scalar(term[:, e % 2, :], b, col("b2", EORD[e]), 1.0 / SH, ALU.add, ALU.mult)
                        else:
                            r = EORD[e] // 4
                            if EORD[e] % 4 == 0:
                                dve.wait_ge(comb_in[r % 2], 16 * (E // 8 * m + r // 2 + 1))
                            ins = dve.scalar_tensor_tensor(term[:, e % 2, :], b, col("b2", EORD[e]),
                                                           combB[:, r % 2, EORD[e] % 4, :], ALU.add, ALU.mult)
                        ins.then_inc(ff_term, 1)
                        done[0] = e + 1

                def token_stats(st, i):
                    b = LN_IN[st][i]
                    dve.wait_ge(ln_t[st], 2 * gs(st) + i + 1)
                    for s, (o, n) in enumerate(SUBS):
                        ins = dve.bn_stats(bn[st][0:n, s, :], b[0:n, 128 * s:128 * s + 128])
                    link(st, ins)
                    own_wait()
                    for s, (o, n) in enumerate(SUBS):
                        ins = dve.bn_aggr(mv[st][0:n, s, :], bn[st][0:n, s, :])
                    ins.then_inc(ln_mv[st], 1)

                def norm_tokens(st, i):
                    b = LN_IN[st][i]
                    dve.wait_ge(ln_rstd[st], 2 * gs(st) + i + 1)
                    for s, (o, n) in enumerate(SUBS):
                        ins = dve.tensor_scalar(xn[st][0:n, s, :], b[0:n, 128 * s:128 * s + 128], mv[st][0:n, s, 0:1],
                                                rstd[st][0:n, s:s + 1], ALU.subtract, ALU.mult)
                    ins.then_inc(ln_xn[st], 1)

                def shift_scores(st):
                    dve.wait_ge(sc_mm[st], gs(st) + 1)
                    s = (B1, B2)[st][0:L, 0:N].rearrange("p (b j) -> p b j", j=L)
                    p = prob[st][:, :].rearrange("p (b j) -> p b j", j=L)
                    link(st, dve.tensor_reduce(amax[st][:, :], s, AX, ALU.max))
                    if st == A:
                        link(st, dve.tensor_scalar(amax[st][:, :], amax[st][:, :], 0.0, None, ALU.max))
                        dve.scalar_tensor_tensor(p, s, 0.0, spread(amax[st], L, GB, L), ALU.max,
                                                 ALU.subtract).then_inc(sc_shift[st], 1)
                    else:
                        dve.tensor_tensor(p, s, spread(amax[st], L, GB, L), ALU.subtract).then_inc(sc_shift[st], 1)

                def sum_exps(st):
                    dve.wait_ge(sc_exp[st], gs(st) + 1)
                    p = prob[st][:, :].rearrange("p (b j) -> p b j", j=L)
                    link(st, dve.tensor_reduce(asum[st][:, :], p, AX, ALU.add))
                    dve.reciprocal(arec[st][:, :], asum[st][:, :]).then_inc(sc_rec[st], 1)

                def query_bias(s):
                    n = SUBS[s][1]
                    dve.wait_ge(q_mm, 3 * gi + s + 1)
                    dve.tensor_tensor(qc[0:n, :], B0[0:n, :], bqc[0:n, :], ALU.add).then_inc(q_biased, 1)

                def query_sum(s):
                    n = SUBS[s][1]
                    dve.wait_ge(q_sq, 3 * gi + s + 1)
                    dve.tensor_reduce(qv[0:n, :], heads(sq, n), AX, ALU.add).then_inc(q_var, 1)

                def query_scale(s):
                    n = SUBS[s][1]
                    dve.wait_ge(q_rstd, 3 * gi + s + 1)
                    dve.tensor_tensor(heads(qc, n), heads(qc, n), spread(qr, n, H, QD), ALU.mult).then_inc(q_z, 1)

                def first_keys(s):
                    n = SUBS[s][1]
                    dve.wait_ge(ks_out, 2 * (3 * gi + s + 1))
                    own_wait()
                    for c in range(2 * H):
                        ins = dve.max(top[0:n, c, 0:8], sc[0:n, c, :])
                    link(B, ins)

                def first_indices(s):
                    n = SUBS[s][1]
                    own_wait()
                    for c in range(2 * H):
                        ins = dve.max_index(idx[0:n, c, 0:8], top[0:n, c, 0:8], sc[0:n, c, :])
                    link(B, ins)

                def drop_keys(s):
                    n = SUBS[s][1]
                    own_wait()
                    for c in range(2 * H):
                        ins = dve.match_replace(sc[0:n, c, :], top[0:n, c, 0:8], sc[0:n, c, :], TAKEN)
                    link(B, ins)

                def next_keys(s):
                    n = SUBS[s][1]
                    own_wait()
                    for c in range(2 * H):
                        ins = dve.max(top[0:n, c, 8:16], sc[0:n, c, :])
                    link(B, ins)

                def next_indices(s):
                    n = SUBS[s][1]
                    own_wait()
                    for c in range(2 * H):
                        ins = dve.max_index(idx[0:n, c, 8:16], top[0:n, c, 8:16], sc[0:n, c, :])
                    link(B, ins)

                def found(s):
                    n = SUBS[s][1]
                    dve.wait_ge(n_inv, 3 * gi + s + 1)
                    dve.tensor_tensor(topn[0:n], top[0:n], spread(inv[:, s % 2, :], n, 2 * H, K), ALU.mult)
                    dve.tensor_copy(idf[0:n], idx[0:n]).then_inc(top_done, 1)

                def first_pairs(s):
                    n = SUBS[s][1]
                    dve.wait_ge(cand_done, 2 * (3 * gi + s) + 1)
                    own_wait()
                    for h in range(H):
                        ins = dve.max(best[0:n, h, 0:8], cand[0:n, h, :])
                    link(B, ins)
                    own_wait()
                    for h in range(H):
                        ins = dve.match_replace(cand2[0:n, h, :], best[0:n, h, 0:8], cand[0:n, h, :], TAKEN)
                    link(B, ins)

                def next_pairs(s):
                    n = SUBS[s][1]
                    own_wait()
                    for h in range(H):
                        ins = dve.max(best[0:n, h, 8:16], cand2[0:n, h, :])
                    link(B, ins)
                    own_wait()
                    for h in range(H):
                        ins = dve.match_replace(cand2[0:n, h, :], best[0:n, h, 8:16], cand2[0:n, h, :], TAKEN)
                    link(B, ins)

                def weigh(s):
                    n = SUBS[s][1]
                    k = 3 * gi + s + 1
                    dve.wait_ge(cand_exp, k)
                    link(B, dve.scalar_tensor_tensor(cw_[0:n].rearrange("p h k -> p (h k)"),
                                                     cand2[0:n].rearrange("p h k -> p (h k)"), TAKEN / 10,
                                                     cexp[0:n].rearrange("p h k -> p (h k)"), ALU.is_lt, ALU.mult))
                    link(B, dve.tensor_reduce(z[0:n], cw_[0:n], AX, ALU.add))
                    link(B, dve.tensor_scalar(z[0:n], z[0:n], 1.0 / WSCALE, None, ALU.mult))
                    dve.reciprocal(zr[0:n], z[0:n]).then_inc(w_raw, 1)
                    dve.wait_ge(cand_done, 2 * k)
                    dve.scalar_tensor_tensor(epick[0:n].rearrange("p h k -> p (h k)"),
                                             cand2[0:n].rearrange("p h k -> p (h k)"), TAKEN / 10,
                                             cexpert[0:n, s % 2].rearrange("p h k -> p (h k)"), ALU.is_lt,
                                             ALU.mult).then_inc(e_picked, 1)

                def hot(s):
                    n = SUBS[s][1]
                    k = 3 * gi + s + 1
                    w = 2 * n
                    dve.wait_ge(slots_mm, k)
                    dve.tensor_scalar(pi[:, 0:w], B0[0:NS, w:2 * w], 0.125, -0.4375, ALU.mult, ALU.add)
                    link(B, dve.tensor_copy(whi[:, 0:w], B0[0:NS, 0:w]))
                    dve.scalar_tensor_tensor(qi[:, 0:w], pi[:, 0:w], -8.0, B0[0:NS, w:2 * w], ALU.mult, ALU.add)
                    dve.tensor_tensor(wlo[:, 0:w], B0[0:NS, 0:w], whi[:, 0:w], ALU.subtract).then_inc(pq_ready, 1)
                    for p in range(P16):
                        dve.tensor_scalar(ph[:, 0:n // 4, p, :], pi[:, 0:w].rearrange("p (g t) -> p g t", t=8),
                                          float(p), None, ALU.is_equal)
                    dve.wait_ge(pq_ready, k)
                    for q in range(Q8):
                        ins = dve.tensor_scalar(qh[:, q, 0:w], qi[:, 0:w], float(q), None, ALU.is_equal)
                    link(B, ins)
                    for part, src in enumerate((whi, wlo)):
                        ins = dve.tensor_tensor(qw[:, part, :, 0:w], qh[:, :, 0:w],
                                                src[:, 0:w].unsqueeze(1).broadcast_to([NS, Q8, w]), ALU.mult)
                    ins.then_inc(q_hot, 1)

                def own_blocks(s):
                    o, n = SUBS[s]
                    if s == 0:
                        dve.wait_ge(act_masked, 2 * gi + 2)
                    dve.wait_ge(pq_mm, 3 * gi + s + 1)
                    for i, b in enumerate((B2, B3)):
                        g = min(8, n // 8 - 8 * i)
                        t = slice(o + 64 * i, o + 64 * i + 8 * g)
                        ins = dve.tensor_tensor(
                            act[:, :, t].rearrange("p q (g t) -> p q g t", t=8),
                            b[:, 0:64 * g].rearrange("p (g q t) -> p q g t", q=Q8, t=8),
                            act[:, :, t].rearrange("p q (g t) -> p q g t", t=8), ALU.mult)
                    ins.then_inc(peer_x, 1)

                if peer:
                    query_bias(0)
                    query_sum(0)
                    query_scale(0)
                    moe_to(AT["k0"])
                    first_keys(0)
                    query_bias(1)
                    first_indices(0)
                    query_sum(1)
                    moe_to(AT["q1"])
                    drop_keys(0)
                    query_scale(1)
                    next_keys(0)
                    moe_to(AT["z1"])
                    next_indices(0)
                    moe_to(AT["k1"])
                    found(0)
                    query_bias(2)
                    moe_to(AT["c0"])
                    first_pairs(0)
                    query_sum(2)
                    next_pairs(0)
                    query_scale(2)
                    moe_to(AT["z2"])
                    weigh(0)
                    moe_to(AT["t0"])
                    first_keys(1)
                    first_indices(1)
                    hot(0)
                    moe_to(AT["t0"] + 4)
                    drop_keys(1)
                    next_keys(1)
                    moe_to(AT["u0"])
                    own_blocks(0)
                    next_indices(1)
                    found(1)
                    moe_to(AT["c1"])
                    first_pairs(1)
                    next_pairs(1)
                    weigh(1)
                    moe_to(AT["t1"])
                    first_keys(2)
                    first_indices(2)
                    hot(1)
                    moe_to(AT["t1"] + 4)
                    drop_keys(2)
                    moe_to(AT["u1"])
                    own_blocks(1)
                    next_keys(2)
                    next_indices(2)
                    found(2)
                    moe_to(AT["c2"])
                    first_pairs(2)
                    next_pairs(2)
                    weigh(2)
                    moe_to(AT["t2"])
                    hot(2)
                    moe_to(AT["u2"])
                    own_blocks(2)
                if nxt:
                    dve.wait_ge(xt_done, 2 * gj + 2)
                    dve.tensor_copy(xT[:, 1, :], B1[:, 0:GB * XR]).then_inc(xt_copied, 1)
                moe_to(AT["up"])
                if peer:
                    dve.wait_ge(up_mm, gi + 1)
                    dve.scalar_tensor_tensor(hT[:, :], B2[:, 0:N], 1.0 / WSCALE, hAT[:, :], ALU.mult,
                                             ALU.add).then_inc(h_ready[B], 1)
                    token_stats(B, 0)
                moe_to(AT["ln0"])
                if peer:
                    norm_tokens(B, 0)
                if nxt:
                    token_stats(A, 0)
                moe_to(AT["back0"])
                if peer:
                    dve.wait_ge(ln_b[B], 2 * gi + 1)
                    dve.tensor_tensor(inT[:, :].rearrange("p (b l) -> p b l", l=L),
                                      B2[:, 0:N].rearrange("p (b l) -> p b l", l=L),
                                      posT[:, :].unsqueeze(1).broadcast_to([128, GB, L]), ALU.add).then_inc(ln_out[B], 1)
                if nxt:
                    norm_tokens(A, 0)
                moe_to(AT["qk"])
                for i in range(2):
                    if nxt:
                        dve.wait_ge(hw_act, 4 * gj + 2 * i + 2)
                        src, dst = ((inA, x1T), (x1T, x2T))[i]
                        link(A, dve.tensor_tensor(dT[:, :], tT[:, :], src[:, :], ALU.subtract))
                        link(A, dve.scalar_tensor_tensor(dT[:, :], cT[:, :], 1.0, dT[:, :], ALU.add, ALU.mult))
                        dve.scalar_tensor_tensor(dst[:, :], dT[:, :], 0.5, src[:, :], ALU.mult, ALU.add).then_inc(hw_x, 1)
                    if i == 0:
                        moe_to(AT["hw1"])
                        if peer:
                            shift_scores(B)
                    elif nxt:
                        dve.wait_ge(hw_x, 2 * gj + 2)
                        dve.tensor_scalar(uT[:, :], x2T[:, :], col("aw", 2), col("aw", 1), ALU.mult,
                                          ALU.add).then_inc(u_ready, 1)
                if peer:
                    sum_exps(B)
                moe_to(AT["s1"])
                if nxt:
                    shift_scores(A)
                moe_to(AT["e0"])
                if peer:
                    dve.wait_ge(att_mm[B], gi + 1)
                    dve.scalar_tensor_tensor(hT[:, :], B2[:, 0:N], col("bv"), hT[:, :], ALU.add,
                                             ALU.add).then_inc(h_ready[B], 1)
                if nxt:
                    sum_exps(A)
                moe_to(AT["lnB1"])
                if peer:
                    token_stats(B, 1)
                moe_to(STEPS)
                if peer:
                    norm_tokens(B, 1)
                    dve.wait_ge(lg_mm, gi + 1)
                    for s, (o, n) in enumerate(SUBS):
                        ins = dve.tensor_copy(lg[0:n, s, 0:E], B3[0:n, E * s:E * s + E])
                    link(B, ins)
                    link(B, dve.tensor_reduce(gs_[:, :], lg[:, :, 0:E], AX, ALU.max))
                    dve.tensor_tensor(ge[:, :, :], lg[:, :, 0:E], spread(gs_, 128, NSUB, E),
                                      ALU.subtract).then_inc(lg_shift, 1)
                if nxt:
                    dve.wait_ge(gate_act, 2 * gj + 2)
                    dve.scalar_tensor_tensor(dT[:, :], cT[:, :], 1.0, inA[:, :], ALU.add, ALU.mult)
                    link(A, dve.tensor_scalar(tT[:, :], tT[:, :], 0.5, 0.5, ALU.mult, ALU.add))
                    dve.scalar_tensor_tensor(x1T[:, :], dT[:, :], 0.5, hAT[:, :], ALU.mult, ALU.add)
                    link(A, dve.tensor_tensor(x2T[:, :], tT[:, :], tT[:, :], ALU.mult))
                    dve.tensor_tensor(hAT[:, :], x1T[:, :], x2T[:, :], ALU.add).then_inc(h_ready[A], 1)
                    token_stats(A, 1)
                if peer:
                    dve.wait_ge(lg_exp, 2 * gi + 1)
                    link(B, dve.tensor_reduce(gs_[:, :], ge[:, :, :], AX, ALU.add))
                    link(B, dve.reciprocal(gr[:, :], gs_[:, :]))
                    link(B, dve.tensor_tensor(lg[:, :, 0:E], ge[:, :, :], spread(gr, 128, NSUB, E), ALU.mult))
                    own_wait()
                    for s, (o, n) in enumerate(SUBS):
                        ins = dve.max(m8[0:n, s, :], lg[0:n, s, :])
                    link(B, ins)
                    dve.tensor_tensor(ge[:, :, :], lg[:, :, 0:E], m8[:, :, 0:1].broadcast_to([128, NSUB, E]),
                                      ALU.subtract).then_inc(lg_shift, 1)
                    link(B, dve.tensor_copy(t8[:, :, 0:TOPK], m8[:, :, 0:TOPK]))
                    own_wait()
                    for s, (o, n) in enumerate(SUBS):
                        ins = dve.match_replace(lg2[0:n, s, :], t8[0:n, s, :], lg[0:n, s, :], TAKEN)
                    link(B, ins)
                if nxt:
                    norm_tokens(A, 1)
                if peer:
                    dve.wait_ge(lg_exp, 2 * gi + 2)
                    link(B, dve.scalar_tensor_tensor(comb[:, :, :], lg2[:, :, 0:E], TAKEN / 10, ge[:, :, :],
                                                     ALU.is_lt, ALU.mult))
                    link(B, dve.tensor_reduce(gs_[:, :], comb[:, :, :], AX, ALU.add))
                    link(B, dve.reciprocal(gr[:, :], gs_[:, :]))
                    dve.tensor_tensor(comb[:, :, :], comb[:, :, :], spread(gr, 128, NSUB, E),
                                      ALU.mult).then_inc(comb_ready, 1)
                assert links == [nxt * V_LINKS[A], peer * V_LINKS[B]], f"V_LINKS {links}"

            group(-1, False, True, False)
            group(0, True, True, False)
            with dve.Fori(1, G - 1) as g:
                group(g, True, True, True)
            group(G - 1, True, False, True)
            group(G, False, False, True)


_INS = ['x', 'L0_tok_W', 'L0_tok_b', 'L0_attn_tW', 'L0_attn_tb', 'L0_attn_cW', 'L0_attn_cb', 'L0_attn_aW',
        'L0_attn_ab', 'L0_attn_frW', 'L0_attn_frb', 'L0_attn_ffW', 'L0_attn_ffb', 'L0_ffn_Wq', 'L0_ffn_bq',
        'L0_ffn_ln_g', 'L0_ffn_ln_b', 'L0_ffn_keys0', 'L0_ffn_keys1', 'L0_ffn_expert_down',
        'L0_ffn_expert_up', 'L1_attn_Wq', 'L1_attn_bq', 'L1_attn_Wk', 'L1_attn_bk', 'L1_attn_Wv',
        'L1_attn_bv', 'L1_ffn_gate_w', 'L1_ffn_re_w1', 'L1_ffn_re_b1', 'L1_ffn_re_w2', 'L1_ffn_re_b2',
        'L1_ffn_se_w1', 'L1_ffn_se_b1', 'L1_ffn_se_w2', 'L1_ffn_se_b2']


def merge_table():
    def area(a, b):
        return sum(max([c + 1 for r, c in (a, b) if r >= row], default=0) for row in range(K))

    grid = [(r + i, c) for r, m, w in CELLS for i in range(m) for c in range(w)]
    slot = {}
    for cell in sorted(grid, key=lambda x: (x[0] + 1) * (x[1] + 1)):
        if area(cell, cell) > K:
            slot[cell] = 0
            continue
        used = {s for other, s in slot.items() if area(cell, other) <= K}
        slot[cell] = min(set(range(len(grid))) - used)
    assert max(slot.values()) < SLOTS
    table = np.zeros((2 * NC, 2, 4 * SLOTS), np.float32)
    for pair in range(2):
        for head in range(2):
            for i, cell in enumerate(grid):
                table[head * NC + i, pair, (2 * pair + head) * SLOTS + slot[cell]] = 1.0
    return table


def shape_constants():
    pos = np.arange(L, dtype=np.float32)[:, None]
    div = np.exp(np.arange(0, D, 2, dtype=np.float32) * np.float32(-np.log(np.float32(10000.0)) / D))
    ang = (pos * div.astype(np.float32)).astype(np.float32)
    mask = np.tile(np.eye(8, dtype=np.float32), (P16, 1))
    return {"c_ident": np.eye(128, dtype=np.float32),
            "c_posT": np.ascontiguousarray(np.concatenate([np.sin(ang), np.cos(ang)], axis=-1).T.astype(np.float32)),
            "c_blockmask": mask,
            "c_merge": merge_table(),
            "c_halfones": np.repeat(np.eye(4, dtype=np.float32), HALF, axis=0)}


def kernel(**inputs):
    import concourse.bacc as bacc
    from concourse.bass_utils import run_bass_kernel_spmd

    nc = bacc.Bacc("TRN2", target_bir_lowering=False, num_devices=1)
    arrays, aps = {}, {}
    for name, v in [(n, inputs[n]) for n in _INS] + list(shape_constants().items()):
        v = np.ascontiguousarray(v)
        arrays[f"in_{name}_dram"] = v
        aps[name] = nc.dram_tensor(f"in_{name}_dram", v.shape, mybir.dt.from_np(v.dtype), kind="ExternalInput").ap()
    out = nc.dram_tensor("out_0_dram", (NB, L, D), F32, kind="ExternalOutput").ap()
    build(nc, aps, out)
    r = run_bass_kernel_spmd(nc, [arrays], core_ids=[0])
    return r.results[0]["out_0_dram"]
```

```python
from contextlib import ExitStack

import numpy as np

import concourse.bass as bass
from concourse import mybir

F32 = mybir.dt.float32
F16 = mybir.dt.float16
U16 = mybir.dt.uint16
I32 = mybir.dt.int32
I16 = mybir.dt.int16
ALU = mybir.AluOpType
ACT = mybir.ActivationFunctionType
AX = mybir.AxisListType.X

D = 128
NB, T, CH = 32, 750, 32
PL, PS = 16, 8
L = (T - PL) // PS + 1
GB = 4
G = NB // GB
N = GB * L
SUBS = [(0, 128), (128, 128), (256, N - 256)]
NSUB = len(SUBS)
XR = L + 1
H, QD, PK, K = 8, 64, 64, 16
HALF = QD // 2
HP = H // 2
CELLS = [(0, 1, 16), (1, 1, 8), (2, 2, 5), (4, 4, 3), (8, 8, 1)]
SLOTS = 24
NC = sum(n * w for _, n, w in CELLS)
P16, Q8 = 16, 8
E, SH, F, TOPK = 16, 2, 512, 4
FC = F // 128
NE = E + SH
EPS = 1e-5
CB = 2
TAKEN = -1e30

ROWS = [("b1", NE * FC), ("b2", NE), ("tok_b", 1), ("tb", 2), ("cb", 2), ("aw", 3), ("frb", 1),
        ("ffb", 1), ("lng", 1), ("lnb", 1), ("bq", 1), ("bk", 1), ("bv", 1)]
COL, NROWS = {}, 0
for _name, _n in ROWS:
    COL[_name] = NROWS
    NROWS += _n

EORD = list(range(E, NE)) + list(range(E))
WSCALE = 1024.0
V_LINKS, P_LINKS = (16, 49, 6), (5, 5)
A, B, C = 0, 1, 2

STEPS = (NE + 1) * FC
XSCALE_EXP, WEXP, BIAS = 10, 14, 127
HEAD = FC
AT = dict(a2=5, z1=6, k1=8, a3=8, cb=8, s1c=8, c0=11, a5=15, z2=16, t0=17, a7=19, u0=23, a9=24, k2=26, s2c=27,
          c1=29, a10=30, a11=32, t1=34, a12=35, ea=35, u1=40, a13=41, a14=41, c2=43, a15=43, t2=46, a16=48,
          u2=53, a17=55, up=55, a18=56, ln0=56, back0=59, zq=60, qk=60, kq=61, v=62, e1=65, i0=67, pt=67, e0=69,
          lnB1=71, i1=73)


def build(nc, a, out):
    ctx = ExitStack()
    with ctx:
        def sb(name, shape, dt=F32):
            return ctx.enter_context(nc.sbuf_tensor(name, shape, dt))

        def sem(name):
            return ctx.enter_context(nc.semaphore(name))

        bank = [ctx.enter_context(nc.psum_tensor(f"bank{i}", [128, 512], F32)) for i in range(8)]
        B0, B1, B2, B3 = bank[:4]
        UP, DN = bank[4:6], bank[6:8]
        comb_dram = nc.dram_tensor("comb_dram", [G, E, N], F32, kind="Internal").ap()

        ident = sb("ident", [128, 128])
        posT = sb("posT", [128, L])
        blockmask = sb("blockmask", [128, 8])
        halfones = sb("halfones", [128, 4])
        ones = sb("ones", [1, 128])
        onesE = sb("onesE", [NE, 128])
        nhalf = sb("nhalf", [128, 16])
        rows = sb("rows", [NROWS, 128])
        cols = sb("cols", [128, NROWS])
        hcols = sb("hcols", [128, NROWS])
        ab = sb("ab", [1, 1])
        wtokT = sb("wtokT", [128, 4, 128])
        wqcT = sb("wqcT", [128, 512])
        wqkvT = sb("wqkvT", [128, 3, 128])
        gateT = sb("gateT", [128, E])
        bqc = sb("bqc", [128, 512])
        bqm = sb("bqm", [128, H])
        tw = sb("tw", [128, 2, 128])
        cw = sb("cw", [128, 2, 128])
        ffw = sb("ffw", [128, 2, 128])
        frw = sb("frw", [128, 2, 128])
        keys = sb("keys", [PK, 4, HALF])
        keys2 = sb("keys2", [PK, 4, HALF])
        kn = sb("kn", [PK, 2])
        keysBD = sb("keysBD", [128, 256])
        merge = sb("merge", [2 * NC, 2, 4 * SLOTS])
        merge16 = sb("merge16", [2 * NC, 2, 4 * SLOTS], F16)
        dnT = sb("dnT", [128, Q8, 128])
        upR = sb("upR", [128, Q8, 128])
        w1 = sb("w1", [128, NE, F])
        w2 = sb("w2", [128, NE, FC, 128])

        xin = sb("xin", [XR, GB, 2, 128])
        hT = sb("hT", [128, N])
        shared = sb("shared", [128, 5120])
        qT, kT, probs, probsT = (shared[:, i * N:(i + 1) * N] for i in range(4))
        vtokB = shared[0:L, 4 * N:4 * N + GB * 128].rearrange("p (b d) -> p b d", b=GB)
        xnB = shared[:, 4 * N + GB * 128:4 * N + GB * 128 + NSUB * 128]
        xd = shared[:, 4 * N + GB * 128 + NSUB * 128:5 * N + GB * 128 + NSUB * 128]
        early = sb("early", [128, 2 * GB * XR + 4 * N + GB * 128])
        xT = early[:, 0:2 * GB * XR].rearrange("p (s r) -> p s r", s=2)
        tT, cT = early[:, 0:N], early[:, N:2 * N]
        at = 2 * GB * XR
        dT, x1T, x2T, inA = (early[:, at + i * N:at + (i + 1) * N] for i in range(4))
        vtokA = early[0:L, at + 4 * N:at + 4 * N + GB * 128].rearrange("p (b d) -> p b d", b=GB)
        xnA = early[:, at + N:at + N + NSUB * 128]
        uT, attT = tT, cT
        prob, probT = (dT[0:L, :], probs[0:L, :]), (x1T[0:L, :], probsT[0:L, :])
        xn = [t.rearrange("p (s d) -> p s d", s=NSUB) for t in (xnA, xnB)]
        vtok = (vtokA, vtokB)
        bn = [sb(f"bn{i}", [128, NSUB, 6]) for i in range(2)]
        mv = [sb(f"mv{i}", [128, NSUB, 2]) for i in range(2)]
        rstd = [sb(f"rstd{i}", [128, NSUB]) for i in range(2)]
        inT = sb("inT", [128, N])
        hAT = sb("hAT", [128, N])
        s1row = cT[0:1, :]
        amax = [sb(f"amax{i}", [L, GB]) for i in range(2)]
        asum = [sb(f"asum{i}", [L, GB]) for i in range(2)]
        arec = [sb(f"arec{i}", [L, GB]) for i in range(2)]
        hnT = sb("hnT", [128, N])
        act = sb("act", [128, Q8, N])
        act_raw = act[:, 0:5, :].rearrange("p q n -> p (q n)")[:, 0:12 * 128].rearrange("p (j n) -> p j n", n=128)
        dnraw = act[:, 5:8, :].rearrange("p q n -> p (q n)")[:, 0:Q8 * 128].rearrange("p (j n) -> p j n", n=128)
        qc = sb("qc", [128, 512])
        sq = sb("sq", [128, 512])
        qv = sb("qv", [128, H])
        qr = sb("qr", [128, H])
        qnT = sb("qnT", [128, HP, 128])
        sqT = sb("sqT", [128, HP, 128])
        sc = sb("sc", [128, 2 * H, PK])
        nrm = sb("nrm", [128, 2 * H])
        inv = sb("inv", [128, 2, 2 * H])
        top = sb("top", [128, 2 * H, K])
        topn = sb("topn", [128, 2 * H, K])
        idx = sb("idx", [128, 2 * H, K], U16)
        idf = sb("idf", [128, 2 * H, K])
        cand = sb("cand", [128, H, NC])
        cand2 = sb("cand2", [128, H, NC])
        best = sb("best", [128, H, K])
        cexp = sb("cexp", [128, H, NC])
        cexpert = sb("cexpert", [128, 2, H, NC], F16)
        cw_ = sb("cw_", [128, H, NC])
        z = sb("z", [128, H])
        zr = sb("zr", [128, H])
        NK = 2 * NC
        NS = 4 * SLOTS
        epick = sb("epick", [128, H, NC])
        wcell = sq[0:NK, :]
        ecell = sb("ecell", [NK, 512], F16)
        pi = sb("pi", [NS, 256], I16)
        qi = sb("qi", [NS, 256], F16)
        whi = sb("whi", [NS, 256], F16)
        wlo = sb("wlo", [NS, 256], F16)
        hot16 = shared[0:NS, 0:5120].bitcast(F16)
        ph = hot16[:, 0:P16 * 256].rearrange("p (g k t) -> p g k t", k=P16, t=8)
        qh = hot16[:, P16 * 256:(P16 + Q8) * 256].rearrange("p (k n) -> p k n", k=Q8)
        qw = hot16[:, (P16 + Q8) * 256:(P16 + 3 * Q8) * 256].rearrange("p (h k n) -> p h k n", h=2, k=Q8)
        lg = sb("lg", [128, NSUB, E + 4])
        lg2 = sb("lg2", [128, NSUB, E + 4])
        ge = sb("ge", [128, NSUB, E])
        gs_ = sb("gs_", [128, NSUB])
        gr = sb("gr", [128, NSUB])
        m8 = sb("m8", [128, NSUB, 8])
        t8 = sb("t8", [128, NSUB, 8])
        comb = sb("comb", [128, NSUB, E])
        combT = sb("combT", [E, N])
        combB = sb("combB", [128, 2, CB, N])
        xd16 = sb("xd16", [128, 2, N], F16)
        wmax = sb("wmax", [128, NE])
        wtop = sb("wtop", [NE, 1])
        wpow = sb("wpow", [NE, 2], I32)
        wdiag = sb("wdiag", [NE, 2, NE])
        wscale = sb("wscale", [128, 2, NE])
        hid = sb("hid", [128, 2, FC, N])
        halves = hid[:, :, :, :].rearrange("p h f n -> p (h f n)")[:, 0:4 * F].bitcast(F16).rearrange(
            "p (r h f) -> p r h f", r=4, h=2)
        w1h = w1[:, :, :].rearrange("p e f -> p (e f)").bitcast(F16).rearrange("p (e h f) -> p e h f", h=2, f=F)
        term = sb("term", [128, 2, N])
        acc = sb("acc", [128, N])
        otile = sb("otile", [128, NSUB, 128])

        x_in, const_in, wts_in, exp_in, peer_in = (sem("x_in"), sem("const_in"), sem("wts_in"), sem("exp_in"),
                                                   sem("peer_in"))
        setup_v, setup_p, setup_pe, setup_a, v_set = (sem("setup_v"), sem("setup_p"), sem("setup_pe"),
                                                      sem("setup_a"), sem("v_set"))
        comb_out, out_done = sem("comb_out"), sem("out_done")
        comb_in = [sem("comb_in_even"), sem("comb_in_odd")]
        def sems(name):
            return sem(name + "_A"), sem(name + "_B")

        v_link, p_link = (*sems("v_link"), sem("v_link_C")), sems("p_link")
        v_met, p_met = sem("v_met"), sem("p_met")
        xt_done, xt_copied, tok_mm = sem("xt_done"), sem("xt_copied"), sem("tok_mm")
        h_ready = sems("h_ready")
        ln_t, ln_mv, ln_rstd, ln_xn, ln_b, ln_out = (sems("ln_t"), sems("ln_mv"), sems("ln_rstd"), sems("ln_xn"),
                                                     sems("ln_b"), sems("ln_out"))
        h_kept = sem("h_kept")
        hw_mm, hw_act, hw_x, u_ready = sem("hw_mm"), sem("hw_act"), sem("hw_x"), sem("u_ready")
        s1_mm, s1_row, gate_mm, gate_act = sem("s1_mm"), sem("s1_row"), sem("gate_mm"), sem("gate_act")
        qk_mm, qk_out, v_mm, v_out = sem("qk_mm"), sem("qk_out"), sems("v_mm"), sems("v_out")
        sc_mm, sc_shift, sc_exp, sc_rec, prob_ready = (sems("sc_mm"), sems("sc_shift"), sems("sc_exp"),
                                                       sems("sc_rec"), sems("prob_ready"))
        pt_mm, pt_out, att_mm, att_out = sems("pt_mm"), sems("pt_out"), sems("att_mm"), sem("att_out")
        in_mm, in_act, act_masked = sem("in_mm"), sem("in_act"), sem("act_masked")
        q_mm, q_biased, q_sq, q_var, q_rstd, q_z = (sem("q_mm"), sem("q_biased"), sem("q_sq"), sem("q_var"),
                                                    sem("q_rstd"), sem("q_z"))
        norm_mm = sem("norm_mm")
        z_t, q_out, ks_mm, ks_out, n_inv = sem("z_t"), sem("q_out"), sem("ks_mm"), sem("ks_out"), sem("n_inv")
        top_done, cand_done, cand_exp, w_raw, w_norm = (sem("top_done"), sem("cand_done"), sem("cand_exp"),
                                                        sem("w_raw"), sem("w_norm"))
        cell_t, cell_out, slots_mm, pq_ready, e_picked, q_hot, pq_mm, peer_x, up_mm = (
            sem("cell_t"), sem("cell_out"), sem("slots_mm"), sem("pq_ready"), sem("e_picked"), sem("q_hot"), sem("pq_mm"), sem("peer_x"), sem("up_mm"))
        lg_mm, lg_shift, lg_exp, comb_ready, comb_t, comb_copied = (
            sem("lg_mm"), sem("lg_shift"), sem("lg_exp"), sem("comb_ready"), sem("comb_t"), sem("comb_copied"))
        ff_up, ff_gelu, ff_dn, ff_term, ff_acc = (sem("ff_up"), sem("ff_gelu"), sem("ff_dn"), sem("ff_term"),
                                                  sem("ff_acc"))
        out_t, out_copied = sem("out_t"), sem("out_copied")
        w1_in, w_max, w_top, w_pow, w_scales, w_scaled = (sem("w1_in"), sem("w_max"), sem("w_top"), sem("w_pow"),
                                                          sem("w_scales"), sem("w_scaled"))
        split_high, split_low = sem("split_high"), sem("split_low")
        split_out = [sem(f"split_out{r}") for r in range(4)]
        x_split = sem("x_split")

        out_v = out.rearrange("(g b) l d -> g (b l) d", b=GB)
        x_v = a["x"].rearrange("(g b) t c -> g b (t c)", b=GB)

        def col(name, i=0):
            return cols[:, COL[name] + i:COL[name] + i + 1]

        def hcol(name, i=0):
            return hcols[:, COL[name] + i:COL[name] + i + 1]

        def of_group(v, gi):
            if isinstance(gi, int):
                return v[gi]
            return v[bass.ds(gi, 1)].rearrange("o a b -> (o a) b")

        def heads(t, n):
            return t[0:n, :].rearrange("p (h k) -> p h k", h=H)

        def spread(t, n, h, k):
            return t[0:n, 0:h].unsqueeze(2).broadcast_to([n, h, k])

        KEY_BANKS = (B1, B0), (B2, B3)
        LN_IN, LN_BACK = (B1, B3), (B1, B2)

        N_CONST, N_WTS = [0], [0]

        block = ctx.enter_context(nc.Block())

        @block.sync
        def _(sp):
            def load_x(gi):
                src = of_group(x_v, gi)
                sp.dma_start(xin[:, :, :, :].rearrange("p b s k -> p b (s k)"),
                             src[:, 0:XR * 256].rearrange("b (p k) -> p b k", k=256)).then_inc(x_in, 16)

            def const(dst, src):
                N_CONST[0] += 16
                sp.dma_start(dst, src).then_inc(const_in, 16)

            def wts(dst, src):
                N_WTS[0] += 16
                sp.dma_start(dst, src).then_inc(wts_in, 16)

            sp.sem_inc(out_done, 16)
            load_x(0)
            const(ident[:, :], a["c_ident"])
            for name, src in (("tok_b", "L0_tok_b"), ("tb", "L0_attn_tb"), ("cb", "L0_attn_cb"),
                              ("aw", "L0_attn_aW"), ("frb", "L0_attn_frb"), ("ffb", "L0_attn_ffb"),
                              ("bq", "L1_attn_bq"), ("bk", "L1_attn_bk"), ("bv", "L1_attn_bv")):
                v = a[src]
                v = v.rearrange("(o d) -> o d", d=128) if len(v.shape) == 1 else v
                const(rows[COL[name]:COL[name] + v.shape[0], :], v)
            for name, src in (("lng", "L0_ffn_ln_g"), ("lnb", "L0_ffn_ln_b")):
                for i in range(2):
                    const(rows[COL[name]:COL[name] + 1, 64 * i:64 * i + 64],
                          a[src].rearrange("(o d) -> o d", o=1))
            const(rows[0:E * FC, :], a["L1_ffn_re_b1"].rearrange("e (c f) -> (e c) f", f=128))
            const(rows[E * FC:NE * FC, :], a["L1_ffn_se_b1"].rearrange("e (c f) -> (e c) f", f=128))
            const(rows[COL["b2"]:COL["b2"] + E, :], a["L1_ffn_re_b2"])
            const(rows[COL["b2"] + E:COL["b2"] + NE, :], a["L1_ffn_se_b2"])
            const(ab[:, :], a["L0_attn_ab"].rearrange("(o d) -> o d", o=1))
            const(act_raw[:, 0:4, :], a["L0_tok_W"].rearrange("d (j k) -> d j k", k=128))
            const(act_raw[:, 4:8, :], a["L0_ffn_Wq"].rearrange("(j r) d -> r j d", r=128))
            wts(tw[:, :, :], a["L0_attn_tW"].rearrange("i d n -> d i n"))
            wts(cw[:, :, :], a["L0_attn_cW"].rearrange("i d n -> d i n"))
            wts(ffw[:, :, :], a["L0_attn_ffW"].rearrange("(i d) n -> d i n", d=128))
            wts(frw[:, :, :], a["L0_attn_frW"].rearrange("(i d) n -> d i n", d=128))
            for i in range(4):
                wts(keys[:, i, :], a[f"L0_ffn_keys{i % 2}"])
            wts(bqc[:, :], a["L0_ffn_bq"].rearrange("(o n) -> o n", o=1).broadcast_to([128, 512]))
            wts(posT[:, :], a["c_posT"])
            wts(blockmask[:, :], a["c_blockmask"])
            wts(halfones[:, :], a["c_halfones"])
            wts(merge[:, :, :], a["c_merge"])
            for i, name in enumerate(("L1_attn_Wq", "L1_attn_Wk", "L1_attn_Wv")):
                wts(act_raw[:, 8 + i, :], a[name])
            wts(act_raw[0:E, 11, :], a["L1_ffn_gate_w"])
            for dst, name in ((dnraw, "L0_ffn_expert_down"), (upR, "L0_ffn_expert_up")):
                v = a[name][0:128, :].rearrange("(p q) d -> p (q d)", q=Q8)
                for p in range(P16):
                    sp.dma_start(dst[8 * p:8 * p + 8, :, :].rearrange("t q d -> t (q d)"),
                                 v[p:p + 1, :].broadcast_to([8, Q8 * 128])).then_inc(peer_in, 16)
            for e0 in range(0, E, 4):
                sp.dma_start(w1[:, e0:e0 + 4, :], a["L1_ffn_re_w1"][e0:e0 + 4].rearrange("e d f -> d e f")).then_inc(w1_in, 16)
            sp.dma_start(w1[:, E:NE, :], a["L1_ffn_se_w1"].rearrange("e d f -> d e f")).then_inc(w1_in, 16)
            for e0 in range(0, E, 4):
                sp.dma_start(w2[:, e0:e0 + 4, :, :].rearrange("p e c d -> p (e c) d"),
                             a["L1_ffn_re_w2"][e0:e0 + 4].rearrange("e (c p) d -> p (e c) d", p=128)).then_inc(exp_in, 16)
            sp.dma_start(w2[:, E:NE, :, :].rearrange("p e c d -> p (e c) d"),
                         a["L1_ffn_se_w2"].rearrange("e (c p) d -> p (e c) d", p=128)).then_inc(exp_in, 16)

            def next_x(gi):
                sp.wait_ge(xt_done, 2 * gi)
                load_x(gi)

            def store(m):
                sp.wait_ge(out_copied, m + 2)
                dst = of_group(out_v, m)
                for s, (o, n) in enumerate(SUBS):
                    sp.dma_start(dst[o:o + n, :], otile[0:n, s, :]).then_inc(out_done, 16)

            def gates(m):
                sp.wait_ge(comb_copied, m + 1)
                mem = of_group(comb_dram, m)
                sp.dma_start(mem, combT[:, :]).then_inc(comb_out, 16)
                sp.wait_ge(comb_out, 16 * m + 16)
                for r in range(E // CB):
                    sp.wait_ge(ff_term, NE * m + 2 + (SH + CB * (r - 1) if r > 1 else 0))
                    sp.dma_start(combB[:, r % 2, :, :].rearrange("p e n -> p (e n)"),
                                 mem[CB * r:CB * r + CB, :].rearrange("(o e) n -> o (e n)", o=1).broadcast_to([128, CB * N])
                                 ).then_inc(comb_in[r % 2], 16)

            next_x(1)
            for e in range(NE):
                sp.wait_ge(split_low, e + 1)
                sp.dma_start(w1h[:, e, :, :].rearrange("p h f -> p (h f)"),
                             halves[:, e % 4, :, :].rearrange("p h f -> p (h f)")).then_inc(split_out[e % 4], 16)
            next_x(2)
            gates(0)
            with sp.Fori(1, G - 2) as g:
                next_x(g + 2)
                store(g - 1)
                gates(g)
            store(G - 3)
            gates(G - 2)
            store(G - 2)
            gates(G - 1)
            store(G - 1)
            sp.wait_ge(out_done, 16 * NSUB * G + 16)

        @block.tensor
        def _(pe):
            def mm(o, lhsT, rhs, start=True, stop=True):
                return pe.matmul(o, lhsT, rhs, start=start, stop=stop)

            def tr(o, src):
                n = src.shape[0]
                return pe.transpose(o, src, ident[0:n, 0:n])

            pe.wait_ge(const_in, N_CONST[0])
            tr(B0[:, 0:NROWS], rows[:, :]).then_inc(setup_pe, 1)
            for j in range(4):
                ins = tr(B1[:, 128 * j:128 * j + 128], act_raw[:, j, :])
            ins.then_inc(setup_pe, 1)
            for j in range(4):
                ins = tr(B2[:, 128 * j:128 * j + 128], act_raw[:, 4 + j, :])
            ins.then_inc(setup_pe, 1)
            pe.wait_ge(setup_a, 2)

            def setup_rest():
                for j in range(3):
                    tr(B3[:, 128 * j:128 * j + 128], act_raw[:, 8 + j, :])
                tr(B3[:, 384:384 + E], act_raw[0:E, 11, :]).then_inc(setup_pe, 1)
                pe.wait_ge(setup_p, 3)
                tr(UP[0][:, 0:PK], keys2[:, :, :].rearrange("p c k -> p (c k)")).then_inc(setup_pe, 1)
                pe.wait_ge(peer_in, 16 * 2 * P16)
                for q in range(Q8):
                    ins = tr(DN[q // 4][:, 128 * (q % 4):128 * (q % 4) + 128], dnraw[:, q, :])
                ins.then_inc(setup_pe, 1)
                pe.wait_ge(setup_a, 4)
                pe.wait_ge(setup_v, 3)

            def group(gi, peer, nxt, moe):
                m, gj = gi - 1, gi + 1
                done = [HEAD]

                def first_product(m, step):
                    e, f = step // FC, step % FC
                    pe.wait_ge(ff_gelu, NE * FC * m + step + 1)
                    for wh, xh in ((0, 0), (0, 1), (1, 0)):
                        ins = mm(UP[f % 2][:, 0:N], w1h[:, EORD[e], wh, 128 * f:128 * f + 128], xd16[:, xh, :],
                                 start=(wh == 0 and xh == 0), stop=(wh == 1))
                    ins.then_inc(ff_up, 1)

                def moe_to(upto):
                    if not moe:
                        return
                    for step in range(done[0], upto):
                        e, f = step // FC, step % FC
                        if e < NE:
                            first_product(m, step)
                        if e > 0:
                            x = NE * m + e
                            if f == 0:
                                pe.wait_ge(ff_term, x)
                                if e == 2:
                                    pe.wait_ge(comb_copied, m + 1)
                                if e == 1:
                                    pe.wait_ge(out_copied, m + 1)
                            pe.wait_ge(ff_gelu, (x - 1) * FC + f + 3)
                            ins = mm(DN[(e - 1) % 2][:, 0:N], w2[:, EORD[e - 1], f, :], hid[:, (e - 1) % 2, f, :],
                                     start=(f == 0), stop=(f == FC - 1))
                            if f == FC - 1:
                                ins.then_inc(ff_dn, 1)
                    done[0] = max(upto, done[0])

                def gs(st):
                    return (gj, gi)[st]

                def tile(s, ahead):
                    return 3 * (gj if s < ahead else gi) + s + 1

                def ln_in(st, i):
                    pe.wait_ge(h_ready[st], 2 * gs(st) + i + 1)
                    h = (hAT, hT)[st]
                    for s, (o, n) in enumerate(SUBS):
                        ins = tr(LN_IN[st][0:n, 128 * s:128 * s + 128], h[:, o:o + n])
                    ins.then_inc(ln_t[st], 1)

                def ln_back(st, i):
                    pe.wait_ge(ln_xn[st], 2 * gs(st) + i + 1)
                    for s, (o, n) in enumerate(SUBS):
                        ins = tr(LN_BACK[st][:, o:o + n], xn[st][0:n, s, :])
                    ins.then_inc(ln_b[st], 1)

                def turn_probs(st):
                    pe.wait_ge(v_out[st], gs(st) + 1)
                    pe.wait_ge(prob_ready[st], gs(st) + 1)
                    for b in range(GB):
                        ins = tr((B1, B3)[st][0:L, L * b:L * b + L], prob[st][:, L * b:L * b + L])
                    ins.then_inc(pt_mm[st], 1)

                def probs_times_values(st):
                    pe.wait_ge(pt_out[st], gs(st) + 1)
                    for b in range(GB):
                        ins = mm((B1, B2)[st][:, L * b:L * b + L], vtok[st][:, b, :], probT[st][:, L * b:L * b + L])
                    ins.then_inc(att_mm[st], 1)

                def queries(s):
                    o, n = SUBS[s]
                    k = tile(s, 2)
                    if s > 0:
                        pe.wait_ge(ks_out, 2 * (k - 1) - (s > 1))
                    mm(B0[0:n, :], hnT[:, o:o + n], wqcT[:, :]).then_inc(q_mm, 1)

                def turn_queries(s):
                    n = SUBS[s][1]
                    pe.wait_ge(q_z, tile(s, 1))
                    for c in range(HP):
                        ins = tr(B1[:, 128 * c:128 * c + n], qc[0:n, 128 * c:128 * c + 128])
                    ins.then_inc(z_t, 1)

                def key_scores(s):
                    n = SUBS[s][1]
                    k = tile(s, 1)
                    pe.wait_ge(q_out, k)
                    if s == 1 and moe:
                        pe.wait_ge(lg_shift, 2 * gi - 1)
                    elif s == 2:
                        pe.wait_ge(peer_x, 3 * gi + 1)
                    for c in range(HP):
                        ins = mm(B0[0:n, 4 * c:4 * c + 4], sqT[:, c, 0:n], halfones[:, :])
                    ins.then_inc(norm_mm, 1)
                    for c in range(HP):
                        if s == 0 and c == HP // 2:
                            pe.wait_ge(ks_out, 2 * k - 1)
                        b = KEY_BANKS[s > 0][c // 2]
                        ins = mm(b[0:n, 256 * (c % 2):256 * (c % 2) + 256], qnT[:, c, 0:n], keysBD[:, :])
                    ins.then_inc(ks_mm, 1)

                def turn_cells(s):
                    n = SUBS[s][1]
                    k = 3 * gi + s + 1
                    pe.wait_ge(w_norm, k)
                    pe.wait_ge(e_picked, k)
                    if nxt:
                        if s == 0:
                            pe.wait_ge(ln_out[A], 2 * gj + 1)
                        elif s == 1:
                            pe.wait_ge(v_out[A], gj + 1)
                        else:
                            pe.wait_ge(gate_act, 2 * gj + 1)
                    if s == 0:
                        pe.wait_ge(q_biased, k + 2)
                        pe.wait_ge(q_out, k + 2)
                    elif s == 1:
                        pe.wait_ge(ks_out, 2 * (k + 1))
                    for c in range(HP):
                        tr(B0[0:NK, n * c:n * c + n], cw_[0:n, 2 * c:2 * c + 2, :].rearrange("p h k -> p (h k)"))
                        ins = tr(B1[0:NK, n * c:n * c + n],
                                 epick[0:n, 2 * c:2 * c + 2, :].rearrange("p h k -> p (h k)"))
                    ins.then_inc(cell_t, 1)

                def slots(s):
                    n = SUBS[s][1]
                    pe.wait_ge(cell_out, 3 * gi + s + 1)
                    for i in range(2):
                        for c in range(2):
                            mm(B0[0:NS, i * n:i * n + n], merge[:, c, :], wcell[:, (2 * i + c) * n:(2 * i + c + 1) * n],
                               start=(c == 0), stop=(c == 1))
                        for c in range(2):
                            ins = mm(B0[0:NS, (2 + i) * n:(3 + i) * n], merge16[:, c, :],
                                     ecell[:, (2 * i + c) * n:(2 * i + c + 1) * n], start=(c == 0), stop=(c == 1))
                    ins.then_inc(slots_mm, 1)

                def sums(s):
                    n = SUBS[s][1]
                    k = 3 * gi + s + 1
                    pe.wait_ge(q_hot, k)
                    if s < 2:
                        pe.wait_ge(ks_out, 2 * (k + 1))
                    else:
                        pe.wait_ge(peer_x, k - 1)
                    for t in range(n // 8):
                        for c in range(2):
                            x = n * c + 8 * t
                            for part in range(2):
                                ins = mm((B2, B3)[t // 8][:, 64 * (t % 8):64 * (t % 8) + 64],
                                         ph[:, x // 8, :, :].rearrange("p k t -> p (k t)"),
                                         qw[:, part, :, x:x + 8], start=(c == 0 and part == 0),
                                         stop=(c == 1 and part == 1))
                    ins.then_inc(pq_mm, 1)

                def expert_inputs(q0, q1):
                    for q in range(q0, q1):
                        if q >= 2:
                            pe.wait_ge(in_act, Q8 * gj + q - 1)
                        mm((B1, B0)[q % 2][:, 0:N], dnT[:, q, :], hnT[:, :]).then_inc(in_mm, 1)

                def patch_pieces(i):
                    if i == 0:
                        pe.wait_ge(x_in, 16 * gj + 16)
                    else:
                        pe.wait_ge(xt_copied, 2 * gj + 1)
                    for b in range(GB):
                        ins = tr(B1[:, XR * b:XR * b + XR], xin[:, b, i, :])
                    ins.then_inc(xt_done, 1)

                def patch_product():
                    pe.wait_ge(xt_copied, 2 * gj + 2)
                    for j in range(4):
                        v = xT[:, j % 2, :].rearrange("p (b r) -> p b r", r=XR)[:, :, j // 2:j // 2 + L]
                        ins = mm(B1[:, 0:N], wtokT[:, j, :], v, start=(j == 0), stop=(j == 3))
                    ins.then_inc(tok_mm, 1)

                def gated(i, part):
                    if part == 1:
                        pe.wait_ge(hw_act, 4 * gj + 2 * i + 1)
                    elif i == 0:
                        pe.wait_ge(ln_out[A], 2 * gj + 1)
                    else:
                        pe.wait_ge(hw_x, 2 * gj + 1)
                    mm(B1[:, 0:N], (tw, cw)[part][:, i, :], (inA, x1T)[i][:, :]).then_inc(hw_mm, 1)

                def first_scores():
                    pe.wait_ge(u_ready, gj + 1)
                    pe.wait_ge(v_out[A], gj + 1)
                    for b in range(GB):
                        t = slice(L * b, L * b + L)
                        mm(B1[0:L, t], uT[:, t], x2T[:, t], stop=False)
                        ins = mm(B1[0:L, t], s1row[0:1, t], ones[0:1, 0:L], start=False)
                    ins.then_inc(sc_mm[A], 1)

                def gate(i):
                    if i == 0:
                        pe.wait_ge(att_out, gj + 1)
                    else:
                        pe.wait_ge(gate_act, 2 * gj + 1)
                    w = (ffw, frw)[i]
                    mm(B1[:, 0:N], w[:, 0, :], inA[:, :], stop=False)
                    mm(B1[:, 0:N], w[:, 1, :], attT[:, :], start=False).then_inc(gate_mm, 1)

                if peer and not moe:
                    pe.wait_ge(w_max, 1)
                    tr(UP[0][0:NE, 0:128], wmax[:, :]).then_inc(w_top, 1)
                    pe.wait_ge(w_pow, 2)
                    mm(UP[1][:, 0:2 * NE], onesE[:, :],
                       wdiag[:, :, :].rearrange("p i e -> p (i e)")).then_inc(w_scales, 1)
                if nxt:
                    if peer:
                        pe.wait_ge(in_act, Q8 * gi + Q8)
                    patch_pieces(0)
                moe_to(AT["a2"])
                if nxt:
                    patch_pieces(1)
                moe_to(AT["z1"])
                if peer:
                    if nxt:
                        pe.wait_ge(xt_copied, 2 * gj + 2)
                    else:
                        pe.wait_ge(in_act, Q8 * gi + Q8)
                    turn_queries(1)
                moe_to(AT["k1"])
                if peer:
                    key_scores(1)
                    queries(2)
                moe_to(AT["a3"])
                if nxt:
                    patch_product()
                moe_to(AT["cb"])
                if moe:
                    pe.wait_ge(comb_ready, gi)
                    for s, (o, n) in enumerate(SUBS):
                        ins = tr(DN[1][0:E, o:o + n], comb[0:n, s, :])
                    ins.then_inc(comb_t, 1)
                moe_to(AT["c0"])
                if nxt:
                    ln_in(A, 0)
                moe_to(AT["a5"])
                if nxt:
                    ln_back(A, 0)
                moe_to(AT["z2"])
                if peer:
                    if nxt:
                        pe.wait_ge(ln_out[A], 2 * gj + 1)
                    turn_queries(2)
                moe_to(AT["t0"])
                if peer:
                    turn_cells(0)
                    moe_to(AT["t0"] + 1)
                    slots(0)
                if nxt:
                    if not peer:
                        pe.wait_ge(wts_in, N_WTS[0])
                    gated(0, 0)
                moe_to(AT["a7"])
                if nxt:
                    gated(0, 1)
                moe_to(AT["u0"])
                if peer:
                    sums(0)
                if nxt:
                    gated(1, 0)
                moe_to(AT["a9"])
                if nxt:
                    gated(1, 1)
                moe_to(AT["k2"])
                if peer:
                    key_scores(2)
                moe_to(AT["a10"])
                if nxt:
                    pe.wait_ge(hw_x, 2 * gj + 2)
                    mm(B1[0:1, 0:N], col("aw", 0), x2T[:, :]).then_inc(s1_mm, 1)
                moe_to(AT["a11"])
                if nxt:
                    pe.wait_ge(s1_row, gj + 1)
                    for b in range(GB):
                        ins = tr(B1[0:L, 128 * b:128 * b + 128], x2T[:, L * b:L * b + L])
                    ins.then_inc(v_mm[A], 1)
                moe_to(AT["t1"])
                if peer:
                    turn_cells(1)
                    moe_to(AT["t1"] + 1)
                    slots(1)
                moe_to(AT["a12"])
                if nxt:
                    first_scores()
                moe_to(AT["u1"])
                if peer:
                    sums(1)
                moe_to(AT["a13"])
                if nxt:
                    turn_probs(A)
                moe_to(AT["a14"])
                if nxt:
                    probs_times_values(A)
                moe_to(AT["a15"])
                if nxt:
                    gate(0)
                moe_to(AT["t2"])
                if peer:
                    turn_cells(2)
                    moe_to(AT["t2"] + 1)
                    slots(2)
                moe_to(AT["a16"])
                if nxt:
                    gate(1)
                moe_to(AT["u2"])
                if peer:
                    sums(2)
                moe_to(AT["a17"])
                if nxt:
                    ln_in(A, 1)
                moe_to(AT["up"])
                if peer:
                    pe.wait_ge(peer_x, 3 * gi + 3)
                    for q in range(Q8):
                        ins = mm(B2[:, 0:N], upR[:, q, :], act[:, q, :], start=(q == 0), stop=(q == Q8 - 1))
                    ins.then_inc(up_mm, 1)
                moe_to(AT["a18"])
                if nxt:
                    ln_back(A, 1)
                if peer:
                    ln_in(B, 0)
                moe_to(AT["ln0"])
                if nxt:
                    if not peer:
                        setup_rest()
                    pe.wait_ge(ln_out[A], 2 * gj + 2)
                    queries(0)
                moe_to(AT["back0"])
                if peer:
                    ln_back(B, 0)
                moe_to(AT["zq"])
                if nxt:
                    turn_queries(0)
                moe_to(AT["qk"])
                if peer:
                    pe.wait_ge(ln_out[B], 2 * gi + 1)
                    mm(B3[:, 0:N], wqkvT[:, 0, :], inT[:, :]).then_inc(qk_mm, 1)
                    mm(B2[:, 0:N], wqkvT[:, 1, :], inT[:, :]).then_inc(qk_mm, 1)
                moe_to(AT["kq"])
                if nxt:
                    key_scores(0)
                moe_to(AT["v"])
                if peer:
                    pe.wait_ge(qk_out, 2 * gi + 1)
                    for b in range(GB):
                        ins = mm(B3[0:L, 128 * b:128 * b + 128], inT[:, L * b:L * b + L], wqkvT[:, 2, :])
                    ins.then_inc(v_mm[B], 1)
                    pe.wait_ge(qk_out, 2 * gi + 2)
                    for b in range(GB):
                        t = slice(L * b, L * b + L)
                        ins = mm(B2[0:L, t], qT[:, t], kT[:, t])
                    ins.then_inc(sc_mm[B], 1)
                if nxt:
                    queries(1)
                moe_to(AT["i0"])
                if nxt:
                    expert_inputs(0, 1)
                    pe.wait_ge(q_biased, 3 * gj + 2)
                    expert_inputs(1, 4)
                moe_to(AT["pt"])
                if peer:
                    turn_probs(B)
                    moe_to(AT["pt"] + 1)
                    probs_times_values(B)
                moe_to(AT["lnB1"])
                if peer:
                    ln_in(B, 1)
                moe_to(AT["i1"])
                if nxt:
                    expert_inputs(4, 6)
                moe_to(STEPS)
                if moe:
                    pe.wait_ge(ff_acc, (NE + 1) * gi)
                    for s, (o, n) in enumerate(SUBS):
                        ins = tr(DN[0][0:n, 128 * s:128 * s + 128], acc[:, o:o + n])
                    ins.then_inc(out_t, 1)
                if peer:
                    ln_back(B, 1)
                    pe.wait_ge(ln_out[B], 2 * gi + 2)
                    for s, (o, n) in enumerate(SUBS):
                        ins = mm(B3[0:n, E * s:E * s + E], xd[:, o:o + n], gateT[:, :])
                    ins.then_inc(lg_mm, 1)
                if nxt:
                    expert_inputs(6, 8)
                if peer:
                    if not moe:
                        pe.wait_ge(exp_in, 80)
                        for r in range(4):
                            pe.wait_ge(split_out[r], 16 * ((NE - r + 3) // 4))
                    pe.wait_ge(x_split, gi + 1)
                    for step in range(HEAD):
                        first_product(gi, step)
            group(-1, False, True, False)
            group(0, True, True, False)
            with pe.Fori(1, G - 1) as g:
                group(g, True, True, True)
            group(G - 1, True, False, True)
            group(G, False, False, True)

        @block.gpsimd
        def _(pool):
            pool.memset(ones[:, :], 1.0)
            pool.memset(onesE[:, :], 1.0)
            pool.memset(nhalf[:, :], -0.5)
            pool.memset(keysBD[:, :], 0.0)
            for i in range(2):
                pool.memset(mv[i][:, :, :], 1.0)
            pool.memset(lg[:, :, :], -1.0)
            pool.memset(m8[:, :, :], -1.0)
            pool.memset(lg2[:, :, :], TAKEN)
            pool.memset(ge[:, :, :], 0.0)
            pool.memset(t8[:, :, :], -1.0).then_inc(setup_p, 1)
            pool.wait_ge(setup_p, 1)
            pool.wait_ge(setup_v, 1)
            pool.tensor_tensor(kn[:, :], kn[:, :], nhalf[0:PK, 0:2], ALU.pow).then_inc(setup_p, 1)
            pool.wait_ge(setup_p, 2)
            for i in range(2):
                ins = pool.tensor_tensor(keys2[:, 2 * i:2 * i + 2, :], keys[:, 2 * i:2 * i + 2, :],
                                         spread(kn, PK, 2, HALF), ALU.mult)
            ins.then_inc(setup_p, 1)

            def group(gi, peer, nxt, moe):
                m, gj = gi - 1, gi + 1
                links, added = [0, 0], [0]

                def gs(st):
                    return (gj, gi)[st]

                def tile(s, ahead):
                    return 3 * (gj if s < ahead else gi) + s + 1

                def link(st, ins):
                    links[st] += 1
                    ins.then_inc(p_link[st], 1)
                    pool.wait_ge(p_link[st], gs(st) * P_LINKS[st] + links[st])

                def own_wait():
                    pool.sem_inc(p_met, 1)

                def moe_to(upto):
                    if not moe:
                        return
                    for e in range(added[0], upto // FC - 1):
                        pool.wait_ge(ff_term, NE * m + e + 3)
                        pool.wait_ge(ff_acc, (NE + 1) * m + e + 1)
                        pool.tensor_tensor(acc[:, :], acc[:, :], term[:, e % 2, :], ALU.add).then_inc(ff_acc, 1)
                        added[0] = e + 1

                def ln(st, i):
                    pool.wait_ge(ln_mv[st], 2 * gs(st) + i + 1)
                    own_wait()
                    link(st, pool.tensor_scalar(rstd[st][:, :], mv[st][:, :, 1], EPS, None, ALU.add))
                    pool.tensor_tensor(rstd[st][:, :], rstd[st][:, :], nhalf[:, 0:NSUB], ALU.pow).then_inc(ln_rstd[st], 1)

                def attention(st):
                    pool.wait_ge(sc_rec[st], gs(st) + 1)
                    v = prob[st][:, :].rearrange("p (b j) -> p b j", j=L)
                    pool.tensor_tensor(v, v, spread(arec[st], L, GB, L), ALU.mult).then_inc(prob_ready[st], 1)

                def mask_inputs(g, q0, q1):
                    pool.wait_ge(in_act, Q8 * g + q1)
                    v = act[:, q0:q1, :].rearrange("p q (g t) -> p (q g) t", t=8)
                    pool.tensor_tensor(v, v, blockmask[:, :].unsqueeze(1).broadcast_to([128, (q1 - q0) * N // 8, 8]),
                                       ALU.mult).then_inc(act_masked, 1)

                def query_norm(s):
                    n = SUBS[s][1]
                    pool.wait_ge(q_var, tile(s, 2))
                    own_wait()
                    link(A if s < 2 else B, pool.tensor_scalar(qr[0:n, :], qv[0:n, :], 1.0 / QD, EPS, ALU.mult, ALU.add))
                    pool.tensor_tensor(qr[0:n, :], qr[0:n, :], nhalf[0:n, 0:H], ALU.pow).then_inc(q_rstd, 1)

                def half_norms(s):
                    n = SUBS[s][1]
                    pool.wait_ge(ks_out, 2 * tile(s, 1) - 1)
                    own_wait()
                    link(A if s < 1 else B, pool.tensor_scalar(inv[0:n, s % 2, :], nrm[0:n, :], 1e-24, None, ALU.max))
                    pool.tensor_tensor(inv[0:n, s % 2, :], inv[0:n, s % 2, :], nhalf[0:n, :], ALU.pow).then_inc(n_inv, 1)

                def cells(s):
                    n = SUBS[s][1]
                    pool.wait_ge(top_done, 3 * gi + s + 1)
                    for src, dst in ((topn, cand[0:n]), (idf, cexpert[0:n, s % 2])):
                        v = src[0:n, :, :].rearrange("p (h t) k -> p h t k", t=2)
                        o = 0
                        for r, k, w in CELLS:
                            d = dst[:, :, o:o + k * w].rearrange("p h (m w) -> p h m w", w=w)
                            ins = pool.tensor_tensor(
                                d, v[:, :, 0, r:r + k].unsqueeze(3).broadcast_to([n, H, k, w]),
                                v[:, :, 1, 0:w].unsqueeze(2).broadcast_to([n, H, k, w]), ALU.add)
                            o += k * w
                        ins.then_inc(cand_done, 1)

                def weights(s):
                    n = SUBS[s][1]
                    pool.wait_ge(w_raw, 3 * gi + s + 1)
                    pool.tensor_tensor(cw_[0:n, :, :], cw_[0:n, :, :], spread(zr, n, H, NC), ALU.mult).then_inc(w_norm, 1)

                if peer:
                    cells(0)
                    mask_inputs(gi, 4, 8)
                moe_to(AT["z1"])
                if peer:
                    weights(0)
                    half_norms(1)
                    query_norm(2)
                moe_to(AT["c0"])
                if nxt:
                    ln(A, 0)
                moe_to(AT["u0"])
                if peer:
                    half_norms(2)
                    cells(1)
                moe_to(AT["c1"])
                if peer:
                    weights(1)
                moe_to(AT["u1"])
                if nxt:
                    attention(A)
                if peer:
                    cells(2)
                    weights(2)
                moe_to(AT["u2"])
                if nxt:
                    ln(A, 1)
                moe_to(AT["up"])
                if peer:
                    ln(B, 0)
                if nxt:
                    query_norm(0)
                moe_to(AT["qk"])
                if nxt:
                    half_norms(0)
                    query_norm(1)
                if peer:
                    attention(B)
                moe_to(AT["pt"])
                if nxt:
                    mask_inputs(gj, 0, 4)
                moe_to(AT["lnB1"])
                if peer:
                    ln(B, 1)
                moe_to(STEPS)
                if peer:
                    pool.wait_ge(h_ready[B], 2 * gi + 2)
                    if moe:
                        pool.wait_ge(out_t, gi)
                    own_wait()
                    pool.tensor_copy(acc[:, :], hT[:, :]).then_inc(ff_acc, 1)
                assert links == [nxt * P_LINKS[A], peer * P_LINKS[B]], f"P_LINKS {links}"

            group(-1, False, True, False)
            group(0, True, True, False)
            with pool.Fori(1, G - 1) as g:
                group(g, True, True, True)
            group(G - 1, True, False, True)
            group(G, False, False, True)

        @block.scalar
        def _(ae):
            ae.sem_inc(ff_gelu, 2)
            ae.sem_inc(out_copied, 1)
            ae.wait_ge(setup_pe, 1)
            ae.copy(cols[:, :], B0[:, 0:NROWS])
            ae.mul(hcols[:, :], B0[:, 0:NROWS], 0.5).then_inc(setup_a, 1)
            ae.wait_ge(setup_pe, 2)
            ae.copy(wtokT[:, :, :].rearrange("p j d -> p (j d)"), B1[:, :]).then_inc(setup_a, 1)
            ae.wait_ge(setup_a, 2)

            halved = [0]

            def group(gi, peer, nxt, moe):
                m, gj = gi - 1, gi + 1
                done = [HEAD]

                def split(upto):
                    for e in range(halved[0], min(upto, NE)):
                        if e == 0:
                            ae.wait_ge(w_scales, 1)
                            ae.copy(wscale[:, :, :].rearrange("p i e -> p (i e)"), UP[1][:, 0:2 * NE]).then_inc(w_scaled, 1)
                            ae.wait_ge(w_scaled, 1)
                        if e >= 4:
                            ae.wait_ge(split_out[e % 4], 16 * (e // 4))
                        ae.activation(halves[:, e % 4, 0, :], w1[:, e, :], ACT.Copy,
                                      scale=wscale[:, 0, e:e + 1]).then_inc(split_high, 1)
                        halved[0] = e + 1

                def gelu(m, step):
                    e, f = step // FC, step % FC
                    ae.wait_ge(ff_up, NE * FC * m + step + 1)
                    if f == 0:
                        ae.wait_ge(ff_dn, NE * m + e + 1)
                    ae.activation(hid[:, e % 2, f, :], UP[f % 2][:, 0:N], ACT.Gelu,
                                  bias=col("b1", EORD[e] * FC + f),
                                  scale=wscale[:, 1, EORD[e]:EORD[e] + 1]).then_inc(ff_gelu, 1)

                def moe_to(upto):
                    if peer and not moe:
                        split(upto // FC)
                    if not moe:
                        return
                    for step in range(done[0], min(upto, NE * FC)):
                        gelu(m, step)
                    done[0] = max(upto, done[0])

                def gs(st):
                    return (gj, gi)[st]

                def tile(s, ahead):
                    return 3 * (gj if s < ahead else gi) + s + 1

                def tanh_half(dst, src, name, i=0):
                    return ae.activation(dst, src, ACT.Tanh, bias=hcol(name, i), scale=0.5)

                def exps(st):
                    ae.wait_ge(sc_shift[st], gs(st) + 1)
                    ae.activation(prob[st][:, :], prob[st][:, :], ACT.Exp).then_inc(sc_exp[st], 1)

                def prob_turned(st):
                    ae.wait_ge(pt_mm[st], gs(st) + 1)
                    ae.copy(probT[st][:, :], (B1, B3)[st][0:L, 0:N]).then_inc(pt_out[st], 1)

                def values(st):
                    ae.wait_ge(v_mm[st], gs(st) + 1)
                    ae.copy(vtok[st][:, :, :].rearrange("p b d -> p (b d)"), (B1, B3)[st][0:L, :]).then_inc(v_out[st], 1)

                def normed(st, i, dst):
                    ae.wait_ge(ln_b[st], 2 * gs(st) + i + 1)
                    ae.copy(dst[:, :], LN_BACK[st][:, 0:N]).then_inc(ln_out[st], 1)

                def query_squares(s):
                    n = SUBS[s][1]
                    ae.wait_ge(q_biased, tile(s, 2))
                    ae.activation(sq[0:n, :], qc[0:n, :], ACT.Square).then_inc(q_sq, 1)

                def turned_queries(s):
                    n = SUBS[s][1]
                    ae.wait_ge(z_t, tile(s, 1))
                    v = B1[:, :].rearrange("p (c n) -> p c n", n=128)[:, :, 0:n]
                    ae.activation(qnT[:, :, 0:n], v, ACT.Identity, bias=col("lnb"), scale=col("lng"))
                    ae.activation(sqT[:, :, 0:n], v, ACT.Square, bias=col("lnb"), scale=col("lng")).then_inc(q_out, 1)

                def norms(s):
                    n = SUBS[s][1]
                    k = tile(s, 1)
                    ae.wait_ge(norm_mm, k)
                    if s > 0 or peer:
                        ae.wait_ge(n_inv, k - 1)
                    ae.copy(nrm[0:n, :], B0[0:n, 0:2 * H]).then_inc(ks_out, 1)

                def scores(s):
                    n = SUBS[s][1]
                    k = tile(s, 1)
                    ae.wait_ge(ks_mm, k)
                    if s > 0 or peer:
                        ae.wait_ge(top_done, k - 1)
                    b = KEY_BANKS[s > 0]
                    ae.copy(sc[0:n, 0:H, :].rearrange("p c k -> p (c k)"), b[0][0:n, :])
                    ae.copy(sc[0:n, H:2 * H, :].rearrange("p c k -> p (c k)"), b[1][0:n, :]).then_inc(ks_out, 1)

                def cells_turned(s):
                    n = SUBS[s][1]
                    ae.wait_ge(cell_t, 3 * gi + s + 1)
                    ae.copy(wcell[:, 0:4 * n], B0[0:NK, 0:4 * n])
                    ae.copy(ecell[:, 0:4 * n], B1[0:NK, 0:4 * n]).then_inc(cell_out, 1)

                def cell_exps(s):
                    n = SUBS[s][1]
                    ae.wait_ge(cand_done, 2 * (3 * gi + s) + 1)
                    ae.activation(cexp[0:n, :, :], cand[0:n, :, :], ACT.Exp).then_inc(cand_exp, 1)

                def expert_inputs(q0, q1):
                    for q in range(q0, q1):
                        ae.wait_ge(in_mm, Q8 * gj + q + 1)
                        ae.activation(act[:, q, :], (B1, B0)[q % 2][:, 0:N], ACT.Gelu).then_inc(in_act, 1)

                def gated(i, part):
                    ae.wait_ge(hw_mm, 4 * gj + 2 * i + part + 1)
                    if part == 0:
                        ae.activation(tT[:, :], B1[:, 0:N], ACT.Relu, bias=col("tb", i)).then_inc(hw_act, 1)
                    else:
                        tanh_half(cT[:, :], B1[:, 0:N], "cb", i).then_inc(hw_act, 1)

                def gate_exps(g, i):
                    ae.wait_ge(lg_shift, 2 * g + i + 1)
                    if i == 0:
                        ae.activation(ge[:, :, :], ge[:, :, :], ACT.Exp).then_inc(lg_exp, 1)
                    else:
                        ae.activation(ge[:, :, :], ge[:, :, :], ACT.Tanh, scale=0.5).then_inc(lg_exp, 1)

                def pieces(i):
                    ae.wait_ge(xt_done, 2 * gj + i + 1)
                    ae.copy(xT[:, i, :], B1[:, 0:GB * XR]).then_inc(xt_copied, 1)

                if peer:
                    if moe:
                        ae.wait_ge(ff_acc, (NE + 1) * (gi - 1) + 1)
                    ae.wait_ge(h_ready[A], 2 * gi + 2)
                    ae.copy(hT[:, :], hAT[:, :]).then_inc(h_kept, 1)
                if nxt:
                    pieces(0)
                if moe:
                    gate_exps(m, 1)
                if peer:
                    cell_exps(0)
                moe_to(AT["a2"])
                if nxt:
                    pieces(1)
                moe_to(AT["z1"])
                if peer:
                    turned_queries(1)
                moe_to(AT["k1"])
                if peer:
                    norms(1)
                moe_to(AT["a3"])
                if nxt:
                    ae.wait_ge(tok_mm, gj + 1)
                    ae.activation(hAT[:, :], B1[:, 0:N], ACT.Identity, bias=col("tok_b")).then_inc(h_ready[A], 1)
                moe_to(AT["cb"])
                if moe:
                    ae.wait_ge(comb_t, gi)
                    ae.copy(combT[:, :], DN[1][0:E, 0:N]).then_inc(comb_copied, 1)
                moe_to(AT["s1c"])
                if peer:
                    scores(1)
                    query_squares(2)
                moe_to(AT["c0"])
                moe_to(AT["a5"])
                if nxt:
                    normed(A, 0, inA)
                moe_to(AT["z2"])
                if peer:
                    turned_queries(2)
                moe_to(AT["t0"])
                if peer:
                    cells_turned(0)
                if nxt:
                    gated(0, 0)
                moe_to(AT["a7"])
                if nxt:
                    gated(0, 1)
                moe_to(AT["u0"])
                if nxt:
                    gated(1, 0)
                moe_to(AT["a9"])
                if nxt:
                    gated(1, 1)
                moe_to(AT["k2"])
                if peer:
                    norms(2)
                moe_to(AT["s2c"])
                if peer:
                    scores(2)
                moe_to(AT["c1"])
                if peer:
                    cell_exps(1)
                moe_to(AT["a10"])
                if nxt:
                    ae.wait_ge(s1_mm, gj + 1)
                    ae.activation(s1row[:, :], B1[0:1, 0:N], ACT.Identity, bias=ab[0:1, 0:1]).then_inc(s1_row, 1)
                moe_to(AT["a11"])
                if nxt:
                    values(A)
                moe_to(AT["t1"])
                if peer:
                    cells_turned(1)
                moe_to(AT["ea"])
                if nxt:
                    exps(A)
                moe_to(AT["a13"])
                if nxt:
                    prob_turned(A)
                moe_to(AT["a14"])
                if nxt:
                    ae.wait_ge(att_mm[A], gj + 1)
                    ae.copy(attT[:, :], B1[:, 0:N]).then_inc(att_out, 1)
                moe_to(AT["c2"])
                if peer:
                    cell_exps(2)
                moe_to(AT["a15"])
                if nxt:
                    ae.wait_ge(gate_mm, 2 * gj + 1)
                    tanh_half(tT[:, :], B1[:, 0:N], "ffb").then_inc(gate_act, 1)
                moe_to(AT["t2"])
                if peer:
                    cells_turned(2)
                moe_to(AT["a16"])
                if nxt:
                    ae.wait_ge(gate_mm, 2 * gj + 2)
                    tanh_half(cT[:, :], B1[:, 0:N], "frb").then_inc(gate_act, 1)
                moe_to(AT["a18"])
                if nxt:
                    normed(A, 1, hnT)
                moe_to(AT["ln0"])
                if nxt:
                    if not peer:
                        setup_rest()
                    query_squares(0)
                moe_to(AT["zq"])
                if nxt:
                    turned_queries(0)
                moe_to(AT["qk"])
                if peer:
                    ae.wait_ge(qk_mm, 2 * gi + 1)
                    ae.activation(qT[:, :], B3[:, 0:N], ACT.Identity, bias=col("bq")).then_inc(qk_out, 1)
                    ae.wait_ge(qk_mm, 2 * gi + 2)
                    ae.activation(kT[:, :], B2[:, 0:N], ACT.Identity, bias=col("bk")).then_inc(qk_out, 1)
                moe_to(AT["kq"])
                if nxt:
                    norms(0)
                    scores(0)
                moe_to(AT["v"])
                if peer:
                    values(B)
                moe_to(AT["e1"])
                if nxt:
                    query_squares(1)
                if peer:
                    exps(B)
                moe_to(AT["i0"])
                if nxt:
                    expert_inputs(0, 4)
                moe_to(AT["pt"])
                if peer:
                    prob_turned(B)
                moe_to(AT["i1"])
                if nxt:
                    expert_inputs(4, 6)
                moe_to(STEPS)
                if moe:
                    ae.wait_ge(out_t, gi)
                    ae.wait_ge(out_done, 16 * NSUB * (gi - 1) + 16)
                    for s, (o, n) in enumerate(SUBS):
                        ins = ae.copy(otile[0:n, s, :], DN[0][0:n, 128 * s:128 * s + 128])
                    ins.then_inc(out_copied, 1)
                if peer:
                    ae.wait_ge(ln_b[B], 2 * gi + 2)
                    ae.activation(xd16[:, 0, :], LN_BACK[B][:, 0:N], ACT.Copy, scale=float(2 ** XSCALE_EXP))
                    normed(B, 1, xd)
                if nxt:
                    expert_inputs(6, 8)
                if peer:
                    for step in range(HEAD):
                        gelu(gi, step)
                    gate_exps(gi, 0)

            def setup_rest():
                ae.wait_ge(setup_pe, 4)
                ae.copy(wqkvT[:, :, :].rearrange("p j d -> p (j d)"), B3[:, 0:384])
                ae.copy(gateT[:, :], B3[:, 384:384 + E]).then_inc(setup_a, 1)
                ae.wait_ge(setup_pe, 6)
                for i in range(2):
                    ins = ae.copy(dnT[:, 4 * i:4 * i + 4, :].rearrange("p q d -> p (q d)"), DN[i][:, :])
                ins.then_inc(setup_a, 1)

            group(-1, False, True, False)
            group(0, True, True, False)
            with ae.Fori(1, G - 1) as g:
                group(g, True, True, True)
            group(G - 1, True, False, True)
            group(G, False, False, True)

        @block.vector
        def _(dve):
            dve.sem_inc(ff_dn, 2)
            dve.sem_inc(ff_term, 2)
            chain = [0]

            def set_link(ins):
                chain[0] += 1
                ins.then_inc(v_set, 1)
                dve.wait_ge(v_set, chain[0])

            dve.wait_ge(setup_p, 1)
            dve.wait_ge(wts_in, N_WTS[0])
            set_link(dve.tensor_tensor(sq[0:PK, 0:2 * HALF], keys[:, 0:2, :].rearrange("p c k -> p (c k)"),
                                       keys[:, 0:2, :].rearrange("p c k -> p (c k)"), ALU.mult))
            set_link(dve.tensor_reduce(kn[:, :], sq[0:PK, 0:2 * HALF].rearrange("p (c k) -> p c k", k=HALF), AX, ALU.add))
            dve.tensor_scalar(kn[:, :], kn[:, :], 1e-24, None, ALU.max).then_inc(setup_v, 1)
            dve.wait_ge(setup_pe, 3)
            set_link(dve.tensor_copy(wqcT[:, :], B2[:, :]))
            for t in (wqcT, bqc):
                set_link(dve.tensor_reduce(bqm[:, :], heads(t, 128), AX, ALU.add))
                set_link(dve.tensor_scalar(bqm[:, :], bqm[:, :], 1.0 / QD, None, ALU.mult))
                set_link(dve.tensor_tensor(heads(t, 128), heads(t, 128), spread(bqm, 128, H, QD), ALU.subtract))
            dve.sem_inc(setup_v, 1)
            dve.tensor_copy(merge16[:, :, :], merge[:, :, :])

            def largest_weights(e0, e1):
                dve.wait_ge(w1_in, 80)
                ins = dve.tensor_reduce(wmax[:, e0:e1], w1[:, e0:e1, :], AX, ALU.max, apply_absolute_value=True)
                if e1 == NE:
                    ins.then_inc(w_max, 1)

            def weight_scales():
                dve.wait_ge(w_top, 1)
                set_link(dve.tensor_reduce(wtop[:, :], UP[0][0:NE, 0:128], AX, ALU.max))
                set_link(dve.tensor_scalar(wtop[:, :], wtop[:, :], 2.0 ** -100, None, ALU.max))
                set_link(dve.tensor_scalar(wpow[:, 0:1], wtop[:, :].bitcast(I32), 0x7F800000, None, ALU.bitwise_and))
                set_link(dve.tensor_scalar(wpow[:, 1:2], wpow[:, 0:1], float((WEXP + XSCALE_EXP) << 23), None, ALU.subtract))
                set_link(dve.tensor_scalar(wpow[:, 0:1], wpow[:, 0:1], -1.0, float((2 * BIAS + WEXP) << 23), ALU.mult, ALU.add))
                for i in range(2):
                    dve.tensor_scalar(wdiag[:, i, :], ident[0:NE, 0:NE], wpow[:, i:i + 1].bitcast(F32), None,
                                      ALU.mult).then_inc(w_pow, 1)

            halved = [0]

            def setup_rest():
                dve.wait_ge(setup_pe, 5)
                for c in range(4):
                    ins = dve.tensor_copy(keysBD[HALF * c:HALF * c + HALF, PK * c:PK * c + PK],
                                          UP[0][HALF * c:HALF * c + HALF, 0:PK])
                ins.then_inc(setup_v, 1)

            def group(gi, peer, nxt, moe):
                m, gj = gi - 1, gi + 1
                links, done = [0, 0, 0], [0]

                def gs(st):
                    return (gj, gi, m)[st]

                def tile(s, ahead):
                    return 3 * (gj if s < ahead else gi) + s + 1

                def link(st, ins):
                    links[st] += 1
                    ins.then_inc(v_link[st], 1)
                    dve.wait_ge(v_link[st], gs(st) * V_LINKS[st] + links[st])

                def own_wait():
                    dve.sem_inc(v_met, 1)

                def split(upto):
                    if not peer:
                        return
                    for e in range(halved[0], min(upto, NE)):
                        if e == 0:
                            dve.wait_ge(w_scaled, 1)
                        dve.wait_ge(split_high, e + 1)
                        dve.scalar_tensor_tensor(halves[:, e % 4, 1, :], w1[:, e, :], wscale[:, 0, e:e + 1],
                                                 halves[:, e % 4, 0, :], ALU.mult, ALU.subtract).then_inc(split_low, 1)
                        halved[0] = e + 1

                def moe_to(upto):
                    if not moe:
                        split(upto // FC)
                    if not moe:
                        return
                    for e in range(done[0], upto // FC - 1):
                        x = NE * m + e
                        dve.wait_ge(ff_dn, x + 3)
                        dve.wait_ge(ff_acc, (NE + 1) * m + max(e, 1))
                        b = DN[e % 2][:, 0:N]
                        if EORD[e] >= E:
                            ins = dve.tensor_scalar(term[:, e % 2, :], b, col("b2", EORD[e]), 1.0 / SH, ALU.add, ALU.mult)
                        else:
                            r = EORD[e] // CB
                            if EORD[e] % CB == 0:
                                dve.wait_ge(comb_in[r % 2], 16 * (E // CB // 2 * m + r // 2 + 1))
                            ins = dve.scalar_tensor_tensor(term[:, e % 2, :], b, col("b2", EORD[e]),
                                                           combB[:, r % 2, EORD[e] % CB, :], ALU.add, ALU.mult)
                        ins.then_inc(ff_term, 1)
                        done[0] = e + 1

                def token_stats(st, i):
                    b = LN_IN[st]
                    dve.wait_ge(ln_t[st], 2 * gs(st) + i + 1)
                    for s, (o, n) in enumerate(SUBS):
                        ins = dve.bn_stats(bn[st][0:n, s, :], b[0:n, 128 * s:128 * s + 128])
                    link(st, ins)
                    own_wait()
                    for s, (o, n) in enumerate(SUBS):
                        ins = dve.bn_aggr(mv[st][0:n, s, :], bn[st][0:n, s, :])
                    ins.then_inc(ln_mv[st], 1)

                def norm_tokens(st, i):
                    b = LN_IN[st]
                    dve.wait_ge(ln_rstd[st], 2 * gs(st) + i + 1)
                    for s, (o, n) in enumerate(SUBS):
                        ins = dve.tensor_scalar(xn[st][0:n, s, :], b[0:n, 128 * s:128 * s + 128], mv[st][0:n, s, 0:1],
                                                rstd[st][0:n, s:s + 1], ALU.subtract, ALU.mult)
                    ins.then_inc(ln_xn[st], 1)

                def shift_scores(st):
                    dve.wait_ge(sc_mm[st], gs(st) + 1)
                    s = (B1, B2)[st][0:L, 0:N].rearrange("p (b j) -> p b j", j=L)
                    p = prob[st][:, :].rearrange("p (b j) -> p b j", j=L)
                    link(st, dve.tensor_reduce(amax[st][:, :], s, AX, ALU.max))
                    if st == A:
                        link(st, dve.tensor_scalar(amax[st][:, :], amax[st][:, :], 0.0, None, ALU.max))
                        dve.scalar_tensor_tensor(p, s, 0.0, spread(amax[st], L, GB, L), ALU.max,
                                                 ALU.subtract).then_inc(sc_shift[st], 1)
                    else:
                        dve.tensor_tensor(p, s, spread(amax[st], L, GB, L), ALU.subtract).then_inc(sc_shift[st], 1)

                def sum_exps(st):
                    dve.wait_ge(sc_exp[st], gs(st) + 1)
                    p = prob[st][:, :].rearrange("p (b j) -> p b j", j=L)
                    link(st, dve.tensor_reduce(asum[st][:, :], p, AX, ALU.add))
                    dve.reciprocal(arec[st][:, :], asum[st][:, :]).then_inc(sc_rec[st], 1)

                def query_bias(s):
                    n = SUBS[s][1]
                    dve.wait_ge(q_mm, tile(s, 2))
                    dve.tensor_tensor(qc[0:n, :], B0[0:n, :], bqc[0:n, :], ALU.add).then_inc(q_biased, 1)

                def query_sum(s):
                    n = SUBS[s][1]
                    dve.wait_ge(q_sq, tile(s, 2))
                    dve.tensor_reduce(qv[0:n, :], heads(sq, n), AX, ALU.add).then_inc(q_var, 1)

                def query_scale(s):
                    n = SUBS[s][1]
                    dve.wait_ge(q_rstd, tile(s, 2))
                    dve.tensor_tensor(heads(qc, n), heads(qc, n), spread(qr, n, H, QD), ALU.mult).then_inc(q_z, 1)

                def first_keys(s):
                    n = SUBS[s][1]
                    dve.wait_ge(ks_out, 2 * tile(s, 1))
                    own_wait()
                    for c in range(2 * H):
                        ins = dve.max(top[0:n, c, 0:8], sc[0:n, c, :])
                    link(A if s < 1 else B, ins)

                def first_indices(s):
                    n = SUBS[s][1]
                    own_wait()
                    for c in range(2 * H):
                        ins = dve.max_index(idx[0:n, c, 0:8], top[0:n, c, 0:8], sc[0:n, c, :])
                    link(A if s < 1 else B, ins)

                def drop_keys(s):
                    n = SUBS[s][1]
                    own_wait()
                    for c in range(2 * H):
                        ins = dve.match_replace(sc[0:n, c, :], top[0:n, c, 0:8], sc[0:n, c, :], TAKEN)
                    link(A if s < 1 else B, ins)

                def next_keys(s):
                    n = SUBS[s][1]
                    own_wait()
                    for c in range(2 * H):
                        ins = dve.max(top[0:n, c, 8:16], sc[0:n, c, :])
                    link(A if s < 1 else B, ins)

                def next_indices(s):
                    n = SUBS[s][1]
                    own_wait()
                    for c in range(2 * H):
                        ins = dve.max_index(idx[0:n, c, 8:16], top[0:n, c, 8:16], sc[0:n, c, :])
                    link(A if s < 1 else B, ins)

                def found(s):
                    n = SUBS[s][1]
                    dve.wait_ge(n_inv, tile(s, 1))
                    dve.tensor_tensor(topn[0:n], top[0:n], spread(inv[:, s % 2, :], n, 2 * H, K), ALU.mult)
                    dve.tensor_copy(idf[0:n], idx[0:n]).then_inc(top_done, 1)

                def first_pairs(s):
                    n = SUBS[s][1]
                    dve.wait_ge(cand_done, 2 * (3 * gi + s) + 1)
                    own_wait()
                    for h in range(H):
                        ins = dve.max(best[0:n, h, 0:8], cand[0:n, h, :])
                    link(B, ins)
                    own_wait()
                    for h in range(H):
                        ins = dve.match_replace(cand2[0:n, h, :], best[0:n, h, 0:8], cand[0:n, h, :], TAKEN)
                    link(B, ins)

                def next_pairs(s):
                    n = SUBS[s][1]
                    own_wait()
                    for h in range(H):
                        ins = dve.max(best[0:n, h, 8:16], cand2[0:n, h, :])
                    link(B, ins)
                    own_wait()
                    for h in range(H):
                        ins = dve.match_replace(cand2[0:n, h, :], best[0:n, h, 8:16], cand2[0:n, h, :], TAKEN)
                    link(B, ins)

                def weigh(s):
                    n = SUBS[s][1]
                    k = 3 * gi + s + 1
                    dve.wait_ge(cand_exp, k)
                    link(B, dve.scalar_tensor_tensor(cw_[0:n].rearrange("p h k -> p (h k)"),
                                                     cand2[0:n].rearrange("p h k -> p (h k)"), TAKEN / 10,
                                                     cexp[0:n].rearrange("p h k -> p (h k)"), ALU.is_lt, ALU.mult))
                    link(B, dve.tensor_reduce(z[0:n], cw_[0:n], AX, ALU.add))
                    link(B, dve.tensor_scalar(z[0:n], z[0:n], 1.0 / WSCALE, None, ALU.mult))
                    dve.reciprocal(zr[0:n], z[0:n]).then_inc(w_raw, 1)
                    dve.wait_ge(cand_done, 2 * k)
                    dve.scalar_tensor_tensor(epick[0:n].rearrange("p h k -> p (h k)"),
                                             cand2[0:n].rearrange("p h k -> p (h k)"), TAKEN / 10,
                                             cexpert[0:n, s % 2].rearrange("p h k -> p (h k)"), ALU.is_lt,
                                             ALU.mult).then_inc(e_picked, 1)

                def hot(s):
                    n = SUBS[s][1]
                    k = 3 * gi + s + 1
                    w = 2 * n
                    dve.wait_ge(slots_mm, k)
                    dve.tensor_scalar(pi[:, 0:w], B0[0:NS, w:2 * w], 0.125, -0.4375, ALU.mult, ALU.add)
                    link(B, dve.tensor_copy(whi[:, 0:w], B0[0:NS, 0:w]))
                    dve.scalar_tensor_tensor(qi[:, 0:w], pi[:, 0:w], -8.0, B0[0:NS, w:2 * w], ALU.mult, ALU.add)
                    dve.tensor_tensor(wlo[:, 0:w], B0[0:NS, 0:w], whi[:, 0:w], ALU.subtract).then_inc(pq_ready, 1)
                    for p in range(P16):
                        dve.tensor_scalar(ph[:, 0:n // 4, p, :], pi[:, 0:w].rearrange("p (g t) -> p g t", t=8),
                                          float(p), None, ALU.is_equal)
                    dve.wait_ge(pq_ready, k)
                    for q in range(Q8):
                        ins = dve.tensor_scalar(qh[:, q, 0:w], qi[:, 0:w], float(q), None, ALU.is_equal)
                    link(B, ins)
                    for part, src in enumerate((whi, wlo)):
                        ins = dve.tensor_tensor(qw[:, part, :, 0:w], qh[:, :, 0:w],
                                                src[:, 0:w].unsqueeze(1).broadcast_to([NS, Q8, w]), ALU.mult)
                    ins.then_inc(q_hot, 1)

                def own_blocks(s):
                    o, n = SUBS[s]
                    if s == 0:
                        dve.wait_ge(act_masked, 2 * gi + 2)
                    dve.wait_ge(pq_mm, 3 * gi + s + 1)
                    for i, b in enumerate((B2, B3)):
                        g = min(8, n // 8 - 8 * i)
                        t = slice(o + 64 * i, o + 64 * i + 8 * g)
                        ins = dve.tensor_tensor(
                            act[:, :, t].rearrange("p q (g t) -> p q g t", t=8),
                            b[:, 0:64 * g].rearrange("p (g q t) -> p q g t", q=Q8, t=8),
                            act[:, :, t].rearrange("p q (g t) -> p q g t", t=8), ALU.mult)
                    ins.then_inc(peer_x, 1)

                def gated(i):
                    dve.wait_ge(hw_act, 4 * gj + 2 * i + 2)
                    src, dst = ((inA, x1T), (x1T, x2T))[i]
                    link(A, dve.tensor_tensor(dT[:, :], tT[:, :], src[:, :], ALU.subtract))
                    link(A, dve.scalar_tensor_tensor(dT[:, :], cT[:, :], 1.0, dT[:, :], ALU.add, ALU.mult))
                    dve.scalar_tensor_tensor(dst[:, :], dT[:, :], 0.5, src[:, :], ALU.mult, ALU.add).then_inc(hw_x, 1)
                    if i == 1:
                        dve.wait_ge(hw_x, 2 * gj + 2)
                        dve.tensor_scalar(uT[:, :], x2T[:, :], col("aw", 2), col("aw", 1), ALU.mult,
                                          ALU.add).then_inc(u_ready, 1)

                if peer:
                    first_pairs(0)
                if moe:
                    dve.wait_ge(lg_exp, 2 * gi)
                    link(C, dve.tensor_scalar(comb[:, :, :], ge[:, :, :], -1.0, 1.0, ALU.mult, ALU.add))
                    link(C, dve.reciprocal(comb[:, :, :], comb[:, :, :]))
                    link(C, dve.scalar_tensor_tensor(ge[:, :, :], ge[:, :, :], 1.0, comb[:, :, :], ALU.add, ALU.mult))
                    link(C, dve.scalar_tensor_tensor(comb[:, :, :], lg2[:, :, 0:E], TAKEN / 10, ge[:, :, :],
                                                     ALU.is_lt, ALU.mult))
                    link(C, dve.tensor_reduce(gs_[:, :], comb[:, :, :], AX, ALU.add))
                    link(C, dve.reciprocal(gr[:, :], gs_[:, :]))
                    dve.tensor_tensor(comb[:, :, :], comb[:, :, :], spread(gr, 128, NSUB, E),
                                      ALU.mult).then_inc(comb_ready, 1)
                if peer:
                    next_pairs(0)
                    weigh(0)
                moe_to(AT["k1"])
                if peer:
                    query_bias(2)
                moe_to(AT["c0"])
                if peer:
                    first_keys(1)
                    query_sum(2)
                if nxt:
                    token_stats(A, 0)
                if peer:
                    first_indices(1)
                    query_scale(2)
                if nxt:
                    norm_tokens(A, 0)
                moe_to(AT["a5"])
                if peer:
                    drop_keys(1)
                moe_to(AT["t0"])
                if peer:
                    hot(0)
                moe_to(AT["a7"])
                if nxt:
                    gated(0)
                if peer:
                    next_keys(1)
                moe_to(AT["u0"])
                if peer:
                    own_blocks(0)
                    next_indices(1)
                    found(1)
                moe_to(AT["a9"])
                if nxt:
                    gated(1)
                moe_to(AT["c1"])
                if peer:
                    first_pairs(1)
                    next_pairs(1)
                    weigh(1)
                moe_to(AT["t1"])
                if peer:
                    first_keys(2)
                    first_indices(2)
                if nxt:
                    if not peer:
                        largest_weights(0, 6)
                    shift_scores(A)
                if peer:
                    hot(1)
                moe_to(AT["a12"])
                if peer:
                    drop_keys(2)
                moe_to(AT["u1"])
                if nxt:
                    if not peer:
                        largest_weights(6, 12)
                    sum_exps(A)
                    if not peer:
                        largest_weights(12, NE)
                if peer:
                    own_blocks(1)
                    next_keys(2)
                    next_indices(2)
                    found(2)
                moe_to(AT["c2"])
                if peer:
                    first_pairs(2)
                    next_pairs(2)
                    weigh(2)
                moe_to(AT["t2"])
                if peer:
                    hot(2)
                moe_to(AT["u2"])
                if nxt:
                    dve.wait_ge(gate_act, 2 * gj + 2)
                    dve.scalar_tensor_tensor(dT[:, :], cT[:, :], 1.0, inA[:, :], ALU.add, ALU.mult)
                    link(A, dve.tensor_scalar(tT[:, :], tT[:, :], 0.5, 0.5, ALU.mult, ALU.add))
                    dve.scalar_tensor_tensor(x1T[:, :], dT[:, :], 0.5, hAT[:, :], ALU.mult, ALU.add)
                    link(A, dve.tensor_tensor(x2T[:, :], tT[:, :], tT[:, :], ALU.mult))
                    dve.tensor_tensor(hAT[:, :], x1T[:, :], x2T[:, :], ALU.add).then_inc(h_ready[A], 1)
                if peer:
                    own_blocks(2)
                if nxt:
                    token_stats(A, 1)
                moe_to(AT["up"])
                if nxt:
                    norm_tokens(A, 1)
                if peer:
                    dve.wait_ge(up_mm, gi + 1)
                    dve.wait_ge(h_kept, gi + 1)
                    dve.scalar_tensor_tensor(hT[:, :], B2[:, 0:N], 1.0 / WSCALE, hT[:, :], ALU.mult,
                                             ALU.add).then_inc(h_ready[B], 1)
                    token_stats(B, 0)
                moe_to(AT["ln0"])
                if nxt:
                    if not peer:
                        setup_rest()
                    query_bias(0)
                if peer:
                    norm_tokens(B, 0)
                if nxt:
                    query_sum(0)
                moe_to(AT["back0"])
                if peer:
                    dve.wait_ge(ln_b[B], 2 * gi + 1)
                    dve.tensor_tensor(inT[:, :].rearrange("p (b l) -> p b l", l=L),
                                      B2[:, 0:N].rearrange("p (b l) -> p b l", l=L),
                                      posT[:, :].unsqueeze(1).broadcast_to([128, GB, L]), ALU.add).then_inc(ln_out[B], 1)
                if nxt:
                    query_scale(0)
                moe_to(AT["kq"])
                if nxt:
                    first_keys(0)
                    query_bias(1)
                moe_to(AT["v"])
                if peer:
                    shift_scores(B)
                if nxt:
                    first_indices(0)
                    query_sum(1)
                if peer:
                    sum_exps(B)
                moe_to(AT["i0"])
                if nxt:
                    drop_keys(0)
                    query_scale(1)
                moe_to(AT["pt"])
                if peer:
                    dve.wait_ge(att_mm[B], gi + 1)
                    dve.scalar_tensor_tensor(hT[:, :], B2[:, 0:N], col("bv"), hT[:, :], ALU.add,
                                             ALU.add).then_inc(h_ready[B], 1)
                if nxt:
                    next_keys(0)
                moe_to(AT["lnB1"])
                if peer:
                    token_stats(B, 1)
                if nxt:
                    next_indices(0)
                moe_to(STEPS)
                if peer:
                    norm_tokens(B, 1)
                    dve.wait_ge(ln_out[B], 2 * gi + 2)
                    dve.scalar_tensor_tensor(xd16[:, 1, :], xd[:, :], float(2 ** XSCALE_EXP), xd16[:, 0, :],
                                             ALU.mult, ALU.subtract).then_inc(x_split, 1)
                    dve.wait_ge(lg_mm, gi + 1)
                    for s, (o, n) in enumerate(SUBS):
                        ins = dve.tensor_copy(lg[0:n, s, 0:E], B3[0:n, E * s:E * s + E])
                    link(B, ins)
                    link(B, dve.tensor_reduce(gs_[:, :], lg[:, :, 0:E], AX, ALU.max))
                    dve.tensor_tensor(ge[:, :, :], lg[:, :, 0:E], spread(gs_, 128, NSUB, E),
                                      ALU.subtract).then_inc(lg_shift, 1)
                if nxt:
                    found(0)
                if peer:
                    dve.wait_ge(lg_exp, 2 * gi + 1)
                    link(B, dve.tensor_reduce(gs_[:, :], ge[:, :, :], AX, ALU.add))
                    link(B, dve.reciprocal(gr[:, :], gs_[:, :]))
                    link(B, dve.tensor_tensor(lg[:, :, 0:E], ge[:, :, :], spread(gr, 128, NSUB, E), ALU.mult))
                    own_wait()
                    for s, (o, n) in enumerate(SUBS):
                        ins = dve.max(m8[0:n, s, :], lg[0:n, s, :])
                    link(B, ins)
                    dve.tensor_tensor(ge[:, :, :], lg[:, :, 0:E], m8[:, :, 0:1].broadcast_to([128, NSUB, E]),
                                      ALU.subtract).then_inc(lg_shift, 1)
                    link(B, dve.tensor_copy(t8[:, :, 0:TOPK], m8[:, :, 0:TOPK]))
                    own_wait()
                    for s, (o, n) in enumerate(SUBS):
                        ins = dve.match_replace(lg2[0:n, s, :], t8[0:n, s, :], lg[0:n, s, :], TAKEN)
                    link(B, ins)
                assert links == [nxt * V_LINKS[A], peer * V_LINKS[B], moe * V_LINKS[C]], f"V_LINKS {links}"

            group(-1, False, True, False)
            weight_scales()
            group(0, True, True, False)
            with dve.Fori(1, G - 1) as g:
                group(g, True, True, True)
            group(G - 1, True, False, True)
            group(G, False, False, True)


_INS = ['x', 'L0_tok_W', 'L0_tok_b', 'L0_attn_tW', 'L0_attn_tb', 'L0_attn_cW', 'L0_attn_cb', 'L0_attn_aW',
        'L0_attn_ab', 'L0_attn_frW', 'L0_attn_frb', 'L0_attn_ffW', 'L0_attn_ffb', 'L0_ffn_Wq', 'L0_ffn_bq',
        'L0_ffn_ln_g', 'L0_ffn_ln_b', 'L0_ffn_keys0', 'L0_ffn_keys1', 'L0_ffn_expert_down',
        'L0_ffn_expert_up', 'L1_attn_Wq', 'L1_attn_bq', 'L1_attn_Wk', 'L1_attn_bk', 'L1_attn_Wv',
        'L1_attn_bv', 'L1_ffn_gate_w', 'L1_ffn_re_w1', 'L1_ffn_re_b1', 'L1_ffn_re_w2', 'L1_ffn_re_b2',
        'L1_ffn_se_w1', 'L1_ffn_se_b1', 'L1_ffn_se_w2', 'L1_ffn_se_b2']


def merge_table():
    def area(a, b):
        return sum(max([c + 1 for r, c in (a, b) if r >= row], default=0) for row in range(K))

    grid = [(r + i, c) for r, m, w in CELLS for i in range(m) for c in range(w)]
    slot = {}
    for cell in sorted(grid, key=lambda x: (x[0] + 1) * (x[1] + 1)):
        if area(cell, cell) > K:
            slot[cell] = 0
            continue
        used = {s for other, s in slot.items() if area(cell, other) <= K}
        slot[cell] = min(set(range(len(grid))) - used)
    assert max(slot.values()) < SLOTS
    table = np.zeros((2 * NC, 2, 4 * SLOTS), np.float32)
    for pair in range(2):
        for head in range(2):
            for i, cell in enumerate(grid):
                table[head * NC + i, pair, (2 * pair + head) * SLOTS + slot[cell]] = 1.0
    return table


def shape_constants():
    pos = np.arange(L, dtype=np.float32)[:, None]
    div = np.exp(np.arange(0, D, 2, dtype=np.float32) * np.float32(-np.log(np.float32(10000.0)) / D))
    ang = (pos * div.astype(np.float32)).astype(np.float32)
    mask = np.tile(np.eye(8, dtype=np.float32), (P16, 1))
    return {"c_ident": np.eye(128, dtype=np.float32),
            "c_posT": np.ascontiguousarray(np.concatenate([np.sin(ang), np.cos(ang)], axis=-1).T.astype(np.float32)),
            "c_blockmask": mask,
            "c_merge": merge_table(),
            "c_halfones": np.repeat(np.eye(4, dtype=np.float32), HALF, axis=0)}


def kernel(**inputs):
    import concourse.bacc as bacc
    from concourse.bass_utils import run_bass_kernel_spmd

    nc = bacc.Bacc("TRN2", target_bir_lowering=False, num_devices=1)
    arrays, aps = {}, {}
    for name, v in [(n, inputs[n]) for n in _INS] + list(shape_constants().items()):
        v = np.ascontiguousarray(v)
        arrays[f"in_{name}_dram"] = v
        aps[name] = nc.dram_tensor(f"in_{name}_dram", v.shape, mybir.dt.from_np(v.dtype), kind="ExternalInput").ap()
    out = nc.dram_tensor("out_0_dram", (NB, L, D), F32, kind="ExternalOutput").ap()
    build(nc, aps, out)
    r = run_bass_kernel_spmd(nc, [arrays], core_ids=[0])
    return r.results[0]["out_0_dram"]
```
